# Optimizing a Trainium2 kernel written in Bass

```python
import numpy as np
import jax
import jax.numpy as jnp

def _softmax(x, axis=-1):
    return jax.nn.softmax(x, axis=axis)

def _gelu(x):
    return jax.nn.gelu(x, approximate=True)

def _silu(x):
    return jax.nn.silu(x)

def _sigmoid(x):
    return jax.nn.sigmoid(x)

def _layernorm(x, axis=-1, eps=1e-05):
    m = jnp.mean(x, axis=axis, keepdims=True)
    v = jnp.var(x, axis=axis, keepdims=True)
    return (x - m) / jnp.sqrt(v + eps)

def _scatter_add(tgt, idx, src, axis=0):
    return tgt.at[idx].add(src)

def _segment_sum(src, seg, n):
    return jax.ops.segment_sum(src, seg, n)
kernel_name = 'mk_adj_resnorm_d2_adj_r2_2f964a'

def setup_inputs(seed: int=0):
    np.random.seed(seed)
    _w = jnp.asarray

    def _rec_inputs():
        import jax
        import jax.numpy as jnp
        _gk = jax.random.key(seed)
        x = -0.000929 + 1 * jax.random.normal(jax.random.fold_in(_gk, 1), (4096, 128), jnp.float32)
        _a = jax.random.bernoulli(jax.random.fold_in(_gk, 2), 0.00390625, (4096, 4096))
        _a = jnp.logical_or(_a, jnp.eye(4096, dtype=bool))
        _af = _a.astype(jnp.float32)
        _af = _af * jax.random.uniform(jax.random.fold_in(_gk, 3), (4096, 4096), jnp.float32, 0.05, 1)
        adj = _af
        return (x, adj)
    x, adj = _rec_inputs()

    def _L0_gnn_setup():
        import jax, jax.numpy as jnp
        import numpy as np
        N, H, HEADS = (2048, 128, 3)
        ALPHA = 0.2
        NEG_INF = -9000000000000000.0

        def _sign_adj(key, n, density):
            k1, k2 = jax.random.split(key)
            mask = jax.random.uniform(k1, (n, n)) < density
            sign = jnp.where(jax.random.uniform(k2, (n, n)) < 0.5, -1.0, 1.0)
            adj = jnp.where(mask, sign, 0.0).astype(jnp.float32)
            idx = jnp.arange(n)
            return adj.at[idx, idx].set(1.0)

        def _gru_cell(x, hstate, Wih, Whh, bih, bhh):
            gi = x @ Wih.T + bih
            gh = hstate @ Whh.T + bhh
            ir, iz, inn = jnp.split(gi, 3, axis=1)
            hr, hz, hn = jnp.split(gh, 3, axis=1)
            r = jax.nn.sigmoid(ir + hr)
            z = jax.nn.sigmoid(iz + hz)
            n = jnp.tanh(inn + r * hn)
            return (1.0 - z) * n + z * hstate

        def _gat_head(h, node_adj, edge_adj, W, a):
            hW = h @ W
            hp = (node_adj > 0).astype(hW.dtype) @ hW
            hm = (node_adj < 0).astype(hW.dtype) @ hW
            e_plus = jax.nn.leaky_relu(jnp.concatenate([hp, hm], axis=1) @ a, ALPHA)[:, 0]
            e_minus = jax.nn.leaky_relu(jnp.concatenate([hm, hp], axis=1) @ a, ALPHA)[:, 0]
            att = jnp.where(edge_adj > 0, e_plus[None, :], NEG_INF)
            att = jnp.where(edge_adj < 0, e_minus[None, :], att)
            att = jax.nn.softmax(att, axis=1)
            return att * edge_adj @ hW
        key = jax.random.key(seed)
        ks = jax.random.split(key, 16)
        std = 0.01
        gain = 1.414
        return {'h': jax.random.normal(ks[0], (N, H), jnp.float32), 'node_adj': _sign_adj(ks[1], N, 0.005), 'edge_adj': _sign_adj(ks[2], N, 0.005), 'gat_W': jax.random.normal(ks[3], (HEADS, H, H), jnp.float32) * (gain / np.sqrt(H, dtype=np.float32)), 'gat_a': jax.random.normal(ks[4], (HEADS, 2 * H, 1), jnp.float32) * 0.1, 'edge_Wih': jax.random.normal(ks[5], (3 * H, H), jnp.float32) * std, 'edge_Whh': jax.random.normal(ks[6], (3 * H, H), jnp.float32) * std, 'edge_bih': jnp.zeros((3 * H,), jnp.float32), 'edge_bhh': jnp.zeros((3 * H,), jnp.float32), 'node_Wih': jax.random.normal(ks[7], (3 * H, H), jnp.float32) * std, 'node_Whh': jax.random.normal(ks[8], (3 * H, H), jnp.float32) * std, 'node_bih': jnp.zeros((3 * H,), jnp.float32), 'node_bhh': jnp.zeros((3 * H,), jnp.float32)}
    _L0_gnn_all = _L0_gnn_setup()
    _L0_gnn_in = {k: v for k, v in _L0_gnn_all.items() if k in ('gat_W', 'gat_a', 'edge_Wih', 'edge_Whh', 'edge_bih', 'edge_bhh', 'node_Wih', 'node_Whh', 'node_bih', 'node_bhh')}
    del _L0_gnn_all

    def _L1_gnn_setup():
        import jax, jax.numpy as jnp
        import numpy as np
        N = 3072
        HID = 128
        T = 350
        DENSITY = 0.05
        key = jax.random.key(seed)
        k1, k2, k3, k4, k5, k6 = jax.random.split(key, 6)
        h = jax.random.normal(k1, (N, HID), dtype=jnp.float32)
        a = jax.random.uniform(k2, (N, N), dtype=jnp.float32)
        mask = jax.random.uniform(k3, (N, N)) < DENSITY
        adj = jnp.where(mask, a, 0.0)
        simlar = jax.random.normal(k4, (N, N), dtype=jnp.float32)
        s = 1.0 / np.sqrt(HID)
        W_proj = jax.random.uniform(k5, (HID, HID), minval=-s, maxval=s, dtype=jnp.float32)
        b_proj = jnp.zeros((HID,), dtype=jnp.float32)
        W_gcn = jax.random.uniform(k6, (HID, HID), minval=-s, maxval=s, dtype=jnp.float32)
        b_gcn = jnp.zeros((HID,), dtype=jnp.float32)
        return {'h': h, 'adj': adj, 'simlar': simlar, 'W_proj': W_proj, 'b_proj': b_proj, 'W_gcn': W_gcn, 'b_gcn': b_gcn}
    _L1_gnn_all = _L1_gnn_setup()
    _L1_gnn_in = {k: v for k, v in _L1_gnn_all.items() if k in ('W_proj', 'b_proj', 'W_gcn', 'b_gcn')}
    del _L1_gnn_all
    return {'x': x, 'adj': adj, 'L0_gnn_gat_W': _L0_gnn_in['gat_W'], 'L0_gnn_gat_a': _L0_gnn_in['gat_a'], 'L0_gnn_edge_Wih': _L0_gnn_in['edge_Wih'], 'L0_gnn_edge_Whh': _L0_gnn_in['edge_Whh'], 'L0_gnn_edge_bih': _L0_gnn_in['edge_bih'], 'L0_gnn_edge_bhh': _L0_gnn_in['edge_bhh'], 'L0_gnn_node_Wih': _L0_gnn_in['node_Wih'], 'L0_gnn_node_Whh': _L0_gnn_in['node_Whh'], 'L0_gnn_node_bih': _L0_gnn_in['node_bih'], 'L0_gnn_node_bhh': _L0_gnn_in['node_bhh'], 'L1_gnn_W_proj': _L1_gnn_in['W_proj'], 'L1_gnn_b_proj': _L1_gnn_in['b_proj'], 'L1_gnn_W_gcn': _L1_gnn_in['W_gcn'], 'L1_gnn_b_gcn': _L1_gnn_in['b_gcn']}

def reference(x, adj, L0_gnn_gat_W, L0_gnn_gat_a, L0_gnn_edge_Wih, L0_gnn_edge_Whh, L0_gnn_edge_bih, L0_gnn_edge_bhh, L0_gnn_node_Wih, L0_gnn_node_Whh, L0_gnn_node_bih, L0_gnn_node_bhh, L1_gnn_W_proj, L1_gnn_b_proj, L1_gnn_W_gcn, L1_gnn_b_gcn):
    import jax
    import jax.numpy as jnp

    def _L0_gnn_ref(h, node_adj, edge_adj, gat_W, gat_a, edge_Wih, edge_Whh, edge_bih, edge_bhh, node_Wih, node_Whh, node_bih, node_bhh):
        import jax, jax.numpy as jnp
        import numpy as np
        N, H, HEADS = (2048, 128, 3)
        ALPHA = 0.2
        NEG_INF = -9000000000000000.0

        def _sign_adj(key, n, density):
            k1, k2 = jax.random.split(key)
            mask = jax.random.uniform(k1, (n, n)) < density
            sign = jnp.where(jax.random.uniform(k2, (n, n)) < 0.5, -1.0, 1.0)
            adj = jnp.where(mask, sign, 0.0).astype(jnp.float32)
            idx = jnp.arange(n)
            return adj.at[idx, idx].set(1.0)

        def _gru_cell(x, hstate, Wih, Whh, bih, bhh):
            gi = x @ Wih.T + bih
            gh = hstate @ Whh.T + bhh
            ir, iz, inn = jnp.split(gi, 3, axis=1)
            hr, hz, hn = jnp.split(gh, 3, axis=1)
            r = jax.nn.sigmoid(ir + hr)
            z = jax.nn.sigmoid(iz + hz)
            n = jnp.tanh(inn + r * hn)
            return (1.0 - z) * n + z * hstate

        def _gat_head(h, node_adj, edge_adj, W, a):
            hW = h @ W
            hp = (node_adj > 0).astype(hW.dtype) @ hW
            hm = (node_adj < 0).astype(hW.dtype) @ hW
            e_plus = jax.nn.leaky_relu(jnp.concatenate([hp, hm], axis=1) @ a, ALPHA)[:, 0]
            e_minus = jax.nn.leaky_relu(jnp.concatenate([hm, hp], axis=1) @ a, ALPHA)[:, 0]
            att = jnp.where(edge_adj > 0, e_plus[None, :], NEG_INF)
            att = jnp.where(edge_adj < 0, e_minus[None, :], att)
            att = jax.nn.softmax(att, axis=1)
            return att * edge_adj @ hW
        dn = jnp.diag(node_adj)
        de = jnp.diag(edge_adj)
        idx = jnp.arange(node_adj.shape[0])
        node_adj_norm = node_adj.at[idx, idx].add(-dn)
        edge_adj_norm = edge_adj.at[idx, idx].add(-de)
        node_support = node_adj_norm @ h
        edge_output = _gru_cell(node_support, h, edge_Wih, edge_Whh, edge_bih, edge_bhh)
        edge_support = _gat_head(h, node_adj_norm, edge_adj_norm, gat_W[0], gat_a[0])
        for i in range(1, HEADS):
            edge_support = edge_support + _gat_head(h, node_adj_norm, edge_adj_norm, gat_W[i], gat_a[i])
        edge_support = edge_support / HEADS
        node_output = _gru_cell(edge_support, h, node_Wih, node_Whh, node_bih, node_bhh)
        return de[:, None] * edge_output + dn[:, None] * node_output

    def _L1_gnn_ref(h, adj, simlar, W_proj, b_proj, W_gcn, b_gcn):
        import jax, jax.numpy as jnp
        import numpy as np
        N = 3072
        HID = 128
        T = 350
        DENSITY = 0.05
        sim = jnp.tanh(adj * simlar)
        filt = sim * (adj > 0).astype(sim.dtype)
        vals, idx = jax.lax.top_k(filt, T)
        nnz = jnp.sum(filt != 0, axis=1)
        keep = jnp.arange(T)[None, :] < nnz[:, None]
        rows = jnp.arange(filt.shape[0])[:, None]
        new_adj = jnp.zeros_like(filt).at[rows, idx].set(jnp.where(keep, vals, 0.0))
        h2 = jnp.tanh(h @ W_proj + b_proj)
        feat = jax.nn.relu(new_adj @ (h2 @ W_gcn) + b_gcn)
        return feat
    x = _layernorm(x + _L0_gnn_ref(x, adj, adj, L0_gnn_gat_W, L0_gnn_gat_a, L0_gnn_edge_Wih, L0_gnn_edge_Whh, L0_gnn_edge_bih, L0_gnn_edge_bhh, L0_gnn_node_Wih, L0_gnn_node_Whh, L0_gnn_node_bih, L0_gnn_node_bhh), axis=-1)
    x = _layernorm(x + _L1_gnn_ref(x, adj, adj, L1_gnn_W_proj, L1_gnn_b_proj, L1_gnn_W_gcn, L1_gnn_b_gcn), axis=-1)
    return x

_drawn_inputs = setup_inputs


def setup_inputs(seed=0):
    import zlib

    import numpy as np

    out = dict(_drawn_inputs(seed))
    spreads = {'L0_gnn_edge_bih': (0.0, 0.334),
     'L0_gnn_edge_bhh': (0.0, 0.583),
     'L0_gnn_node_bih': (0.0, 0.37),
     'L0_gnn_node_bhh': (0.0, 0.582),
     'L1_gnn_b_proj': (0.0, 0.1),
     'L1_gnn_b_gcn': (0.0, 0.1)}
    factors = {'L0_gnn_gat_W': 6.338,
     'L0_gnn_gat_a': 6.823,
     'L0_gnn_edge_Whh': 4.184,
     'L0_gnn_node_Wih': 6.334,
     'L0_gnn_node_Whh': 4.12}
    for name, (base, spread) in spreads.items():
        noise = np.random.default_rng([zlib.crc32(name.encode()), seed]).standard_normal(out[name].shape)
        drawn = base * np.exp(spread * noise) if base else spread * noise
        out[name] = jnp.asarray(drawn.astype(out[name].dtype))
    for name, factor in factors.items():
        out[name] = (out[name] * factor).astype(out[name].dtype)
    return out
```

```python
from contextlib import ExitStack

import concourse.bass as bass
from concourse import mybir

ALU = mybir.AluOpType
ACT = mybir.ActivationFunctionType
AX_X = mybir.AxisListType.X
F32 = mybir.dt.float32
BF16 = mybir.dt.bfloat16
I32 = mybir.dt.int32

P = 128
N = 4096
H = 128
HEADS = 3
NB = N // P
CHUNK = 4
CW = CHUNK * P
NCHUNK = NB // CHUNK
GRP = 8
NGRP = NB // GRP
ALPHA = 0.2
NEG_INF = -9000000000000000.0
TOPK = 350
EPS = 1e-5
NPART = 3
NUV = 2 * HEADS
NST = 1 + NPART * NUV
LOWEST = -3.0e38
SCRATCH = {
    "e": (NUV, N),
    "ns_t": (P, N),
    "y_t": (NB, P, HEADS * P),
    "adj_top_t": (NB, P, N),
}


class Mem:

    def __init__(self, nc, ctx):
        self.nc, self.ctx = nc, ctx

    def sb(self, name, shape, dt=F32):
        return self.ctx.enter_context(self.nc.sbuf_tensor(name, shape, dt))

    def ps(self, name, shape, dt=F32):
        return self.ctx.enter_context(self.nc.psum_tensor(name, shape, dt))


def setup_phase(nc, sem, dram, keep):
    x_ready, x_t_ready, w_ready = sem("s_x"), sem("s_xT"), sem("s_w")
    folded, folded_out = sem("s_folded"), sem("s_folded_out")
    uv_done, uv_out = sem("s_uv_done"), sem("s_uv_out")
    split = sem("s_split")
    with ExitStack() as ctx:
        m = Mem(nc, ctx)
        x_t = m.sb("x_t", [P, N])
        w_t = m.sb("w_t", [P, HEADS, H])
        a_sb = m.sb("a_sb", [P, HEADS, 2])
        w6 = m.sb("w6", [P, NUV])
        uv = m.sb("uv", [P, NB, NUV])
        rest = m.sb("rest", [P, NB, NUV])
        w6_ps = m.ps("w6_ps", [P, 512])
        uv_ps = m.ps("uv_ps", [P, 512])
        x_sb, uv_parts, ident, off_diag = keep["x_sb"], keep["uv_parts"], keep["ident"], keep["off_diag"]
        part = [uv_parts[:, :, 1 + k * NUV:1 + (k + 1) * NUV] for k in range(NPART)]
        block = ctx.enter_context(nc.Block())

        @block.sync
        def _(sp):
            sp.dma_start(w_t[:, :, :], dram["gat_W_t"].rearrange("h g f -> g h f")).then_inc(w_ready, 16)
            sp.dma_start(a_sb[:, :, :], dram["gat_a"]).then_inc(w_ready, 16)
            sp.dma_start(x_t[:, :], dram["x_t"]).then_inc(x_t_ready, 16)
            sp.dma_start(x_sb[:, :, :], dram["x"].rearrange("(t p) f -> p t f", p=P)).then_inc(x_ready, 16)
            sp.dma_start(ident[:, :], dram["ident"]).then_inc(x_ready, 16)
            sp.dma_start(off_diag[:, :], dram["off_diag"]).then_inc(x_ready, 16)
            sp.dma_start(keep["sel"][:, :], dram["sel"]).then_inc(x_ready, 16)
            sp.wait_ge(x_ready, 64)

        @block.tensor
        def _(pe):
            pe.wait_ge(w_ready, 32)
            for h in range(HEADS):
                last = nc.tensor.matmul(w6_ps[:, 2 * h:2 * h + 2], w_t[:, h, :], a_sb[:, h, :], start=True, stop=True)
            last.then_inc(folded, 1)
            pe.wait_ge(folded_out, 1)
            pe.wait_ge(x_t_ready, 16)
            for t in range(NB):
                last = nc.tensor.matmul(uv_ps[:, t * NUV:(t + 1) * NUV], x_t[:, t * P:(t + 1) * P], w6[:, :],
                                        start=True, stop=True)
            last.then_inc(uv_done, 1)

        @block.vector
        def _(dve):
            nc.vector.memset(keep["run_max"][:, :], 0.0)
            dve.wait_ge(x_ready, 64)
            nc.vector.tensor_scalar(keep["diag_bias"][:, :], ident[:, :], NEG_INF, None, ALU.mult)
            nc.vector.memset(uv_parts[:, :, 0:1], 1.0)
            dve.wait_ge(folded, 1)
            nc.vector.tensor_copy(w6[:, :], w6_ps[:, 0:NUV]).then_inc(folded_out, 1)
            dve.wait_ge(uv_done, 1)
            nc.vector.tensor_copy(uv[:, :, :], uv_ps[:, 0:NB * NUV].rearrange("p (t j) -> p t j", j=NUV)).then_inc(uv_out, 1)
            dve.wait_ge(uv_out, 1)
            left = uv
            for k in range(NPART):
                nc.vector.tensor_copy(part[k], left[:, :, :]).then_inc(split, 1)
                dve.wait_ge(split, 2 * k + 1)
                if k < NPART - 1:
                    nc.vector.tensor_tensor(rest[:, :, :], left[:, :, :], part[k], ALU.subtract).then_inc(split, 1)
                    dve.wait_ge(split, 2 * k + 2)
                    left = rest


def mask_phase(nc, sem, dram, keep):
    loaded = [sem("a_loaded0"), sem("a_loaded1")]
    cleared, masked, mask_free = sem("a_cleared"), sem("a_masked"), sem("a_mask_free")
    products, products_out = sem("a_products"), sem("a_products_out")
    e_sum, e_step, e_out, flag_step = sem("a_e_sum"), sem("a_e_step"), sem("a_e_out"), sem("a_flag_step")
    e_stored = [sem("a_e_stored0"), sem("a_e_stored1")]
    ns_stored = [sem("a_ns_stored0"), sem("a_ns_stored1")]
    with ExitStack() as ctx:
        m = Mem(nc, ctx)
        a_t = [m.sb(f"a_t{b}", [P, CHUNK, N]) for b in range(2)]
        pos = [m.sb(f"pos{b}", [P, CHUNK, GRP * P], BF16) for b in range(2)]
        neg = [m.sb(f"neg{b}", [P, CHUNK, GRP * P], BF16) for b in range(2)]
        prod_sb = [m.sb(f"prod_sb{b}", [P, 2, CW]) for b in range(2)]
        ns_sb = [m.sb(f"ns_sb{b}", [P, CW]) for b in range(2)]
        e_scl = m.sb("e_scl", [NUV, CW])
        e_sb = [m.sb(f"e_sb{b}", [NUV, CW]) for b in range(2)]
        new_max = m.sb("new_max", [1, 2])
        pos_ps = [m.ps(f"pos_ps{b}", [P, CW]) for b in range(2)]
        neg_ps = [m.ps(f"neg_ps{b}", [P, CW]) for b in range(2)]
        ns_ps = [m.ps(f"ns_ps{b}", [P, CW]) for b in range(2)]
        e_ps = m.ps("e_ps", [P, CW])
        x_sb, uv_parts, off_diag, sel, run_max = (keep[k] for k in ("x_sb", "uv_parts", "off_diag", "sel", "run_max"))
        block = ctx.enter_context(nc.Block())

        @block.sync
        def _(sp):
            def load(b, c):
                for r in range(CHUNK):
                    sp.dma_start(a_t[b][:, r, :],
                                 dram["adj_t"][bass.ds(c * CHUNK + r, 1), :, :].rearrange("a p n -> p (a n)")
                                 ).then_inc(loaded[b], 16)

            for b in range(2):
                load(b, b)
            with sp.Fori(0, NCHUNK // 2 - 1) as i:
                for b in range(2):
                    sp.wait_ge(products, 2 * i + b + 1)
                    load(b, 2 * i + b + 2)

        @block.gpsimd
        def _(pool):
            with pool.Fori(0, NCHUNK // 2) as i:
                for b in range(2):
                    pool.wait_ge(loaded[b], 16 * CHUNK * (i + 1))
                    for r in range(CHUNK):
                        diag = a_t[b][:, r, bass.ds(((2 * i + b) * CHUNK + r) * P, P)]
                        nc.gpsimd.tensor_tensor(diag, diag, off_diag[:, :], ALU.mult).then_inc(cleared, 1)

        @block.vector
        def _(dve):
            for b in range(2):
                nc.vector.memset(prod_sb[b][:, :, :], 0.0).then_inc(e_out, 1)
            with dve.Fori(0, NCHUNK // 2) as i:
                for b in range(2):
                    c = 2 * i + b
                    dve.wait_ge(cleared, CHUNK * (c + 1))
                    for g in range(NGRP):
                        src = a_t[b][:, :, g * GRP * P:(g + 1) * GRP * P]
                        dve.wait_ge(mask_free, NGRP * c + g + 1)
                        nc.vector.tensor_scalar(pos[g % 2][:, :, :], src, 0.0, None, ALU.is_gt)
                        nc.vector.tensor_scalar(neg[g % 2][:, :, :], src, 0.0, None, ALU.is_lt).then_inc(masked, 1)
                    dve.wait_ge(products_out, 3 * (c + 1) + 6)
                    nc.vector.tensor_reduce(new_max[:, :], prod_sb[b][0:1, :, :], AX_X, ALU.max).then_inc(flag_step, 1)
                    dve.wait_ge(flag_step, 2 * c + 1)
                    nc.vector.tensor_tensor(run_max[:, :], run_max[:, :], new_max[:, :], ALU.max).then_inc(flag_step, 1)
                    dve.wait_ge(e_sum, c + 1)
                    nc.vector.tensor_scalar(e_scl[:, :], e_ps[0:NUV, :], ALPHA, None, ALU.mult).then_inc(e_step, 1)
                    dve.wait_ge(e_step, c + 1)
                    dve.wait_ge(e_stored[b], 16 * (i + 1))
                    nc.vector.tensor_tensor(e_sb[b][:, :], e_ps[0:NUV, :], e_scl[:, :], ALU.max).then_inc(e_out, 1)
            dve.wait_ge(flag_step, 2 * NCHUNK)
            nc.vector.tensor_scalar(keep["flags"][0:1, 0:1], run_max[0:1, 1:2], 0.0, None, ALU.is_gt)
            nc.vector.tensor_scalar(keep["flags"][0:1, 1:2], run_max[0:1, 0:1], float(TOPK), None, ALU.is_ge)

        @block.tensor
        def _(pe):
            pe.sem_inc(mask_free, 2)
            with pe.Fori(0, NCHUNK // 2) as i:
                for b in range(2):
                    c = 2 * i + b
                    pe.wait_ge(products_out, 3 * (c + 1))
                    for g in range(NGRP):
                        pe.wait_ge(masked, NGRP * c + g + 1)
                        for j in range(GRP):
                            k = g * GRP + j
                            cols = slice(j * P, (j + 1) * P)
                            first, last = k == 0, k == NB - 1
                            nc.tensor.matmul(pos_ps[b][0:NST, :].rearrange("p (r n) -> p r n", n=P), uv_parts[:, k, :],
                                             pos[g % 2][:, :, cols], start=first, stop=last)
                            mm = nc.tensor.matmul(neg_ps[b][0:NST, :].rearrange("p (r n) -> p r n", n=P), uv_parts[:, k, :],
                                                  neg[g % 2][:, :, cols], start=first, stop=last)
                            if j == GRP - 1:
                                mm.then_inc(mask_free, 1)
                            mm = nc.tensor.matmul(ns_ps[b][:, :].rearrange("p (r n) -> p r n", n=P), x_sb[:, k, :],
                                                  a_t[b][:, :, k * P:(k + 1) * P], start=first, stop=last)
                    mm.then_inc(products, 1)
                    pe.wait_ge(products_out, 3 * (c + 1) + 6)
                    pe.wait_ge(e_out, c + 2)
                    nc.tensor.matmul(e_ps[0:NUV, :], sel[:, 0, :], prod_sb[b][:, 0, :], start=True, stop=False)
                    nc.tensor.matmul(e_ps[0:NUV, :], sel[:, 1, :], prod_sb[b][:, 1, :], start=False, stop=True
                                     ).then_inc(e_sum, 1)

        @block.scalar
        def _(act):
            act.sem_inc(products_out, 6)
            for b in range(2):
                act.sem_inc(e_stored[b], 16)
                act.sem_inc(ns_stored[b], 16)
            with act.Fori(0, NCHUNK // 2) as i:
                for b in range(2):
                    c = 2 * i + b
                    act.wait_ge(products, c + 1)
                    act.wait_ge(e_out, c + 1)
                    nc.scalar.copy(prod_sb[b][0:NST, 0, :], pos_ps[b][0:NST, :]).then_inc(products_out, 1)
                    nc.scalar.copy(prod_sb[b][0:NST, 1, :], neg_ps[b][0:NST, :]).then_inc(products_out, 1)
                    act.wait_ge(ns_stored[b], 16 * (i + 1))
                    nc.scalar.copy(ns_sb[b][:, :], ns_ps[b][:, :]).then_inc(products_out, 1)
                    act.wait_ge(products_out, 3 * (c + 1) + 6)
                    act.dma_start(dram["ns_t"][:, bass.ds(c * CW, CW)], ns_sb[b][:, :]).then_inc(ns_stored[b], 16)
                    act.wait_ge(e_out, c + 3)
                    act.dma_start(dram["e"][:, bass.ds(c * CW, CW)], e_sb[b][:, :]).then_inc(e_stored[b], 16)
            for b in range(2):
                act.wait_ge(ns_stored[b], 16 * (NCHUNK // 2 + 1))
                act.wait_ge(e_stored[b], 16 * (NCHUNK // 2 + 1))


QUARTER = N // 4
UNIT = 2
NUNIT = NB // UNIT
SLOTS = 3


def slot_of(u, b):
    return (u + b) % SLOTS


def units_since(u, b, parities):
    if u >= SLOTS:
        return SLOTS
    before = (b - 1) % parities
    return u + NUNIT - max(v for v in range(NUNIT) if slot_of(v, before) == slot_of(u, b))


def attention_phase(nc, sem, dram, keep, signed):
    tag = "s" if signed else "b"
    sets = 1 if signed else 2
    ahead = 1 + max(units_since(u, b, sets) for u in range(SLOTS) for b in range(sets))
    e_loaded = sem(tag + "_e_loaded")
    row_loaded = [sem(f"{tag}_row_loaded{s}") for s in range(2)]
    sign_done, bias_made, bias_ready = sem(tag + "_sign_done"), sem(tag + "_bias_made"), sem(tag + "_bias_ready")
    logits_done, max_negated, exps_done = sem(tag + "_logits_done"), sem(tag + "_max_negated"), sem(tag + "_exps_done")
    cols_loaded = [sem(f"{tag}_cols_loaded{s}") for s in range(2)]
    transposed, scaled, multiplied = sem(tag + "_transposed"), sem(tag + "_scaled"), sem(tag + "_multiplied")
    y_out = sem(tag + "_y_out")
    y_stored = [sem(f"{tag}_y_stored{s}") for s in range(2)]
    e_neg_loaded, e_neg_used, neg_step = (sem(f"{tag}_{n}") for n in ("e_neg_loaded", "e_neg_used", "neg_step")) if signed else (None,) * 3
    with ExitStack() as ctx:
        m = Mem(nc, ctx)
        e_pos = m.sb(tag + "e_pos", [P, HEADS, N])
        q = [m.sb(f"{tag}q{b}", [P, HEADS, N]) for b in range(sets)]
        bias = [m.sb(f"{tag}bias{b}", [P, N], BF16) for b in range(sets)]
        if signed:
            bias_neg = m.sb(tag + "bias_neg", [P, N], BF16)
            e_neg = m.sb(tag + "e_neg", [P, N])
            logits_neg = m.sb(tag + "logits_neg", [P, N])
        row = [m.sb(f"{tag}row{s}", [P, QUARTER]) for s in range(2)]
        cols = [m.sb(f"{tag}cols{s}", [P, QUARTER]) for s in range(2)]
        s_t = [m.sb(f"{tag}s_t{s}", [P, UNIT, HEADS * P]) for s in range(SLOTS)]
        row_max = m.sb(tag + "row_max", [P, 2, HEADS])
        neg_max = m.sb(tag + "neg_max", [P, 2, HEADS])
        y_sb = [m.sb(f"{tag}y_sb{s}", [P, HEADS * P]) for s in range(2)]
        pause = m.sb(tag + "pause", [P, 1])
        q_t = [m.ps(f"{tag}q_t{s}", [P, UNIT, 512]) for s in range(SLOTS)]
        y_ps = [m.ps(f"{tag}y_ps{b}", [P, 512]) for b in range(2)]
        x_sb, ident, diag_bias, den = keep["x_sb"], keep["ident"], keep["diag_bias"], keep["den"]
        block = ctx.enter_context(nc.Block())

        @block.sync
        def _(sp):
            for h in range(HEADS):
                sp.dma_start(e_pos[:, h, :], dram["e"][h, :].partition_broadcast(P)).then_inc(e_loaded, 16)

            def load_cols(t):
                for k in range(4):
                    sp.wait_ge(scaled, NUNIT // 4 * (4 * t + k - 1) + ahead)
                    sp.dma_start(cols[k % 2][:, :], dram["adj_t"][bass.ds(t, 1), :, k * QUARTER:(k + 1) * QUARTER]
                                 .rearrange("a p n -> p (a n)")).then_inc(cols_loaded[k % 2], 16)

            with sp.Fori(0, NB) as t:
                if signed:
                    for h in range(HEADS):
                        sp.wait_ge(e_neg_used, HEADS * t + h + 1)
                        sp.dma_start(e_neg[:, :], dram["e"][HEADS + h, :].partition_broadcast(P)).then_inc(e_neg_loaded, 16)
                load_cols(t)

        @block.gpsimd
        def _(pool):
            per_tile = 8 if signed else 4
            with pool.Fori(0, NB // sets) as i:
                for b in range(sets):
                    t = sets * i + b
                    pool.wait_ge(bias_made, per_tile * (t + 1))
                    for buf in [bias[b]] + ([bias_neg] if signed else []):
                        diag = buf[:, bass.ds(t * P, P)]
                        nc.gpsimd.tensor_tensor(diag, diag, diag_bias[:, :], ALU.add).then_inc(bias_ready, 1)

        @block.scalar
        def _(act):
            def load_row(t, k):
                act.dma_start(row[k % 2][:, :], dram["adj"][bass.ds(t * P, P), k * QUARTER:(k + 1) * QUARTER]
                              ).then_inc(row_loaded[k % 2], 16)

            def make_bias(t, b, more=True):
                for k in range(4):
                    piece = slice(k * QUARTER, (k + 1) * QUARTER)
                    act.wait_ge(row_loaded[k % 2], 16 * (2 * t + k // 2 + 1))
                    if k == 0:
                        act.wait_ge(logits_done, HEADS * (t + 1))
                    sign = (bias_neg if signed else bias[b])[:, piece]
                    nc.scalar.activation(sign, row[k % 2][:, :], ACT.Sign).then_inc(sign_done, 1)
                    act.wait_ge(sign_done, 4 * t + k + 1)
                    if k < 2:
                        load_row(t, k + 2)
                    elif more:
                        load_row(t + 1, k - 2)
                    if signed:
                        nc.scalar.activation(bias[b][:, piece], sign, ACT.Copy, bias=NEG_INF, scale=-NEG_INF).then_inc(bias_made, 1)
                        act.wait_ge(bias_made, 8 * t + 2 * k + 1)
                        nc.scalar.activation(sign, sign, ACT.Copy, bias=NEG_INF, scale=NEG_INF).then_inc(bias_made, 1)
                    else:
                        nc.scalar.activation(sign, sign, ACT.Copy, bias=NEG_INF, scale=-NEG_INF).then_inc(bias_made, 1)

            def make_exps(t, b):
                for h in range(HEADS):
                    act.wait_ge(logits_done, HEADS * (t + sets) + h + 1)
                    nc.scalar.mul(neg_max[:, b, h:h + 1], row_max[:, b, h:h + 1], -1.0).then_inc(max_negated, 1)
                    act.wait_ge(max_negated, HEADS * t + h + 1)
                    nc.scalar.activation(q[b][:, h, :], q[b][:, h, :], ACT.Exp, bias=neg_max[:, b, h:h + 1],
                                         accum_out=den[:, bass.ds(t, 1), h]).then_inc(exps_done, 1)

            def store_y(t, s, i):
                act.wait_ge(multiplied, NUNIT * (t + 1) + ahead)
                act.wait_ge(y_stored[s], 16 * (i + 1))
                nc.scalar.copy(y_sb[s][:, :], y_ps[s][:, 0:HEADS * P]).then_inc(y_out, 1)
                act.wait_ge(y_out, t + 3)
                act.dma_start(dram["y_t"][bass.ds(t, 1), :, :].rearrange("a p n -> p (a n)"), y_sb[s][:, :]
                              ).then_inc(y_stored[s], 16)

            act.sem_inc(y_out, 2)
            for s in range(2):
                act.sem_inc(y_stored[s], 16)
                load_row(0, s)
            if signed:
                with act.Fori(0, NB // 2 - 1) as i:
                    for s in range(2):
                        make_bias(2 * i + s, 0)
                        make_exps(2 * i + s, 0)
                        store_y(2 * i + s, s, i)
                for t in (NB - 2, NB - 1):
                    make_bias(t, 0, more=t < NB - 1)
                    make_exps(t, 0)
                    store_y(t, t % 2, t // 2)
            else:
                make_bias(0, 0)
                make_bias(1, 1)
                make_exps(0, 0)
                make_bias(2, 0)
                with act.Fori(0, NB // 2 - 2) as i:
                    for s in range(2):
                        make_exps(2 * i + s + 1, 1 - s)
                        store_y(2 * i + s, s, i)
                        make_bias(2 * i + s + 3, 1 - s)
                for t in range(NB - 4, NB):
                    if t + 1 < NB:
                        make_exps(t + 1, 1 - t % 2)
                    store_y(t, t % 2, t // 2)
                    if t + 3 < NB:
                        make_bias(t + 3, 1 - t % 2, more=False)
            for s in range(2):
                act.wait_ge(y_stored[s], 16 * (NB // 2 + 1))

        @block.vector
        def _(dve):
            def logits(t, b, h):
                if h == 0:
                    dve.wait_ge(bias_ready, (2 if signed else 1) * (t + 1))
                    dve.wait_ge(transposed, NUNIT * (t + 1))
                    nc.vector.memset(pause[:, :], 0.0)
                ttr = nc.vector.tensor_tensor_reduce(q[b][:, h, :], bias[b][:, :], e_pos[:, h, :], 1.0, LOWEST,
                                                     ALU.add, ALU.max, row_max[:, b, h:h + 1])
                if not signed:
                    ttr.then_inc(logits_done, 1)
                    return
                ttr.then_inc(neg_step, 1)
                n = 3 * (HEADS * t + h)
                dve.wait_ge(e_neg_loaded, 16 * (HEADS * t + h + 1))
                nc.vector.tensor_tensor(logits_neg[:, :], bias_neg[:, :], e_neg[:, :], ALU.add).then_inc(neg_step, 1)
                dve.wait_ge(neg_step, n + 2)
                dve.sem_inc(e_neg_used, 1)
                nc.vector.tensor_tensor(q[b][:, h, :], q[b][:, h, :], logits_neg[:, :], ALU.max).then_inc(neg_step, 1)
                dve.wait_ge(neg_step, n + 3)
                nc.vector.tensor_reduce(row_max[:, b, h:h + 1], q[b][:, h, :], AX_X, ALU.max).then_inc(logits_done, 1)

            def scale_units(t, b, between):
                for u in range(NUNIT):
                    s, per = slot_of(u, b), NUNIT // 4
                    n = NUNIT * t + u
                    if u % per == 0:
                        k = u // per
                        dve.wait_ge(cols_loaded[k % 2], 16 * (2 * t + k // 2 + 1))
                    dve.wait_ge(transposed, n + 1 + NUNIT * sets)
                    dve.wait_ge(multiplied, n - units_since(u, b, sets) + 1 + ahead)
                    a = cols[u // per % 2][:, (u % per) * UNIT * P:(u % per + 1) * UNIT * P]
                    a = a.rearrange("p (k r) -> p k r", r=P).unsqueeze(2).broadcast_to([P, UNIT, HEADS, P])
                    nc.vector.tensor_tensor(s_t[s][:, :, :].rearrange("p k (h r) -> p k h r", r=P),
                                            q_t[s][:, :, 0:HEADS * P].rearrange("p k (h r) -> p k h r", r=P),
                                            a, ALU.mult).then_inc(scaled, 1)
                    if u in between:
                        between[u]()

            dve.sem_inc(logits_done, HEADS * sets)
            dve.sem_inc(scaled, ahead)
            if signed:
                dve.sem_inc(e_neg_used, 1)
            dve.wait_ge(e_loaded, 16 * HEADS)
            if signed:
                with dve.Fori(0, NB) as t:
                    for h in range(HEADS):
                        logits(t, 0, h)
                    scale_units(t, 0, {})
            else:
                def with_next(t, b):
                    scale_units(t, b, {u: (lambda h=h: logits(t + 1, 1 - b, h)) for h, u in enumerate((0, 3, 6))})

                for h in range(HEADS):
                    logits(0, 0, h)
                with dve.Fori(0, NB // 2 - 1) as i:
                    for b in range(2):
                        with_next(2 * i + b, b)
                with_next(NB - 2, 0)
                scale_units(NB - 1, 1, {})

        @block.tensor
        def _(pe):
            def transposes(t, b, u):
                s = slot_of(u, b)
                pe.wait_ge(scaled, NUNIT * t + u - units_since(u, b, sets) + 1 + ahead)
                for j in range(UNIT):
                    k = UNIT * u + j
                    for h in range(HEADS):
                        mm = nc.tensor.transpose(q_t[s][:, j, h * P:(h + 1) * P], q[b][:, h, k * P:(k + 1) * P], ident[:, :])
                mm.then_inc(transposed, 1)

            def products(t, b, y, u):
                s = slot_of(u, b)
                pe.wait_ge(scaled, NUNIT * t + u + 1 + ahead)
                for j in range(UNIT):
                    k = UNIT * u + j
                    mm = nc.tensor.matmul(y_ps[y][:, 0:HEADS * P], x_sb[:, k, :], s_t[s][:, j, :],
                                          start=k == 0, stop=k == NB - 1)
                mm.then_inc(multiplied, 1)

            def tile(t, b, y):
                pe.wait_ge(exps_done, HEADS * (t + 1))
                pe.wait_ge(y_out, t + 1)
                for u in range(NUNIT + 2):
                    if u < NUNIT:
                        transposes(t, b, u)
                    if u >= 2:
                        products(t, b, y, u - 2)

            pe.sem_inc(transposed, NUNIT * sets)
            pe.sem_inc(multiplied, ahead)
            with pe.Fori(0, NB // 2) as i:
                for y in range(2):
                    tile(2 * i + y, y % sets, y)


def gate_phase(nc, sem, dram, keep):
    w_loaded, bias_step, parts_placed, recip = sem("g_w_loaded"), sem("g_bias_step"), sem("g_parts_placed"), sem("g_recip")
    loaded = [sem("g_loaded0"), sem("g_loaded1")]
    started, es_step, es_transposed, es_copied, node_done = (
        sem("g_" + n) for n in ("started", "es_step", "es_transposed", "es_copied", "node_done"))
    edge_rz, edge_n, node_rz, node_n = (sem("g_" + n) for n in ("edge_rz", "edge_n", "node_rz", "node_n"))
    edge_pre, node_pre, edge_out, node_out, y_step = (
        sem("g_" + n) for n in ("edge_pre", "node_pre", "edge_out", "node_out", "y_step"))
    with ExitStack() as ctx:
        m = Mem(nc, ctx)
        kinds = ("edge", "node")
        gat_w = m.sb("gat_w", [P, HEADS, H])
        wih = {k: m.sb(k + "_wih", [P, 3 * H]) for k in kinds}
        whh = {k: m.sb(k + "_whh", [P, 3 * H]) for k in kinds}
        b_in = {k: m.sb(k + "_b_in", [1, 4 * H]) for k in kinds}
        b_hid = {k: m.sb(k + "_b_hid", [1, 2 * H]) for k in kinds}
        b_parts = {k: m.sb(k + "_b_parts", [1, NPART, 4 * H], BF16) for k in kinds}
        b_rows = {k: m.sb(k + "_b_rows", [NPART, 4 * H], BF16) for k in kinds}
        ones = m.sb("g_ones", [NPART, P], BF16)
        diag = m.sb("g_diag", [P, NB])
        r_den = m.sb("r_den", [P, NB, HEADS])

        def pair(name, shape, make=m.sb):
            return [make(f"{name}{b}", shape) for b in range(2)]

        x_t, ns_t, y_t = pair("g_x_t", [P, P]), pair("g_ns_t", [P, P]), pair("g_y_t", [P, HEADS * P])
        es, es_t = pair("g_es", [P, H]), pair("g_es_t", [P, P])
        rz = {k: pair(k + "_rz", [P, 2 * H]) for k in kinds}
        pre = {k: pair(k + "_pre", [P, H]) for k in kinds}
        n_gate = {k: pair(k + "_n", [P, H]) for k in kinds}
        cell = {k: pair(k + "_cell", [P, H]) for k in kinds}
        z_ps, es_ps = pair("g_z_ps", [P, 512], m.ps), pair("g_es_ps", [P, 512], m.ps)
        gates = {k: pair(k + "_gates", [P, 512], m.ps) for k in kinds}
        x_sb, ident, den, y_all = keep["x_sb"], keep["ident"], keep["den"], keep["y_all"]
        block = ctx.enter_context(nc.Block())

        @block.sync
        def _(sp):
            sp.dma_start(gat_w[:, :, :], dram["gat_W"]).then_inc(w_loaded, 16)
            for k in kinds:
                sp.dma_start(wih[k][:, :], dram[k + "_Wih_t"]).then_inc(w_loaded, 16)
                sp.dma_start(whh[k][:, :], dram[k + "_Whh_t"]).then_inc(w_loaded, 16)
                sp.dma_start(b_in[k][:, 0:3 * H], dram[k + "_bih"].unsqueeze(0)).then_inc(w_loaded, 16)
                sp.dma_start(b_in[k][:, 3 * H:4 * H], dram[k + "_bhh"][2 * H:3 * H].unsqueeze(0)).then_inc(w_loaded, 16)
                sp.dma_start(b_hid[k][:, :], dram[k + "_bhh"][0:2 * H].unsqueeze(0)).then_inc(w_loaded, 16)
            with nc.allow_non_contiguous_dma(reason="the diagonal"):
                sp.dma_start(diag[:, :], dram["adj"].rearrange("a b -> (a b)")[0:N * N:N + 1].rearrange("(t p) -> p t", p=P)
                             ).then_inc(w_loaded, 16)

            def load(t, b):
                sp.wait_ge(started, t + 1)
                sp.dma_start(x_t[b][:, :], dram["x_t"][:, bass.ds(t * P, P)]).then_inc(loaded[b], 16)
                sp.dma_start(ns_t[b][:, :], dram["ns_t"][:, bass.ds(t * P, P)]).then_inc(loaded[b], 16)
                sp.dma_start(y_t[b][:, :], dram["y_t"][bass.ds(t, 1), :, :].rearrange("a p n -> p (a n)")
                             ).then_inc(loaded[b], 16)

            load(0, 0)
            load(1, 1)
            for k in kinds:
                sp.wait_ge(bias_step, 13)
                for j in range(NPART):
                    sp.dma_start(b_rows[k][j:j + 1, :], b_parts[k][:, j, :]).then_inc(parts_placed, 16)
            with sp.Fori(1, NB // 2) as i:
                for b in range(2):
                    load(2 * i + b, b)

        @block.tensor
        def _(pe):
            def start(t, b, half):
                pe.wait_ge(loaded[b], 3 * 16 * (half + 1))
                pe.wait_ge(node_pre, 2 * (t + 1))
                for h in range(HEADS):
                    nc.tensor.matmul(z_ps[b][:, h * H:(h + 1) * H], y_t[b][:, h * P:(h + 1) * P], gat_w[:, h, :],
                                     start=True, stop=True)
                for k in kinds:
                    g = gates[k][b]
                    nc.tensor.matmul(g[:, :], ones[:, :], b_rows[k][:, :], start=True, stop=False)
                    nc.tensor.matmul(g[:, 0:2 * H], x_t[b][:, :], whh[k][:, 0:2 * H], start=False, stop=False)
                    mm = nc.tensor.matmul(g[:, 3 * H:4 * H], x_t[b][:, :], whh[k][:, 2 * H:3 * H], start=False, stop=False)
                    if k == "edge":
                        mm = nc.tensor.matmul(g[:, 0:3 * H], ns_t[b][:, :], wih[k][:, :], start=False, stop=True)
                mm.then_inc(started, 1)

            def transpose_es(t, b):
                pe.wait_ge(es_step, HEADS * (t + 1))
                nc.tensor.transpose(es_ps[b][:, 0:P], es[b][:, :], ident[:, :]).then_inc(es_transposed, 1)

            def finish_node(t, b):
                pe.wait_ge(es_copied, t + 1)
                nc.tensor.matmul(gates["node"][b][:, 0:3 * H], es_t[b][:, :], wih["node"][:, :], start=False, stop=True
                                 ).then_inc(node_done, 1)

            pe.sem_inc(started, 2)
            pe.wait_ge(w_loaded, 16 * 12)
            pe.wait_ge(parts_placed, 16 * 2 * NPART)
            start(0, 0, 0)
            with pe.Fori(0, NB // 2 - 1) as i:
                for b in range(2):
                    transpose_es(2 * i + b, b)
                    start(2 * i + b + 1, 1 - b, i + b)
                    finish_node(2 * i + b, b)
            transpose_es(NB - 2, 0)
            start(NB - 1, 1, NB // 2 - 1)
            finish_node(NB - 2, 0)
            transpose_es(NB - 1, 1)
            finish_node(NB - 1, 1)

        @block.scalar
        def _(act):
            def edge(t, b):
                act.wait_ge(started, t + 3)
                nc.scalar.activation(rz["edge"][b][:, :], gates["edge"][b][:, 0:2 * H], ACT.Tanh, scale=0.5).then_inc(edge_rz, 1)
                act.wait_ge(es_transposed, t + 1)
                nc.scalar.copy(es_t[b][:, :], es_ps[b][:, 0:P]).then_inc(es_copied, 1)
                act.wait_ge(edge_pre, 2 * (t + 1))
                nc.scalar.activation(n_gate["edge"][b][:, :], pre["edge"][b][:, :], ACT.Tanh).then_inc(edge_n, 1)

            def node_last(t, b):
                act.wait_ge(node_pre, 2 * (t + 1) + 4)
                nc.scalar.activation(n_gate["node"][b][:, :], pre["node"][b][:, :], ACT.Tanh).then_inc(node_n, 1)

            def node_first(t, b):
                act.wait_ge(node_done, t + 1)
                nc.scalar.activation(rz["node"][b][:, :], gates["node"][b][:, 0:2 * H], ACT.Tanh, scale=0.5).then_inc(node_rz, 1)

            edge(0, 0)
            node_first(0, 0)
            with act.Fori(0, NB // 2 - 1) as i:
                for s in range(2):
                    t, b = 2 * i + 1 + s, 1 - s
                    edge(t, b)
                    node_last(t - 1, 1 - b)
                    node_first(t, b)
            edge(NB - 1, 1)
            node_last(NB - 2, 0)
            node_first(NB - 1, 1)
            node_last(NB - 1, 1)

        @block.vector
        def _(dve):
            def pre_n(k, t, b, done, rz_ready, extra):
                g = gates[k][b]
                dve.wait_ge(rz_ready, t + 1)
                nc.vector.scalar_tensor_tensor(pre[k][b][:, :], rz[k][b][:, 0:H], 1.0, g[:, 3 * H:4 * H], ALU.add, ALU.mult
                                               ).then_inc(done, 1)
                dve.wait_ge(done, 2 * t + 1 + extra)
                nc.vector.scalar_tensor_tensor(pre[k][b][:, :], pre[k][b][:, :], 0.5, g[:, 2 * H:3 * H], ALU.mult, ALU.add
                                               ).then_inc(done, 1)

            def finish_cell(k, t, b, n_ready, done):
                dve.wait_ge(n_ready, t + 1)
                nc.vector.tensor_tensor(cell[k][b][:, :], x_sb[:, bass.ds(t, 1), :].rearrange("p a f -> p (a f)"),
                                        n_gate[k][b][:, :], ALU.subtract).then_inc(done, 1)
                dve.wait_ge(done, 3 * t + 1)
                nc.vector.scalar_tensor_tensor(cell[k][b][:, :], rz[k][b][:, H:2 * H], 1.0, cell[k][b][:, :], ALU.add, ALU.mult
                                               ).then_inc(done, 1)
                dve.wait_ge(done, 3 * t + 2)
                nc.vector.scalar_tensor_tensor(cell[k][b][:, :], cell[k][b][:, :], 0.5, n_gate[k][b][:, :], ALU.mult, ALU.add
                                               ).then_inc(done, 1)

            def support(t, b):
                dve.wait_ge(started, t + 3)
                for h in range(HEADS):
                    z, r = z_ps[b][:, h * H:(h + 1) * H], r_den[:, bass.ds(t, 1), h]
                    if h == 0:
                        nc.vector.tensor_scalar(es[b][:, :], z, r, None, ALU.mult).then_inc(es_step, 1)
                    else:
                        dve.wait_ge(es_step, HEADS * t + h)
                        nc.vector.scalar_tensor_tensor(es[b][:, :], z, r, es[b][:, :], ALU.mult, ALU.add).then_inc(es_step, 1)

            def finish_tile(t, b):
                dve.wait_ge(edge_out, 3 * (t + 1))
                dve.wait_ge(node_out, 3 * (t + 1))
                nc.vector.tensor_tensor(cell["edge"][b][:, :], cell["edge"][b][:, :], cell["node"][b][:, :], ALU.add
                                        ).then_inc(y_step, 1)
                dve.wait_ge(y_step, 2 * t + 1)
                one = bass.ds(t, 1)
                nc.vector.scalar_tensor_tensor(y_all[:, one, :].rearrange("p a f -> p (a f)"), cell["edge"][b][:, :],
                                               diag[:, one], x_sb[:, one, :].rearrange("p a f -> p (a f)"),
                                               ALU.mult, ALU.add).then_inc(y_step, 1)

            def stage(t, b, before, after):
                if after:
                    support(t, b)
                    pre_n("edge", t, b, edge_pre, edge_rz, 0)
                if before:
                    pre_n("node", t - 1, 1 - b, node_pre, node_rz, 4)
                if after:
                    finish_cell("edge", t, b, edge_n, edge_out)
                if before:
                    finish_cell("node", t - 1, 1 - b, node_n, node_out)
                    finish_tile(t - 1, 1 - b)

            nc.vector.memset(ones[:, :], 1.0).then_inc(bias_step, 1)
            dve.wait_ge(w_loaded, 16 * 12)
            n = 1
            for k in kinds:
                nc.vector.tensor_tensor(b_in[k][:, 0:2 * H], b_in[k][:, 0:2 * H], b_hid[k][:, :], ALU.add).then_inc(bias_step, 1)
                n += 1
                for j in range(NPART):
                    dve.wait_ge(bias_step, n)
                    nc.vector.tensor_copy(b_parts[k][:, j, :], b_in[k][:, :]).then_inc(bias_step, 1)
                    n += 1
                    if j < NPART - 1:
                        dve.wait_ge(bias_step, n)
                        nc.vector.tensor_tensor(b_in[k][:, :], b_in[k][:, :], b_parts[k][:, j, :], ALU.subtract).then_inc(bias_step, 1)
                        n += 1
            nc.vector.reciprocal(r_den[:, :, :], den[:, :, :]).then_inc(recip, 1)
            dve.wait_ge(recip, 1)
            nc.vector.tensor_scalar(r_den[:, :, :], r_den[:, :, :], 1.0 / HEADS, None, ALU.mult).then_inc(recip, 1)
            dve.wait_ge(recip, 2)
            dve.sem_inc(node_pre, 4)
            stage(0, 0, False, True)
            with dve.Fori(0, NB // 2 - 1) as i:
                for s in range(2):
                    stage(2 * i + 1 + s, 1 - s, True, True)
            stage(NB - 1, 1, True, True)
            stage(NB, 0, True, False)


LN_STEPS = 6


def layer_norm(nc, dve, step, squared, rooted, y, mean, var, root, square, rows):
    wide = [P, rows, H]
    nc.vector.tensor_reduce(mean[:, :], y, AX_X, ALU.add).then_inc(step, 1)
    dve.wait_ge(step, 1)
    nc.vector.tensor_scalar(mean[:, :], mean[:, :], 1.0 / H, None, ALU.mult).then_inc(step, 1)
    dve.wait_ge(step, 2)
    nc.vector.tensor_tensor(y, y, mean[:, :].unsqueeze(2).broadcast_to(wide), ALU.subtract).then_inc(step, 1)
    dve.wait_ge(squared, 1)
    nc.vector.tensor_reduce(var[:, :], square[:, :, :], AX_X, ALU.add).then_inc(step, 1)
    dve.wait_ge(step, 4)
    nc.vector.tensor_scalar(var[:, :], var[:, :], 1.0 / H, EPS, ALU.mult, ALU.add).then_inc(step, 1)
    dve.wait_ge(rooted, 1)
    nc.vector.reciprocal(root[:, :], root[:, :]).then_inc(rooted, 1)
    dve.wait_ge(rooted, 2)
    nc.vector.tensor_tensor(y, y, root[:, :].unsqueeze(2).broadcast_to(wide), ALU.mult).then_inc(step, 1)


def layer_norm_act(nc, act, step, squared, rooted, y, var, root, square):
    act.wait_ge(step, 3)
    nc.scalar.activation(square[:, :, :], y, ACT.Square).then_inc(squared, 1)
    act.wait_ge(step, 5)
    nc.scalar.activation(root[:, :], var[:, :], ACT.Sqrt).then_inc(rooted, 1)


def norm_phase(nc, sem, dram, keep):
    w_loaded, step, squared, rooted = sem("u_w_loaded"), sem("u_step"), sem("u_squared"), sem("u_rooted")
    x_turned, x_copied, projected, activated, multiplied, copied = (
        sem("u_" + n) for n in ("x_turned", "x_copied", "projected", "activated", "multiplied", "copied"))
    with ExitStack() as ctx:
        m = Mem(nc, ctx)
        w_proj, w_gcn, b_proj = m.sb("w_proj", [P, H]), m.sb("w_gcn", [P, H]), m.sb("b_proj", [P, 1])
        square = m.sb("u_square", [P, NB, H])
        mean, var, root = m.sb("u_mean", [P, NB]), m.sb("u_var", [P, NB]), m.sb("u_root", [P, NB])
        x1_t = [m.sb(f"x1_t{b}", [P, CW]) for b in range(2)]
        h2_t = [m.sb(f"h2_t{b}", [P, CW]) for b in range(2)]
        x1_ps = [m.ps(f"x1_ps{b}", [P, CW]) for b in range(2)]
        h2_ps = [m.ps(f"h2_ps{b}", [P, CW]) for b in range(2)]
        g_ps = [m.ps(f"g_ps{b}", [P, CW]) for b in range(2)]
        x1, g_all, ident = keep["y_all"], keep["g_all"], keep["ident"]
        block = ctx.enter_context(nc.Block())

        @block.sync
        def _(sp):
            sp.dma_start(w_proj[:, :], dram["W_proj"]).then_inc(w_loaded, 16)
            sp.dma_start(w_gcn[:, :], dram["W_gcn"]).then_inc(w_loaded, 16)
            sp.dma_start(b_proj[:, :], dram["b_proj"].unsqueeze(1)).then_inc(w_loaded, 16)

        @block.vector
        def _(dve):
            layer_norm(nc, dve, step, squared, rooted, x1[:, :, :], mean, var, root, square, NB)
            for c in range(NCHUNK):
                b = c % 2
                dve.wait_ge(x_turned, c + 1)
                nc.vector.tensor_copy(x1_t[b][:, :], x1_ps[b][:, :]).then_inc(x_copied, 1)
                if c >= 1:
                    dve.wait_ge(multiplied, c)
                    nc.vector.tensor_copy(g_all[:, (c - 1) * CHUNK:c * CHUNK, :].rearrange("p r f -> p (r f)"), g_ps[1 - b][:, :]
                                          ).then_inc(copied, 1)
            dve.wait_ge(multiplied, NCHUNK)
            nc.vector.tensor_copy(g_all[:, (NCHUNK - 1) * CHUNK:, :].rearrange("p r f -> p (r f)"), g_ps[(NCHUNK - 1) % 2][:, :]
                                  ).then_inc(copied, 1)

        @block.scalar
        def _(act):
            layer_norm_act(nc, act, step, squared, rooted, x1[:, :, :], var, root, square)
            act.wait_ge(w_loaded, 48)
            for c in range(NCHUNK):
                act.wait_ge(projected, c + 1)
                nc.scalar.activation(h2_t[c % 2][:, :], h2_ps[c % 2][:, :], ACT.Tanh, bias=b_proj[:, :]).then_inc(activated, 1)

        @block.tensor
        def _(pe):
            def turn(c):
                if c >= 2:
                    pe.wait_ge(x_copied, c - 1)
                for r in range(CHUNK):
                    mm = nc.tensor.transpose(x1_ps[c % 2][:, r * P:(r + 1) * P], x1[:, c * CHUNK + r, :], ident[:, :])
                mm.then_inc(x_turned, 1)

            def project(c):
                pe.wait_ge(x_copied, c + 1)
                nc.tensor.matmul(h2_ps[c % 2][:, :], w_proj[:, :], x1_t[c % 2][:, :], start=True, stop=True).then_inc(projected, 1)

            pe.wait_ge(w_loaded, 48)
            pe.wait_ge(step, LN_STEPS)
            turn(0)
            project(0)
            for c in range(NCHUNK):
                if c + 1 < NCHUNK:
                    turn(c + 1)
                    project(c + 1)
                pe.wait_ge(activated, c + 1)
                if c >= 2:
                    pe.wait_ge(copied, c - 1)
                for r in range(CHUNK):
                    mm = nc.tensor.matmul(g_ps[c % 2][:, r * P:(r + 1) * P], h2_t[c % 2][:, r * P:(r + 1) * P], w_gcn[:, :],
                                          start=True, stop=True)
                mm.then_inc(multiplied, 1)


def graph_phase(nc, sem, dram, keep, source):
    tag = {"adj_t": "f", "adj_top_t": "t"}[source]
    loaded = [sem(f"{tag}_loaded0"), sem(f"{tag}_loaded1")]
    b_loaded, squared_a, filtered, products = (sem(tag + n) for n in ("_b_loaded", "_squared_a", "_filtered", "_products"))
    relu_done, turned, y_done = (sem(tag + n) for n in ("_relu_done", "_turned", "_y_done"))
    step, squared, rooted, stored = (sem(tag + n) for n in ("_step", "_squared", "_rooted", "_stored"))
    with ExitStack() as ctx:
        m = Mem(nc, ctx)
        a_t = [m.sb(f"{tag}f_t{b}", [P, CHUNK, N]) for b in range(2)]
        b_gcn = m.sb(tag + "b_gcn", [P, 1])
        feat_t = [m.sb(f"{tag}feat_t{b}", [P, CW]) for b in range(2)]
        y2 = m.sb(tag + "y2", [P, NB, H])
        mean, var, root = (m.sb(tag + n, [P, NB]) for n in ("mean", "var", "root"))
        f_ps = [m.ps(f"{tag}f_ps{b}", [P, CW]) for b in range(2)]
        y_ps = [m.ps(f"{tag}yt_ps{b}", [P, CW]) for b in range(2)]
        x1, g_all, ident = keep["y_all"], keep["g_all"], keep["ident"]
        square = a_t[0][:, 0, :].rearrange("p (t f) -> p t f", f=H)
        block = ctx.enter_context(nc.Block())

        @block.sync
        def _(sp):
            def load(b, c):
                for r in range(CHUNK):
                    sp.dma_start(a_t[b][:, r, :], dram[source][bass.ds(c * CHUNK + r, 1), :, :].rearrange("a p n -> p (a n)")
                                 ).then_inc(loaded[b], 16)

            sp.dma_start(b_gcn[:, :], dram["b_gcn"].unsqueeze(1)).then_inc(b_loaded, 16)
            for b in range(2):
                load(b, b)
            with sp.Fori(0, NCHUNK // 2 - 1) as i:
                for b in range(2):
                    sp.wait_ge(products, 2 * i + b + 1)
                    load(b, 2 * i + b + 2)
            sp.wait_ge(step, LN_STEPS)
            sp.dma_start(dram["out"].rearrange("(t p) f -> p t f", p=P), y2[:, :, :]).then_inc(stored, 16)
            sp.wait_ge(stored, 16)

        @block.gpsimd
        def _(pool):
            pool.sem_inc(y_done, 2)

        def group(b, g):
            return a_t[b][:, :, g * GRP * P:(g + 1) * GRP * P]

        @block.vector
        def _(dve):
            def square_a(c, b, i):
                dve.wait_ge(loaded[b], 16 * CHUNK * (i + 1))
                for g in range(NGRP):
                    nc.vector.scalar_tensor_tensor(group(b, g), group(b, g), 0.0, group(b, g), ALU.max, ALU.mult
                                                   ).then_inc(squared_a, 1)

            def add_x1(c, b):
                dve.wait_ge(turned, c + 3)
                rows = bass.ds(c * CHUNK, CHUNK)
                nc.vector.tensor_tensor(y2[:, rows, :], y_ps[b][:, :].rearrange("p (r f) -> p r f", f=H), x1[:, rows, :],
                                        ALU.add).then_inc(y_done, 1)

            square_a(0, 0, 0)
            with dve.Fori(0, NCHUNK // 2 - 1) as i:
                square_a(2 * i + 1, 1, i)
                add_x1(2 * i, 0)
                square_a(2 * i + 2, 0, i + 1)
                add_x1(2 * i + 1, 1)
            square_a(NCHUNK - 1, 1, NCHUNK // 2 - 1)
            add_x1(NCHUNK - 2, 0)
            add_x1(NCHUNK - 1, 1)
            dve.wait_ge(y_done, NCHUNK + 2)
            layer_norm(nc, dve, step, squared, rooted, y2[:, :, :], mean, var, root, square, NB)

        @block.scalar
        def _(act):
            def tanh(c, b):
                for g in range(NGRP):
                    act.wait_ge(squared_a, NGRP * c + g + 1)
                    nc.scalar.activation(group(b, g), group(b, g), ACT.Tanh).then_inc(filtered, 1)

            def relu(c, b):
                act.wait_ge(products, c + 1)
                act.wait_ge(turned, c + 1)
                nc.scalar.activation(feat_t[b][:, :], f_ps[b][:, :], ACT.Relu, bias=b_gcn[:, :]).then_inc(relu_done, 1)

            tanh(0, 0)
            act.wait_ge(b_loaded, 16)
            with act.Fori(0, NCHUNK // 2 - 1) as i:
                for s in range(2):
                    tanh(2 * i + 1 + s, 1 - s)
                    relu(2 * i + s, s)
            tanh(NCHUNK - 1, 1)
            relu(NCHUNK - 2, 0)
            relu(NCHUNK - 1, 1)
            layer_norm_act(nc, act, step, squared, rooted, y2[:, :, :], var, root, square)

        @block.tensor
        def _(pe):
            def turn(c, b):
                pe.wait_ge(relu_done, c + 1)
                pe.wait_ge(y_done, c + 1)
                for r in range(CHUNK):
                    mm = nc.tensor.transpose(y_ps[b][:, r * P:(r + 1) * P], feat_t[b][:, r * P:(r + 1) * P], ident[:, :])
                mm.then_inc(turned, 1)

            def products_of(c, b, turn_before):
                for g in range(NGRP):
                    pe.wait_ge(filtered, NGRP * c + g + 1)
                    for j in range(GRP):
                        k = g * GRP + j
                        mm = nc.tensor.matmul(f_ps[b][:, :].rearrange("p (r n) -> p r n", n=P), g_all[:, k, :],
                                              a_t[b][:, :, k * P:(k + 1) * P], start=k == 0, stop=k == NB - 1)
                    if g == 1 and turn_before:
                        turn(c - 1, 1 - b)
                mm.then_inc(products, 1)

            pe.sem_inc(turned, 2)
            products_of(0, 0, False)
            with pe.Fori(0, NCHUNK // 2 - 1) as i:
                for s in range(2):
                    products_of(2 * i + 1 + s, 1 - s, True)
            products_of(NCHUNK - 1, 1, True)
            turn(NCHUNK - 1, 1)


def top_k_phase(nc, sem, dram, keep):
    PAD = -TOPK % 8
    ROUNDS = (TOPK + PAD) // 8
    W = PAD + N
    loaded, stored = sem("k_loaded"), sem("k_stored")
    padded, filtered, step, found, removed, kept, turned, copied = (
        sem("k_" + n) for n in ("padded", "filtered", "step", "found", "removed", "kept", "turned", "copied"))
    with ExitStack() as ctx:
        m = Mem(nc, ctx)
        row, f, left, out_t = m.sb("k_row", [P, N]), m.sb("k_f", [P, W]), m.sb("k_left", [P, W]), m.sb("k_out_t", [P, N])
        best, pause = m.sb("k_best", [P, 8]), m.sb("k_pause", [P, 1])
        ps = [m.ps(f"k_ps{b}", [P, CW]) for b in range(2)]
        ident = keep["ident"]
        block = ctx.enter_context(nc.Block())

        @block.sync
        def _(sp):
            with sp.Fori(0, NB) as t:
                sp.wait_ge(turned, NCHUNK * (t + 1))
                sp.dma_start(row[:, :], dram["adj"][bass.ds(t * P, P), :]).then_inc(loaded, 16)
                sp.wait_ge(copied, NCHUNK * (t + 1) + 2)
                sp.dma_start(dram["adj_top_t"][bass.ds(t, 1), :, :].rearrange("a p n -> p (a n)"), out_t[:, :]).then_inc(stored, 16)
            sp.wait_ge(stored, 16 * (NB + 1))

        @block.scalar
        def _(act):
            with act.Fori(0, NB) as t:
                act.wait_ge(step, 3 * t + 1)
                nc.scalar.activation(f[:, PAD:W], f[:, PAD:W], ACT.Tanh).then_inc(filtered, 1)

        @block.vector
        def _(dve):
            nc.vector.memset(f[:, 0:PAD], 2.0).then_inc(padded, 1)
            dve.wait_ge(padded, 1)
            dve.sem_inc(stored, 16)
            with dve.Fori(0, NB) as t:
                dve.wait_ge(loaded, 16 * (t + 1))
                nc.vector.scalar_tensor_tensor(f[:, PAD:W], row[:, :], 0.0, row[:, :], ALU.max, ALU.mult).then_inc(step, 1)
                dve.wait_ge(filtered, t + 1)
                nc.vector.tensor_copy(left[:, :], f[:, :]).then_inc(step, 1)
                dve.wait_ge(step, 3 * t + 2)
                nc.vector.memset(pause[:, :], 0.0)
                with dve.Fori(0, ROUNDS) as r:
                    nc.vector.max(best[:, :], left[:, :]).then_inc(found, 1)
                    dve.wait_ge(found, t * ROUNDS + r + 1)
                    nc.vector.memset(pause[:, :], 0.0)
                    nc.vector.match_replace(left[:, :], best[:, :], left[:, :], -1.0).then_inc(removed, 1)
                    dve.wait_ge(removed, t * ROUNDS + r + 1)
                    nc.vector.memset(pause[:, :], 0.0)
                nc.vector.tensor_tensor(left[:, PAD:W], left[:, PAD:W], f[:, PAD:W], ALU.not_equal).then_inc(step, 1)
                dve.wait_ge(step, 3 * t + 3)
                nc.vector.tensor_tensor(row[:, :], row[:, :], left[:, PAD:W], ALU.mult).then_inc(kept, 1)
                dve.wait_ge(stored, 16 * (t + 1))
                for c in range(NCHUNK):
                    dve.wait_ge(turned, NCHUNK * (t + 1) + c + 1)
                    nc.vector.tensor_copy(out_t[:, c * CW:(c + 1) * CW], ps[c % 2][:, :]).then_inc(copied, 1)

        @block.tensor
        def _(pe):
            pe.sem_inc(turned, NCHUNK)
            pe.sem_inc(copied, 2)
            with pe.Fori(0, NB) as t:
                pe.wait_ge(kept, t + 1)
                for c in range(NCHUNK):
                    pe.wait_ge(copied, NCHUNK * t + c + 1)
                    for r in range(CHUNK):
                        k = c * CHUNK + r
                        mm = nc.tensor.transpose(ps[c % 2][:, r * P:(r + 1) * P], row[:, k * P:(k + 1) * P], ident[:, :])
                    mm.then_inc(turned, 1)


def build(nc, dram):
    with ExitStack() as top:
        def sem(name):
            return top.enter_context(nc.semaphore(name))

        m = Mem(nc, top)
        keep = {
            "ident": m.sb("ident", [P, P]),
            "off_diag": m.sb("off_diag", [P, P]),
            "sel": m.sb("sel", [P, 2, NUV]),
            "diag_bias": m.sb("diag_bias", [P, P], BF16),
            "den": m.sb("den", [P, NB, HEADS]),
            "run_max": m.sb("run_max", [1, 2]),
            "flags": m.sb("flags", [1, 2], I32),
        }
        keep["x_sb"] = keep["y_all"] = m.sb("x_sb", [P, NB, H])
        with ExitStack() as masks:
            keep["uv_parts"] = Mem(nc, masks).sb("uv_parts", [P, NB, NST], BF16)
            setup_phase(nc, sem, dram, keep)
            mask_phase(nc, sem, dram, keep)
        negative = nc.values_load(keep["flags"][0:1, 0:1], min_val=0, max_val=1)
        with nc.If(negative):
            attention_phase(nc, sem, dram, keep, signed=True)
        with nc.Else():
            attention_phase(nc, sem, dram, keep, signed=False)
        gate_phase(nc, sem, dram, keep)
        keep["g_all"] = m.sb("g_all", [P, NB, H])
        norm_phase(nc, sem, dram, keep)
        many = nc.values_load(keep["flags"][0:1, 1:2], min_val=0, max_val=1)
        with nc.If(many):
            top_k_phase(nc, sem, dram, keep)
            graph_phase(nc, sem, dram, keep, "adj_top_t")
        with nc.Else():
            graph_phase(nc, sem, dram, keep, "adj_t")


def host_constants():
    import numpy as np

    ident = np.eye(P, dtype=np.float32)
    sel = np.zeros((P, 2, NUV), np.float32)
    for k in range(NPART):
        for h in range(HEADS):
            u, v = 1 + k * NUV + 2 * h, 1 + k * NUV + 2 * h + 1
            sel[u, 0, h] = sel[v, 1, h] = 1.0
            sel[v, 0, HEADS + h] = sel[u, 1, HEADS + h] = 1.0
    return {"ident": ident, "off_diag": 1.0 - ident, "sel": sel}


def host_layout(inputs):
    import numpy as np

    adj, x = np.asarray(inputs["adj"]), np.asarray(inputs["x"])
    lay = {
        "x": x,
        "x_t": x.T,
        "adj": adj,
        "adj_t": adj.reshape(NB, P, NB, P).transpose(0, 3, 2, 1).reshape(NB, P, N),
        "gat_W": np.asarray(inputs["L0_gnn_gat_W"]).transpose(1, 0, 2),
        "gat_W_t": np.asarray(inputs["L0_gnn_gat_W"]).transpose(0, 2, 1),
        "gat_a": np.asarray(inputs["L0_gnn_gat_a"]).reshape(HEADS, 2, H).transpose(2, 0, 1),
    }
    for k in ("edge", "node"):
        for w in ("Wih", "Whh"):
            lay[f"{k}_{w}_t"] = np.asarray(inputs[f"L0_gnn_{k}_{w}"]).T
        for w in ("bih", "bhh"):
            lay[f"{k}_{w}"] = np.asarray(inputs[f"L0_gnn_{k}_{w}"])
    for k in ("W_proj", "b_proj", "W_gcn", "b_gcn"):
        lay[k] = np.asarray(inputs[f"L1_gnn_{k}"])
    return {k: np.ascontiguousarray(v) for k, v in lay.items()}


def kernel(**inputs):
    import concourse.bacc as bacc
    from concourse.bass_utils import run_bass_kernel_spmd as run

    nc = bacc.Bacc("TRN2", target_bir_lowering=False, num_devices=1)
    arrays, dram = {}, {}
    for name, a in {**host_layout(inputs), **host_constants()}.items():
        arrays["in_" + name] = a
        dram[name] = nc.dram_tensor("in_" + name, a.shape, mybir.dt.from_np(a.dtype), kind="ExternalInput").ap()
    for name, shape in SCRATCH.items():
        dram[name] = nc.dram_tensor("scratch_" + name, shape, F32, kind="Internal").ap()
    dram["out"] = nc.dram_tensor("out", (N, H), F32, kind="ExternalOutput").ap()
    build(nc, dram)
    return run(nc, [arrays], core_ids=[0]).results[0]["out"]
```

```python
from contextlib import ExitStack

import concourse.bass as bass
from concourse import mybir

ALU = mybir.AluOpType
ACT = mybir.ActivationFunctionType
AX_X = mybir.AxisListType.X
F32 = mybir.dt.float32
F32R = mybir.dt.float32r
BF16 = mybir.dt.bfloat16
I32 = mybir.dt.int32

P = 128
N = 4096
H = 128
HEADS = 3
NB = N // P
CHUNK = 4
CW = CHUNK * P
NCHUNK = NB // CHUNK
GRP = 8
NGRP = NB // GRP
PIECE = 4
PW = PIECE * P
NPIECE = NB // PIECE
RING = 8
HIS = 4
ALPHA = 0.2
NEG_INF = -9000000000000000.0
TOPK = 350
EPS = 1e-5
NPART = 3
NUV = 2 * HEADS
NST = 1 + NPART * NUV
LOWEST = -3.0e38
SCRATCH = {
    "e": (HEADS, N),
    "e_signed": (NUV, N),
    "ns_t": (P, N),
    "y_t": (NB, P, HEADS * P),
    "adj_top_t": (NB, P, N),
}


class Mem:

    def __init__(self, nc, ctx):
        self.nc, self.ctx = nc, ctx

    def sb(self, name, shape, dt=F32):
        return self.ctx.enter_context(self.nc.sbuf_tensor(name, shape, dt))

    def ps(self, name, shape, dt=F32):
        return self.ctx.enter_context(self.nc.psum_tensor(name, shape, dt))


def load_piece(sp, dram, keep, c, g):
    sp.dma_start(keep["pieces"][:, g % RING, :, :],
                 dram["adj_t"][bass.ds(c * CHUNK, CHUNK), :, g * PW:(g + 1) * PW].rearrange("r p n -> p r n")
                 ).then_inc(keep["loaded"][g % RING], 16)


def setup_phase(nc, sem, dram, keep):
    x_ready, x_t_ready, w_ready = sem("s_x"), sem("s_xT"), sem("s_w")
    folded, folded_out = sem("s_folded"), sem("s_folded_out")
    uv_done, uv_out = sem("s_uv_done"), sem("s_uv_out")
    split, x_split = sem("s_split"), sem("s_x_split")
    with ExitStack() as ctx:
        m = Mem(nc, ctx)
        x_t = m.sb("x_t", [P, N])
        w_t = m.sb("w_t", [P, HEADS, H])
        a_sb = m.sb("a_sb", [P, HEADS, 2])
        w6 = m.sb("w6", [P, NUV])
        uv = m.sb("uv", [P, NB, NUV])
        rest = m.sb("rest", [P, NB, NUV])
        w6_ps = m.ps("w6_ps", [P, 512])
        uv_ps = m.ps("uv_ps", [P, 512])
        x_sb, uv_parts, ident, off_diag = keep["x_sb"], keep["uv_parts"], keep["ident"], keep["off_diag"]
        part = [uv_parts[:, :, 1 + k * NUV:1 + (k + 1) * NUV] for k in range(NPART)]
        block = ctx.enter_context(nc.Block())

        @block.sync
        def _(sp):
            sp.dma_start(w_t[:, :, :], dram["gat_W_t"].rearrange("h g f -> g h f")).then_inc(w_ready, 16)
            sp.dma_start(a_sb[:, :, :], dram["gat_a"]).then_inc(w_ready, 16)
            sp.dma_start(x_t[:, :], dram["x_t"]).then_inc(x_t_ready, 16)
            sp.dma_start(x_sb[:, :, :], dram["x"].rearrange("(t p) f -> p t f", p=P)).then_inc(x_ready, 16)
            sp.dma_start(ident[:, :], dram["ident"]).then_inc(x_ready, 16)
            sp.dma_start(off_diag[:, :], dram["off_diag"]).then_inc(x_ready, 16)
            sp.dma_start(keep["sel"][:, :], dram["sel"]).then_inc(x_ready, 16)
            for g in range(RING):
                load_piece(sp, dram, keep, 0, g)
            sp.wait_ge(x_ready, 64)

        @block.tensor
        def _(pe):
            pe.wait_ge(w_ready, 32)
            for h in range(HEADS):
                last = nc.tensor.matmul(w6_ps[:, 2 * h:2 * h + 2], w_t[:, h, :], a_sb[:, h, :], start=True, stop=True)
            last.then_inc(folded, 1)
            pe.wait_ge(folded_out, 1)
            pe.wait_ge(x_t_ready, 16)
            for t in range(NB):
                last = nc.tensor.matmul(uv_ps[:, t * NUV:(t + 1) * NUV], x_t[:, t * P:(t + 1) * P], w6[:, :],
                                        start=True, stop=True)
            last.then_inc(uv_done, 1)

        @block.vector
        def _(dve):
            nc.vector.memset(keep["ones"][:, :], 1.0)
            dve.wait_ge(x_ready, 64)
            nc.vector.tensor_scalar(keep["diag_bias"][:, :], ident[:, :], NEG_INF, None, ALU.mult)
            nc.vector.memset(uv_parts[:, :, 0:1], 1.0)
            nc.vector.memset(keep["clear"][:, :, :], 1.0).then_inc(x_split, 1)
            nc.vector.tensor_copy(keep["x_hi"][:, :, :], x_sb[:, :, :]).then_inc(x_split, 1)
            dve.wait_ge(x_split, 2)
            nc.vector.tensor_copy(keep["clear"][:, NPIECE - 1, :], off_diag[:, :])
            nc.vector.tensor_tensor(keep["x_lo"][:, :, :], x_sb[:, :, :], keep["x_hi"][:, :, :].bitcast(F32), ALU.subtract)
            dve.wait_ge(folded, 1)
            nc.vector.tensor_copy(w6[:, :], w6_ps[:, 0:NUV]).then_inc(folded_out, 1)
            dve.wait_ge(uv_done, 1)
            nc.vector.tensor_copy(uv[:, :, :], uv_ps[:, 0:NB * NUV].rearrange("p (t j) -> p t j", j=NUV)).then_inc(uv_out, 1)
            dve.wait_ge(uv_out, 1)
            left = uv
            for k in range(NPART):
                nc.vector.tensor_copy(part[k], left[:, :, :]).then_inc(split, 1)
                dve.wait_ge(split, 2 * k + 1)
                if k < NPART - 1:
                    nc.vector.tensor_tensor(rest[:, :, :], left[:, :, :], part[k], ALU.subtract).then_inc(split, 1)
                    dve.wait_ge(split, 2 * k + 2)
                    left = rest


def support_phase(nc, sem, dram, keep):
    cleared, rounded, made, piece_done = sem("a_cleared"), sem("a_rounded"), sem("a_made"), sem("a_piece_done")
    products_out, e_sum, e_out, counted = sem("a_products_out"), sem("a_e_sum"), sem("a_e_out"), sem("a_counted")
    signed, paused = sem("a_signed"), sem("a_paused")
    e_step, flag_step, signs_added, signs_total = sem("a_e_step"), sem("a_flag_step"), sem("a_signs_added"), sem("a_signs_total")
    e_stored = [sem("a_e_stored0"), sem("a_e_stored1")]
    ns_stored = [sem("a_ns_stored0"), sem("a_ns_stored1")]
    with ExitStack() as ctx:
        m = Mem(nc, ctx)
        a_hi = [m.sb(f"a_hi{b}", [P, CHUNK, PW], F32R) for b in range(HIS)]
        pos = [m.sb(f"pos{b}", [P, CHUNK, PW], BF16) for b in range(2)]
        a_lo = [m.sb(f"a_lo{b}", [P, CHUNK, PW], F32R) for b in range(2)]
        signs = [m.sb(f"signs{b}", [P, CHUNK, PW], BF16) for b in range(2)]
        prod_sb = [m.sb(f"prod_sb{b}", [P, CW]) for b in range(2)]
        ns_sb = [m.sb(f"ns_sb{b}", [P, CW]) for b in range(2)]
        e_scl = m.sb("e_scl", [HEADS, CW])
        e_sb = [m.sb(f"e_sb{b}", [HEADS, CW]) for b in range(2)]
        pause = m.sb("a_pause", [P, 1])
        sign_sums = m.sb("sign_sums", [P, NCHUNK * NPIECE])
        sign_sum = m.sb("sign_sum", [P, 1])
        counts = m.sb("counts", [NST, NCHUNK])
        max_counts = m.sb("max_counts", [1, NCHUNK])
        max_count, count, negatives = m.sb("max_count", [1, 1]), m.sb("count", [1, 1]), m.sb("negatives", [1, 1])
        pos_ps = [m.ps(f"pos_ps{b}", [P, CW]) for b in range(2)]
        ns_ps = [m.ps(f"ns_ps{b}", [P, CW]) for b in range(2)]
        e_ps = m.ps("e_ps", [P, CW])
        total_ps = m.ps("total_ps", [P, CW])
        pieces, loaded, clear, x_hi, x_lo, uv_parts, sel = (
            keep[k] for k in ("pieces", "loaded", "clear", "x_hi", "x_lo", "uv_parts", "sel"))
        block = ctx.enter_context(nc.Block())

        @block.sync
        def _(sp):
            def load(c, g):
                sp.wait_ge(made, 2 * (NPIECE * c + g - RING + 2))
                load_piece(sp, dram, keep, c, g)

            for g in range(RING, NPIECE):
                load(0, g)
            with sp.Fori(1, NCHUNK) as c:
                for g in range(NPIECE):
                    load(c, g)

        @block.gpsimd
        def _(pool):
            pool.sem_inc(paused, 1)
            with pool.Fori(0, NCHUNK) as c:
                for g in range(NPIECE):
                    pool.wait_ge(loaded[g % RING], 16 * (NPIECE // RING * c + g // RING + 1))
                    pool.wait_ge(paused, NPIECE * c + g + 1)
                    nc.gpsimd.tensor_tensor(pause[:, :], keep["ones"][:, :], keep["ones"][:, :], ALU.mult).then_inc(paused, 1)
                    factor = clear[:, bass.ds(NPIECE - 1 + g - c, 1), :].rearrange("p a n -> p (a n)")
                    for r in range(CHUNK):
                        one = pieces[:, g % RING, r, r * P:(r + 1) * P]
                        nc.gpsimd.tensor_tensor(one, one, factor, ALU.mult).then_inc(cleared, 1)

        @block.scalar
        def _(act):
            act.sem_inc(products_out, 4)
            act.sem_inc(signed, 2)
            for b in range(2):
                act.sem_inc(e_stored[b], 16)
                act.sem_inc(ns_stored[b], 16)

            def split(c, b, g):
                n = NPIECE * c + g
                act.wait_ge(cleared, CHUNK * (n + 1))
                act.wait_ge(piece_done, n + 1)
                nc.scalar.copy(a_hi[g % HIS][:, :, :], pieces[:, g % RING, :, :]).then_inc(rounded, 1)
                act.wait_ge(signed, n + 1)
                nc.scalar.activation(signs[g % 2][:, :, :], pieces[:, g % RING, :, :], ACT.Sign,
                                     accum_out=sign_sums[:, bass.ds(n, 1)]).then_inc(signed, 1)

            def take_out(c, b, i):
                act.wait_ge(piece_done, NPIECE * (c + 1) + HIS)
                act.wait_ge(e_sum, c + 1)
                act.wait_ge(counted, c + 1)
                nc.scalar.activation(prod_sb[b][0:NST, :], pos_ps[b][0:NST, :], ACT.Copy,
                                     accum_out=counts[:, bass.ds(c, 1)]).then_inc(products_out, 1)
                act.wait_ge(ns_stored[b], 16 * (i + 1))
                nc.scalar.copy(ns_sb[b][:, :], ns_ps[b][:, :]).then_inc(products_out, 1)
                act.wait_ge(products_out, 2 * (c + 1) + 4)
                act.dma_start(dram["ns_t"][:, bass.ds(c * CW, CW)], ns_sb[b][:, :]).then_inc(ns_stored[b], 16)

            def store_e(c, b):
                act.wait_ge(e_out, c + 3)
                act.dma_start(dram["e"][:, bass.ds(c * CW, CW)], e_sb[b][:, :]).then_inc(e_stored[b], 16)

            for g in range(NPIECE):
                split(0, 0, g)
            with act.Fori(0, NCHUNK // 2 - 1) as i:
                for s in range(2):
                    c, b = 2 * i + 1 + s, 1 - s
                    split(c, b, 0)
                    take_out(c - 1, s, i)
                    for g in range(1, NPIECE):
                        split(c, b, g)
                    store_e(c - 1, s)
            split(NCHUNK - 1, 1, 0)
            take_out(NCHUNK - 2, 0, NCHUNK // 2 - 1)
            for g in range(1, NPIECE):
                split(NCHUNK - 1, 1, g)
            store_e(NCHUNK - 2, 0)
            take_out(NCHUNK - 1, 1, NCHUNK // 2 - 1)
            store_e(NCHUNK - 1, 1)
            for b in range(2):
                act.wait_ge(ns_stored[b], 16 * (NCHUNK // 2 + 1))
                act.wait_ge(e_stored[b], 16 * (NCHUNK // 2 + 1))

        @block.vector
        def _(dve):
            def make(c, b, g):
                n = NPIECE * c + g
                dve.wait_ge(cleared, CHUNK * (n + 1))
                dve.wait_ge(piece_done, n + 3)
                nc.vector.tensor_scalar(pos[g % 2][:, :, :], pieces[:, g % RING, :, :], 0.0, None, ALU.is_gt).then_inc(made, 1)
                dve.wait_ge(rounded, n + 1)
                dve.wait_ge(signed, n + 2)
                nc.vector.tensor_tensor(a_lo[g % 2][:, :, :], pieces[:, g % RING, :, :], a_hi[g % HIS][:, :, :].bitcast(F32),
                                        ALU.subtract).then_inc(made, 1)

            def count_rows(c, b):
                dve.wait_ge(products_out, 2 * (c + 1) + 3)
                nc.vector.tensor_reduce(max_counts[:, bass.ds(c, 1)], prod_sb[b][0:1, :], AX_X, ALU.max).then_inc(counted, 1)

            def make_e(c, b, i):
                dve.wait_ge(e_sum, c + 3)
                nc.vector.tensor_scalar(e_scl[:, :], e_ps[0:HEADS, :], ALPHA, None, ALU.mult).then_inc(e_step, 1)
                dve.wait_ge(e_step, c + 1)
                dve.wait_ge(e_stored[b], 16 * (i + 1))
                nc.vector.tensor_tensor(e_sb[b][:, :], e_ps[0:HEADS, :], e_scl[:, :], ALU.max).then_inc(e_out, 1)

            dve.sem_inc(e_out, 2)
            for b in range(2):
                nc.vector.memset(prod_sb[b][:, :], 0.0).then_inc(counted, 1)
            for g in range(NPIECE):
                make(0, 0, g)
            with dve.Fori(0, NCHUNK // 2 - 1) as i:
                for s in range(2):
                    c, b = 2 * i + 1 + s, 1 - s
                    for g in range(NPIECE):
                        make(c, b, g)
                        if g == 2:
                            count_rows(c - 1, s)
                        if g == 3:
                            make_e(c - 1, s, i)
            for g in range(NPIECE):
                make(NCHUNK - 1, 1, g)
            count_rows(NCHUNK - 2, 0)
            make_e(NCHUNK - 2, 0, NCHUNK // 2 - 1)
            dve.wait_ge(signed, NCHUNK * NPIECE + 2)
            nc.vector.tensor_reduce(sign_sum[:, :], sign_sums[:, :], AX_X, ALU.add).then_inc(signs_added, 1)
            count_rows(NCHUNK - 1, 1)
            dve.wait_ge(counted, NCHUNK + 2)
            nc.vector.tensor_reduce(max_count[:, :], max_counts[:, :], AX_X, ALU.max).then_inc(flag_step, 1)
            nc.vector.tensor_reduce(count[:, :], counts[0:1, :], AX_X, ALU.add).then_inc(flag_step, 1)
            dve.wait_ge(signs_total, 1)
            dve.wait_ge(flag_step, 2)
            nc.vector.tensor_tensor(negatives[:, :], count[:, :], total_ps[0:1, 0:1], ALU.subtract).then_inc(flag_step, 1)
            dve.wait_ge(flag_step, 3)
            nc.vector.tensor_scalar(keep["flags"][0:1, 0:1], negatives[:, :], 0.0, None, ALU.is_gt)
            nc.vector.tensor_scalar(keep["flags"][0:1, 1:2], max_count[:, :], float(TOPK), None, ALU.is_ge)
            make_e(NCHUNK - 1, 1, NCHUNK // 2 - 1)

        @block.tensor
        def _(pe):
            def wide(ps, rows=P):
                return ps[0:rows, :].rearrange("p (r n) -> p r n", n=P)

            def products(c, b, g):
                if g == 0:
                    pe.wait_ge(products_out, 2 * (c + 1))
                pe.wait_ge(made, 2 * (NPIECE * c + g + 1))
                for j in range(PIECE):
                    k = g * PIECE + j
                    cols = slice(j * P, (j + 1) * P)
                    first, last = k == 0, k == NB - 1
                    hi, lo = a_hi[g % HIS][:, :, cols], a_lo[g % 2][:, :, cols]
                    nc.tensor.matmul(wide(pos_ps[b], NST), uv_parts[:, k, :], pos[g % 2][:, :, cols], start=first, stop=last)
                    nc.tensor.matmul(wide(ns_ps[b]), x_hi[:, k, :], hi, start=first, stop=False)
                    nc.tensor.matmul(wide(ns_ps[b]), x_hi[:, k, :], lo, start=False, stop=False)
                    mm = nc.tensor.matmul(wide(ns_ps[b]), x_lo[:, k, :], hi, start=False, stop=last)
                mm.then_inc(piece_done, 1)

            def sum_e(c, b):
                pe.wait_ge(products_out, 2 * (c + 1) + 3)
                pe.wait_ge(e_out, c + 2)
                nc.tensor.matmul(e_ps[0:HEADS, :], sel[:, 0, 0:HEADS], prod_sb[b][:, :], start=True, stop=True
                                 ).then_inc(e_sum, 1)

            pe.sem_inc(piece_done, HIS)
            pe.sem_inc(e_sum, 2)
            for g in range(NPIECE):
                products(0, 0, g)
            with pe.Fori(0, NCHUNK // 2 - 1) as i:
                for s in range(2):
                    c, b = 2 * i + 1 + s, 1 - s
                    for g in range(NPIECE):
                        products(c, b, g)
                        if g == 2:
                            sum_e(c - 1, s)
            for g in range(NPIECE):
                products(NCHUNK - 1, 1, g)
                if g == 2:
                    sum_e(NCHUNK - 2, 0)
            pe.wait_ge(signs_added, 1)
            nc.tensor.matmul(total_ps[0:1, 0:1], sign_sum[:, :], keep["ones"][:, :], start=True, stop=True
                             ).then_inc(signs_total, 1)
            sum_e(NCHUNK - 1, 1)


def signed_scores_phase(nc, sem, dram, keep):
    loaded = [sem("m_loaded0"), sem("m_loaded1")]
    cleared, masked, mask_free = sem("m_cleared"), sem("m_masked"), sem("m_mask_free")
    products_out = sem("m_products_out")
    e_sum, e_step, e_out = sem("m_e_sum"), sem("m_e_step"), sem("m_e_out")
    e_stored = [sem("m_e_stored0"), sem("m_e_stored1")]
    with ExitStack() as ctx:
        m = Mem(nc, ctx)
        a_t = [m.sb(f"m_a_t{b}", [P, CHUNK, N]) for b in range(2)]
        pos = [m.sb(f"m_pos{b}", [P, CHUNK, GRP * P], BF16) for b in range(2)]
        neg = [m.sb(f"m_neg{b}", [P, CHUNK, GRP * P], BF16) for b in range(2)]
        prod_sb = [m.sb(f"m_prod_sb{b}", [P, 2, CW]) for b in range(2)]
        e_scl = m.sb("m_e_scl", [NUV, CW])
        e_sb = [m.sb(f"m_e_sb{b}", [NUV, CW]) for b in range(2)]
        pos_ps = [m.ps(f"m_pos_ps{b}", [P, CW]) for b in range(2)]
        neg_ps = [m.ps(f"m_neg_ps{b}", [P, CW]) for b in range(2)]
        e_ps = m.ps("m_e_ps", [P, CW])
        uv_parts, off_diag, sel = (keep[k] for k in ("uv_parts", "off_diag", "sel"))
        block = ctx.enter_context(nc.Block())

        @block.sync
        def _(sp):
            def load(b, c):
                for r in range(CHUNK):
                    sp.dma_start(a_t[b][:, r, :],
                                 dram["adj_t"][bass.ds(c * CHUNK + r, 1), :, :].rearrange("a p n -> p (a n)")
                                 ).then_inc(loaded[b], 16)

            for b in range(2):
                load(b, b)
            with sp.Fori(0, NCHUNK // 2 - 1) as i:
                for b in range(2):
                    sp.wait_ge(mask_free, NGRP * (2 * i + b + 1) + 2)
                    load(b, 2 * i + b + 2)

        @block.gpsimd
        def _(pool):
            with pool.Fori(0, NCHUNK // 2) as i:
                for b in range(2):
                    pool.wait_ge(loaded[b], 16 * CHUNK * (i + 1))
                    for r in range(CHUNK):
                        diag = a_t[b][:, r, bass.ds(((2 * i + b) * CHUNK + r) * P, P)]
                        nc.gpsimd.tensor_tensor(diag, diag, off_diag[:, :], ALU.mult).then_inc(cleared, 1)

        @block.vector
        def _(dve):
            for b in range(2):
                nc.vector.memset(prod_sb[b][:, :, :], 0.0).then_inc(e_out, 1)
            with dve.Fori(0, NCHUNK // 2) as i:
                for b in range(2):
                    c = 2 * i + b
                    dve.wait_ge(cleared, CHUNK * (c + 1))
                    for g in range(NGRP):
                        src = a_t[b][:, :, g * GRP * P:(g + 1) * GRP * P]
                        dve.wait_ge(mask_free, NGRP * c + g + 1)
                        nc.vector.tensor_scalar(pos[g % 2][:, :, :], src, 0.0, None, ALU.is_gt)
                        nc.vector.tensor_scalar(neg[g % 2][:, :, :], src, 0.0, None, ALU.is_lt).then_inc(masked, 1)
                    dve.wait_ge(e_sum, c + 1)
                    nc.vector.tensor_scalar(e_scl[:, :], e_ps[0:NUV, :], ALPHA, None, ALU.mult).then_inc(e_step, 1)
                    dve.wait_ge(e_step, c + 1)
                    dve.wait_ge(e_stored[b], 16 * (i + 1))
                    nc.vector.tensor_tensor(e_sb[b][:, :], e_ps[0:NUV, :], e_scl[:, :], ALU.max).then_inc(e_out, 1)

        @block.tensor
        def _(pe):
            pe.sem_inc(mask_free, 2)
            with pe.Fori(0, NCHUNK // 2) as i:
                for b in range(2):
                    c = 2 * i + b
                    pe.wait_ge(products_out, 2 * (c + 1))
                    for g in range(NGRP):
                        pe.wait_ge(masked, NGRP * c + g + 1)
                        for j in range(GRP):
                            k = g * GRP + j
                            cols = slice(j * P, (j + 1) * P)
                            first, last = k == 0, k == NB - 1
                            nc.tensor.matmul(pos_ps[b][0:NST, :].rearrange("p (r n) -> p r n", n=P), uv_parts[:, k, :],
                                             pos[g % 2][:, :, cols], start=first, stop=last)
                            mm = nc.tensor.matmul(neg_ps[b][0:NST, :].rearrange("p (r n) -> p r n", n=P), uv_parts[:, k, :],
                                                  neg[g % 2][:, :, cols], start=first, stop=last)
                        mm.then_inc(mask_free, 1)
                    pe.wait_ge(products_out, 2 * (c + 1) + 4)
                    pe.wait_ge(e_out, c + 2)
                    nc.tensor.matmul(e_ps[0:NUV, :], sel[:, 0, :], prod_sb[b][:, 0, :], start=True, stop=False)
                    nc.tensor.matmul(e_ps[0:NUV, :], sel[:, 1, :], prod_sb[b][:, 1, :], start=False, stop=True
                                     ).then_inc(e_sum, 1)

        @block.scalar
        def _(act):
            act.sem_inc(products_out, 4)
            for b in range(2):
                act.sem_inc(e_stored[b], 16)
            with act.Fori(0, NCHUNK // 2) as i:
                for b in range(2):
                    c = 2 * i + b
                    act.wait_ge(mask_free, NGRP * (c + 1) + 2)
                    act.wait_ge(e_out, c + 1)
                    nc.scalar.copy(prod_sb[b][0:NST, 0, :], pos_ps[b][0:NST, :]).then_inc(products_out, 1)
                    nc.scalar.copy(prod_sb[b][0:NST, 1, :], neg_ps[b][0:NST, :]).then_inc(products_out, 1)
                    act.wait_ge(e_out, c + 3)
                    act.dma_start(dram["e_signed"][:, bass.ds(c * CW, CW)], e_sb[b][:, :]).then_inc(e_stored[b], 16)
            for b in range(2):
                act.wait_ge(e_stored[b], 16 * (NCHUNK // 2 + 1))


QUARTER = N // 4
UNIT = 2
NUNIT = NB // UNIT
SLOTS = 3


def slot_of(u, b):
    return (u + b) % SLOTS


def units_since(u, b, parities):
    if u >= SLOTS:
        return SLOTS
    before = (b - 1) % parities
    return u + NUNIT - max(v for v in range(NUNIT) if slot_of(v, before) == slot_of(u, b))


def attention_phase(nc, sem, dram, keep, signed):
    tag = "s" if signed else "b"
    e_dram = dram["e_signed" if signed else "e"]
    sets = 1 if signed else 2
    ahead = 1 + max(units_since(u, b, sets) for u in range(SLOTS) for b in range(sets))
    e_loaded = sem(tag + "_e_loaded")
    row_loaded = [sem(f"{tag}_row_loaded{s}") for s in range(2)]
    sign_done, bias_made, bias_ready = sem(tag + "_sign_done"), sem(tag + "_bias_made"), sem(tag + "_bias_ready")
    logits_done, max_negated, exps_done = sem(tag + "_logits_done"), sem(tag + "_max_negated"), sem(tag + "_exps_done")
    cols_loaded = [sem(f"{tag}_cols_loaded{s}") for s in range(2)]
    transposed, scaled, multiplied = sem(tag + "_transposed"), sem(tag + "_scaled"), sem(tag + "_multiplied")
    y_out = sem(tag + "_y_out")
    y_stored = [sem(f"{tag}_y_stored{s}") for s in range(2)]
    e_neg_loaded, e_neg_used, neg_step = (sem(f"{tag}_{n}") for n in ("e_neg_loaded", "e_neg_used", "neg_step")) if signed else (None,) * 3
    with ExitStack() as ctx:
        m = Mem(nc, ctx)
        e_pos = m.sb(tag + "e_pos", [P, HEADS, N])
        q = [m.sb(f"{tag}q{b}", [P, HEADS, N]) for b in range(sets)]
        bias = [m.sb(f"{tag}bias{b}", [P, N], BF16) for b in range(sets)]
        if signed:
            bias_neg = m.sb(tag + "bias_neg", [P, N], BF16)
            e_neg = m.sb(tag + "e_neg", [P, N])
            logits_neg = m.sb(tag + "logits_neg", [P, N])
        row = [m.sb(f"{tag}row{s}", [P, QUARTER]) for s in range(2)]
        cols = [m.sb(f"{tag}cols{s}", [P, QUARTER]) for s in range(2)]
        s_t = [m.sb(f"{tag}s_t{s}", [P, UNIT, HEADS * P]) for s in range(SLOTS)]
        row_max = m.sb(tag + "row_max", [P, 2, HEADS])
        neg_max = m.sb(tag + "neg_max", [P, 2, HEADS])
        y_sb = [m.sb(f"{tag}y_sb{s}", [P, HEADS * P]) for s in range(2)]
        pause = m.sb(tag + "pause", [P, 1])
        q_t = [m.ps(f"{tag}q_t{s}", [P, UNIT, 512]) for s in range(SLOTS)]
        y_ps = [m.ps(f"{tag}y_ps{b}", [P, 512]) for b in range(2)]
        x_sb, ident, diag_bias, den = keep["x_sb"], keep["ident"], keep["diag_bias"], keep["den"]
        block = ctx.enter_context(nc.Block())

        @block.sync
        def _(sp):
            for h in range(HEADS):
                sp.dma_start(e_pos[:, h, :], e_dram[h, :].partition_broadcast(P)).then_inc(e_loaded, 16)

            def load_cols(t):
                for k in range(4):
                    sp.wait_ge(scaled, NUNIT // 4 * (4 * t + k - 1) + ahead)
                    sp.dma_start(cols[k % 2][:, :], dram["adj_t"][bass.ds(t, 1), :, k * QUARTER:(k + 1) * QUARTER]
                                 .rearrange("a p n -> p (a n)")).then_inc(cols_loaded[k % 2], 16)

            with sp.Fori(0, NB) as t:
                if signed:
                    for h in range(HEADS):
                        sp.wait_ge(e_neg_used, HEADS * t + h + 1)
                        sp.dma_start(e_neg[:, :], e_dram[HEADS + h, :].partition_broadcast(P)).then_inc(e_neg_loaded, 16)
                load_cols(t)

        @block.gpsimd
        def _(pool):
            per_tile = 8 if signed else 4
            with pool.Fori(0, NB // sets) as i:
                for b in range(sets):
                    t = sets * i + b
                    pool.wait_ge(bias_made, per_tile * (t + 1))
                    for buf in [bias[b]] + ([bias_neg] if signed else []):
                        diag = buf[:, bass.ds(t * P, P)]
                        nc.gpsimd.tensor_tensor(diag, diag, diag_bias[:, :], ALU.add).then_inc(bias_ready, 1)

        @block.scalar
        def _(act):
            def load_row(t, k):
                act.dma_start(row[k % 2][:, :], dram["adj"][bass.ds(t * P, P), k * QUARTER:(k + 1) * QUARTER]
                              ).then_inc(row_loaded[k % 2], 16)

            def make_bias(t, b, more=True):
                for k in range(4):
                    piece = slice(k * QUARTER, (k + 1) * QUARTER)
                    act.wait_ge(row_loaded[k % 2], 16 * (2 * t + k // 2 + 1))
                    if k == 0:
                        act.wait_ge(logits_done, HEADS * (t + 1))
                    sign = (bias_neg if signed else bias[b])[:, piece]
                    nc.scalar.activation(sign, row[k % 2][:, :], ACT.Sign).then_inc(sign_done, 1)
                    act.wait_ge(sign_done, 4 * t + k + 1)
                    if k < 2:
                        load_row(t, k + 2)
                    elif more:
                        load_row(t + 1, k - 2)
                    if signed:
                        nc.scalar.activation(bias[b][:, piece], sign, ACT.Copy, bias=NEG_INF, scale=-NEG_INF).then_inc(bias_made, 1)
                        act.wait_ge(bias_made, 8 * t + 2 * k + 1)
                        nc.scalar.activation(sign, sign, ACT.Copy, bias=NEG_INF, scale=NEG_INF).then_inc(bias_made, 1)
                    else:
                        nc.scalar.activation(sign, sign, ACT.Copy, bias=NEG_INF, scale=-NEG_INF).then_inc(bias_made, 1)

            def make_exps(t, b):
                for h in range(HEADS):
                    act.wait_ge(logits_done, HEADS * (t + sets) + h + 1)
                    nc.scalar.mul(neg_max[:, b, h:h + 1], row_max[:, b, h:h + 1], -1.0).then_inc(max_negated, 1)
                    act.wait_ge(max_negated, HEADS * t + h + 1)
                    nc.scalar.activation(q[b][:, h, :], q[b][:, h, :], ACT.Exp, bias=neg_max[:, b, h:h + 1],
                                         accum_out=den[:, bass.ds(t, 1), h]).then_inc(exps_done, 1)

            def store_y(t, s, i):
                act.wait_ge(multiplied, NUNIT * (t + 1) + ahead)
                act.wait_ge(y_stored[s], 16 * (i + 1))
                nc.scalar.copy(y_sb[s][:, :], y_ps[s][:, 0:HEADS * P]).then_inc(y_out, 1)
                act.wait_ge(y_out, t + 3)
                act.dma_start(dram["y_t"][bass.ds(t, 1), :, :].rearrange("a p n -> p (a n)"), y_sb[s][:, :]
                              ).then_inc(y_stored[s], 16)

            act.sem_inc(y_out, 2)
            for s in range(2):
                act.sem_inc(y_stored[s], 16)
                load_row(0, s)
            if signed:
                make_bias(0, 0)
                make_exps(0, 0)
                with act.Fori(0, NB // 2 - 1) as i:
                    for s in range(2):
                        make_bias(2 * i + s + 1, 0)
                        make_exps(2 * i + s + 1, 0)
                        store_y(2 * i + s, s, i)
                make_bias(NB - 1, 0, more=False)
                make_exps(NB - 1, 0)
                store_y(NB - 2, 0, NB // 2 - 1)
                store_y(NB - 1, 1, NB // 2 - 1)
            else:
                make_bias(0, 0)
                make_bias(1, 1)
                make_exps(0, 0)
                make_bias(2, 0)
                with act.Fori(0, NB // 2 - 2) as i:
                    for s in range(2):
                        make_exps(2 * i + s + 1, 1 - s)
                        store_y(2 * i + s, s, i)
                        make_bias(2 * i + s + 3, 1 - s)
                for t in range(NB - 4, NB):
                    if t + 1 < NB:
                        make_exps(t + 1, 1 - t % 2)
                    store_y(t, t % 2, t // 2)
                    if t + 3 < NB:
                        make_bias(t + 3, 1 - t % 2, more=False)
            for s in range(2):
                act.wait_ge(y_stored[s], 16 * (NB // 2 + 1))

        @block.vector
        def _(dve):
            def logits(t, b, h):
                if h == 0:
                    dve.wait_ge(bias_ready, (2 if signed else 1) * (t + 1))
                    dve.wait_ge(transposed, NUNIT * (t + 1))
                    nc.vector.memset(pause[:, :], 0.0)
                ttr = nc.vector.tensor_tensor_reduce(q[b][:, h, :], bias[b][:, :], e_pos[:, h, :], 1.0, LOWEST,
                                                     ALU.add, ALU.max, row_max[:, b, h:h + 1])
                if not signed:
                    ttr.then_inc(logits_done, 1)
                    return
                ttr.then_inc(neg_step, 1)
                n = 3 * (HEADS * t + h)
                dve.wait_ge(e_neg_loaded, 16 * (HEADS * t + h + 1))
                nc.vector.tensor_tensor(logits_neg[:, :], bias_neg[:, :], e_neg[:, :], ALU.add).then_inc(neg_step, 1)
                dve.wait_ge(neg_step, n + 2)
                dve.sem_inc(e_neg_used, 1)
                nc.vector.tensor_tensor(q[b][:, h, :], q[b][:, h, :], logits_neg[:, :], ALU.max).then_inc(neg_step, 1)
                dve.wait_ge(neg_step, n + 3)
                nc.vector.tensor_reduce(row_max[:, b, h:h + 1], q[b][:, h, :], AX_X, ALU.max).then_inc(logits_done, 1)

            def scale_units(t, b, between):
                for u in range(NUNIT):
                    s, per = slot_of(u, b), NUNIT // 4
                    n = NUNIT * t + u
                    if u % per == 0:
                        k = u // per
                        dve.wait_ge(cols_loaded[k % 2], 16 * (2 * t + k // 2 + 1))
                    dve.wait_ge(transposed, n + 1 + NUNIT * sets)
                    dve.wait_ge(multiplied, n - units_since(u, b, sets) + 1 + ahead)
                    a = cols[u // per % 2][:, (u % per) * UNIT * P:(u % per + 1) * UNIT * P]
                    a = a.rearrange("p (k r) -> p k r", r=P).unsqueeze(2).broadcast_to([P, UNIT, HEADS, P])
                    nc.vector.tensor_tensor(s_t[s][:, :, :].rearrange("p k (h r) -> p k h r", r=P),
                                            q_t[s][:, :, 0:HEADS * P].rearrange("p k (h r) -> p k h r", r=P),
                                            a, ALU.mult).then_inc(scaled, 1)
                    if u in between:
                        between[u]()

            dve.sem_inc(logits_done, HEADS * sets)
            dve.sem_inc(scaled, ahead)
            if signed:
                dve.sem_inc(e_neg_used, 1)
            dve.wait_ge(e_loaded, 16 * HEADS)
            if signed:
                with dve.Fori(0, NB) as t:
                    for h in range(HEADS):
                        logits(t, 0, h)
                    scale_units(t, 0, {})
            else:
                def with_next(t, b):
                    scale_units(t, b, {u: (lambda h=h: logits(t + 1, 1 - b, h)) for h, u in enumerate((0, 4, 9))})

                for h in range(HEADS):
                    logits(0, 0, h)
                with dve.Fori(0, NB // 2 - 1) as i:
                    for b in range(2):
                        with_next(2 * i + b, b)
                with_next(NB - 2, 0)
                scale_units(NB - 1, 1, {})

        @block.tensor
        def _(pe):
            def transposes(t, b, u):
                s = slot_of(u, b)
                if u == 0:
                    pe.wait_ge(exps_done, HEADS * (t + 1))
                pe.wait_ge(scaled, NUNIT * t + u - units_since(u, b, sets) + 1 + ahead)
                for j in range(UNIT):
                    k = UNIT * u + j
                    for h in range(HEADS):
                        mm = nc.tensor.transpose(q_t[s][:, j, h * P:(h + 1) * P], q[b][:, h, k * P:(k + 1) * P], ident[:, :])
                mm.then_inc(transposed, 1)

            def products(t, b, y, u):
                s = slot_of(u, b)
                pe.wait_ge(scaled, NUNIT * t + u + 1 + ahead)
                for j in range(UNIT):
                    k = UNIT * u + j
                    mm = nc.tensor.matmul(y_ps[y][:, 0:HEADS * P], x_sb[:, k, :], s_t[s][:, j, :],
                                          start=k == 0, stop=k == NB - 1)
                mm.then_inc(multiplied, 1)

            def tile(t, b, y, more=True):
                for u in range(NUNIT):
                    if u < NUNIT - 2:
                        transposes(t, b, u + 2)
                    elif more:
                        transposes(t + 1, (b + 1) % sets, u + 2 - NUNIT)
                    if u == 0:
                        pe.wait_ge(y_out, t + 1)
                    products(t, b, y, u)

            pe.sem_inc(transposed, NUNIT * sets)
            pe.sem_inc(multiplied, ahead)
            transposes(0, 0, 0)
            transposes(0, 0, 1)
            with pe.Fori(0, NB // 2 - 1) as i:
                for y in range(2):
                    tile(2 * i + y, y % sets, y)
            tile(NB - 2, 0, 0)
            tile(NB - 1, 1 % sets, 1, more=False)


def gate_phase(nc, sem, dram, keep):
    w_loaded, bias_step, parts_placed, recip = sem("g_w_loaded"), sem("g_bias_step"), sem("g_parts_placed"), sem("g_recip")
    loaded = [sem("g_loaded0"), sem("g_loaded1")]
    started, es_step, es_transposed, es_copied, node_done = (
        sem("g_" + n) for n in ("started", "es_step", "es_transposed", "es_copied", "node_done"))
    edge_rz, edge_n, node_rz, node_n = (sem("g_" + n) for n in ("edge_rz", "edge_n", "node_rz", "node_n"))
    edge_pre, node_pre, edge_out, node_out, y_step = (
        sem("g_" + n) for n in ("edge_pre", "node_pre", "edge_out", "node_out", "y_step"))
    with ExitStack() as ctx:
        m = Mem(nc, ctx)
        kinds = ("edge", "node")
        gat_w = m.sb("gat_w", [P, HEADS, H])
        wih = {k: m.sb(k + "_wih", [P, 3 * H]) for k in kinds}
        whh = {k: m.sb(k + "_whh", [P, 3 * H]) for k in kinds}
        b_in = {k: m.sb(k + "_b_in", [1, 4 * H]) for k in kinds}
        b_hid = {k: m.sb(k + "_b_hid", [1, 2 * H]) for k in kinds}
        b_parts = {k: m.sb(k + "_b_parts", [1, NPART, 4 * H], BF16) for k in kinds}
        b_rows = {k: m.sb(k + "_b_rows", [NPART, 4 * H], BF16) for k in kinds}
        ones = m.sb("g_ones", [NPART, P], BF16)
        diag = m.sb("g_diag", [P, NB])
        r_den = m.sb("r_den", [P, NB, HEADS])

        def pair(name, shape, make=m.sb):
            return [make(f"{name}{b}", shape) for b in range(2)]

        x_t, ns_t, y_t = pair("g_x_t", [P, P]), pair("g_ns_t", [P, P]), pair("g_y_t", [P, HEADS * P])
        es, es_t = pair("g_es", [P, H]), pair("g_es_t", [P, P])
        rz = {k: pair(k + "_rz", [P, 2 * H]) for k in kinds}
        pre = {k: pair(k + "_pre", [P, H]) for k in kinds}
        n_gate = {k: pair(k + "_n", [P, H]) for k in kinds}
        cell = {k: pair(k + "_cell", [P, H]) for k in kinds}
        z_ps, es_ps = pair("g_z_ps", [P, 512], m.ps), pair("g_es_ps", [P, 512], m.ps)
        gates = {k: pair(k + "_gates", [P, 512], m.ps) for k in kinds}
        x_sb, ident, den, y_all = keep["x_sb"], keep["ident"], keep["den"], keep["y_all"]
        block = ctx.enter_context(nc.Block())

        @block.sync
        def _(sp):
            sp.dma_start(gat_w[:, :, :], dram["gat_W"]).then_inc(w_loaded, 16)
            for k in kinds:
                sp.dma_start(wih[k][:, :], dram[k + "_Wih_t"]).then_inc(w_loaded, 16)
                sp.dma_start(whh[k][:, :], dram[k + "_Whh_t"]).then_inc(w_loaded, 16)
                sp.dma_start(b_in[k][:, 0:3 * H], dram[k + "_bih"].unsqueeze(0)).then_inc(w_loaded, 16)
                sp.dma_start(b_in[k][:, 3 * H:4 * H], dram[k + "_bhh"][2 * H:3 * H].unsqueeze(0)).then_inc(w_loaded, 16)
                sp.dma_start(b_hid[k][:, :], dram[k + "_bhh"][0:2 * H].unsqueeze(0)).then_inc(w_loaded, 16)
            with nc.allow_non_contiguous_dma(reason="the diagonal"):
                sp.dma_start(diag[:, :], dram["adj"].rearrange("a b -> (a b)")[0:N * N:N + 1].rearrange("(t p) -> p t", p=P)
                             ).then_inc(w_loaded, 16)

            def load(t, b):
                sp.wait_ge(started, t + 1)
                sp.dma_start(x_t[b][:, :], dram["x_t"][:, bass.ds(t * P, P)]).then_inc(loaded[b], 16)
                sp.dma_start(ns_t[b][:, :], dram["ns_t"][:, bass.ds(t * P, P)]).then_inc(loaded[b], 16)
                sp.dma_start(y_t[b][:, :], dram["y_t"][bass.ds(t, 1), :, :].rearrange("a p n -> p (a n)")
                             ).then_inc(loaded[b], 16)

            load(0, 0)
            load(1, 1)
            for k in kinds:
                sp.wait_ge(bias_step, 13)
                for j in range(NPART):
                    sp.dma_start(b_rows[k][j:j + 1, :], b_parts[k][:, j, :]).then_inc(parts_placed, 16)
            with sp.Fori(1, NB // 2) as i:
                for b in range(2):
                    load(2 * i + b, b)

        @block.tensor
        def _(pe):
            def start(t, b, half):
                pe.wait_ge(loaded[b], 3 * 16 * (half + 1))
                pe.wait_ge(node_pre, 2 * (t + 1))
                for h in range(HEADS):
                    nc.tensor.matmul(z_ps[b][:, h * H:(h + 1) * H], y_t[b][:, h * P:(h + 1) * P], gat_w[:, h, :],
                                     start=True, stop=True)
                for k in kinds:
                    g = gates[k][b]
                    nc.tensor.matmul(g[:, :], ones[:, :], b_rows[k][:, :], start=True, stop=False)
                    nc.tensor.matmul(g[:, 0:2 * H], x_t[b][:, :], whh[k][:, 0:2 * H], start=False, stop=False)
                    mm = nc.tensor.matmul(g[:, 3 * H:4 * H], x_t[b][:, :], whh[k][:, 2 * H:3 * H], start=False, stop=False)
                    if k == "edge":
                        mm = nc.tensor.matmul(g[:, 0:3 * H], ns_t[b][:, :], wih[k][:, :], start=False, stop=True)
                mm.then_inc(started, 1)

            def transpose_es(t, b):
                pe.wait_ge(es_step, HEADS * (t + 1))
                nc.tensor.transpose(es_ps[b][:, 0:P], es[b][:, :], ident[:, :]).then_inc(es_transposed, 1)

            def finish_node(t, b):
                pe.wait_ge(es_copied, t + 1)
                nc.tensor.matmul(gates["node"][b][:, 0:3 * H], es_t[b][:, :], wih["node"][:, :], start=False, stop=True
                                 ).then_inc(node_done, 1)

            pe.sem_inc(started, 2)
            pe.wait_ge(w_loaded, 16 * 12)
            pe.wait_ge(parts_placed, 16 * 2 * NPART)
            start(0, 0, 0)
            with pe.Fori(0, NB // 2 - 1) as i:
                for b in range(2):
                    transpose_es(2 * i + b, b)
                    start(2 * i + b + 1, 1 - b, i + b)
                    finish_node(2 * i + b, b)
            transpose_es(NB - 2, 0)
            start(NB - 1, 1, NB // 2 - 1)
            finish_node(NB - 2, 0)
            transpose_es(NB - 1, 1)
            finish_node(NB - 1, 1)

        @block.scalar
        def _(act):
            def edge(t, b):
                act.wait_ge(started, t + 3)
                nc.scalar.activation(rz["edge"][b][:, :], gates["edge"][b][:, 0:2 * H], ACT.Tanh, scale=0.5).then_inc(edge_rz, 1)
                act.wait_ge(es_transposed, t + 1)
                nc.scalar.copy(es_t[b][:, :], es_ps[b][:, 0:P]).then_inc(es_copied, 1)
                act.wait_ge(edge_pre, 2 * (t + 1))
                nc.scalar.activation(n_gate["edge"][b][:, :], pre["edge"][b][:, :], ACT.Tanh).then_inc(edge_n, 1)

            def node_last(t, b):
                act.wait_ge(node_pre, 2 * (t + 1) + 4)
                nc.scalar.activation(n_gate["node"][b][:, :], pre["node"][b][:, :], ACT.Tanh).then_inc(node_n, 1)

            def node_first(t, b):
                act.wait_ge(node_done, t + 1)
                nc.scalar.activation(rz["node"][b][:, :], gates["node"][b][:, 0:2 * H], ACT.Tanh, scale=0.5).then_inc(node_rz, 1)

            edge(0, 0)
            node_first(0, 0)
            with act.Fori(0, NB // 2 - 1) as i:
                for s in range(2):
                    t, b = 2 * i + 1 + s, 1 - s
                    edge(t, b)
                    node_last(t - 1, 1 - b)
                    node_first(t, b)
            edge(NB - 1, 1)
            node_last(NB - 2, 0)
            node_first(NB - 1, 1)
            node_last(NB - 1, 1)

        @block.vector
        def _(dve):
            def pre_n(k, t, b, done, rz_ready, extra):
                g = gates[k][b]
                dve.wait_ge(rz_ready, t + 1)
                nc.vector.scalar_tensor_tensor(pre[k][b][:, :], rz[k][b][:, 0:H], 1.0, g[:, 3 * H:4 * H], ALU.add, ALU.mult
                                               ).then_inc(done, 1)
                dve.wait_ge(done, 2 * t + 1 + extra)
                nc.vector.scalar_tensor_tensor(pre[k][b][:, :], pre[k][b][:, :], 0.5, g[:, 2 * H:3 * H], ALU.mult, ALU.add
                                               ).then_inc(done, 1)

            def finish_cell(k, t, b, n_ready, done):
                dve.wait_ge(n_ready, t + 1)
                nc.vector.tensor_tensor(cell[k][b][:, :], x_sb[:, bass.ds(t, 1), :].rearrange("p a f -> p (a f)"),
                                        n_gate[k][b][:, :], ALU.subtract).then_inc(done, 1)
                dve.wait_ge(done, 3 * t + 1)
                nc.vector.scalar_tensor_tensor(cell[k][b][:, :], rz[k][b][:, H:2 * H], 1.0, cell[k][b][:, :], ALU.add, ALU.mult
                                               ).then_inc(done, 1)
                dve.wait_ge(done, 3 * t + 2)
                nc.vector.scalar_tensor_tensor(cell[k][b][:, :], cell[k][b][:, :], 0.5, n_gate[k][b][:, :], ALU.mult, ALU.add
                                               ).then_inc(done, 1)

            def support(t, b):
                dve.wait_ge(started, t + 3)
                for h in range(HEADS):
                    z, r = z_ps[b][:, h * H:(h + 1) * H], r_den[:, bass.ds(t, 1), h]
                    if h == 0:
                        nc.vector.tensor_scalar(es[b][:, :], z, r, None, ALU.mult).then_inc(es_step, 1)
                    else:
                        dve.wait_ge(es_step, HEADS * t + h)
                        nc.vector.scalar_tensor_tensor(es[b][:, :], z, r, es[b][:, :], ALU.mult, ALU.add).then_inc(es_step, 1)

            def finish_tile(t, b):
                dve.wait_ge(edge_out, 3 * (t + 1))
                dve.wait_ge(node_out, 3 * (t + 1))
                nc.vector.tensor_tensor(cell["edge"][b][:, :], cell["edge"][b][:, :], cell["node"][b][:, :], ALU.add
                                        ).then_inc(y_step, 1)
                dve.wait_ge(y_step, 2 * t + 1)
                one = bass.ds(t, 1)
                nc.vector.scalar_tensor_tensor(y_all[:, one, :].rearrange("p a f -> p (a f)"), cell["edge"][b][:, :],
                                               diag[:, one], x_sb[:, one, :].rearrange("p a f -> p (a f)"),
                                               ALU.mult, ALU.add).then_inc(y_step, 1)

            def stage(t, b, before, after):
                if after:
                    support(t, b)
                    pre_n("edge", t, b, edge_pre, edge_rz, 0)
                if before:
                    pre_n("node", t - 1, 1 - b, node_pre, node_rz, 4)
                if after:
                    finish_cell("edge", t, b, edge_n, edge_out)
                if before:
                    finish_cell("node", t - 1, 1 - b, node_n, node_out)
                    finish_tile(t - 1, 1 - b)

            nc.vector.memset(ones[:, :], 1.0).then_inc(bias_step, 1)
            dve.wait_ge(w_loaded, 16 * 12)
            n = 1
            for k in kinds:
                nc.vector.tensor_tensor(b_in[k][:, 0:2 * H], b_in[k][:, 0:2 * H], b_hid[k][:, :], ALU.add).then_inc(bias_step, 1)
                n += 1
                for j in range(NPART):
                    dve.wait_ge(bias_step, n)
                    nc.vector.tensor_copy(b_parts[k][:, j, :], b_in[k][:, :]).then_inc(bias_step, 1)
                    n += 1
                    if j < NPART - 1:
                        dve.wait_ge(bias_step, n)
                        nc.vector.tensor_tensor(b_in[k][:, :], b_in[k][:, :], b_parts[k][:, j, :], ALU.subtract).then_inc(bias_step, 1)
                        n += 1
            nc.vector.reciprocal(r_den[:, :, :], den[:, :, :]).then_inc(recip, 1)
            dve.wait_ge(recip, 1)
            nc.vector.tensor_scalar(r_den[:, :, :], r_den[:, :, :], 1.0 / HEADS, None, ALU.mult).then_inc(recip, 1)
            dve.wait_ge(recip, 2)
            dve.sem_inc(node_pre, 4)
            stage(0, 0, False, True)
            with dve.Fori(0, NB // 2 - 1) as i:
                for s in range(2):
                    stage(2 * i + 1 + s, 1 - s, True, True)
            stage(NB - 1, 1, True, True)
            stage(NB, 0, True, False)


LN_STEPS = 6


def layer_norm(nc, dve, step, squared, rooted, y, mean, var, root, square, rows):
    wide = [P, rows, H]
    nc.vector.tensor_reduce(mean[:, :], y, AX_X, ALU.add).then_inc(step, 1)
    dve.wait_ge(step, 1)
    nc.vector.tensor_scalar(mean[:, :], mean[:, :], 1.0 / H, None, ALU.mult).then_inc(step, 1)
    dve.wait_ge(step, 2)
    nc.vector.tensor_tensor(y, y, mean[:, :].unsqueeze(2).broadcast_to(wide), ALU.subtract).then_inc(step, 1)
    dve.wait_ge(squared, 1)
    nc.vector.tensor_reduce(var[:, :], square[:, :, :], AX_X, ALU.add).then_inc(step, 1)
    dve.wait_ge(step, 4)
    nc.vector.tensor_scalar(var[:, :], var[:, :], 1.0 / H, EPS, ALU.mult, ALU.add).then_inc(step, 1)
    dve.wait_ge(rooted, 1)
    nc.vector.reciprocal(root[:, :], root[:, :]).then_inc(rooted, 1)
    dve.wait_ge(rooted, 2)
    nc.vector.tensor_tensor(y, y, root[:, :].unsqueeze(2).broadcast_to(wide), ALU.mult).then_inc(step, 1)


def layer_norm_act(nc, act, step, squared, rooted, y, var, root, square):
    act.wait_ge(step, 3)
    nc.scalar.activation(square[:, :, :], y, ACT.Square).then_inc(squared, 1)
    act.wait_ge(step, 5)
    nc.scalar.activation(root[:, :], var[:, :], ACT.Sqrt).then_inc(rooted, 1)


def norm_phase(nc, sem, dram, keep):
    w_loaded, step, squared, rooted = sem("u_w_loaded"), sem("u_step"), sem("u_squared"), sem("u_rooted")
    x_turned, x_copied, projected, activated, multiplied, copied = (
        sem("u_" + n) for n in ("x_turned", "x_copied", "projected", "activated", "multiplied", "copied"))
    with ExitStack() as ctx:
        m = Mem(nc, ctx)
        w_proj, w_gcn, b_proj = m.sb("w_proj", [P, H]), m.sb("w_gcn", [P, H]), m.sb("b_proj", [P, 1])
        square = m.sb("u_square", [P, NB, H])
        mean, var, root = m.sb("u_mean", [P, NB]), m.sb("u_var", [P, NB]), m.sb("u_root", [P, NB])
        x1_t = [m.sb(f"x1_t{b}", [P, CW]) for b in range(2)]
        h2_t = [m.sb(f"h2_t{b}", [P, CW]) for b in range(2)]
        x1_ps = [m.ps(f"x1_ps{b}", [P, CW]) for b in range(2)]
        h2_ps = [m.ps(f"h2_ps{b}", [P, CW]) for b in range(2)]
        g_ps = [m.ps(f"g_ps{b}", [P, CW]) for b in range(2)]
        x1, g_all, ident = keep["y_all"], keep["g_all"], keep["ident"]
        block = ctx.enter_context(nc.Block())

        @block.sync
        def _(sp):
            sp.dma_start(w_proj[:, :], dram["W_proj"]).then_inc(w_loaded, 16)
            sp.dma_start(w_gcn[:, :], dram["W_gcn"]).then_inc(w_loaded, 16)
            sp.dma_start(b_proj[:, :], dram["b_proj"].unsqueeze(1)).then_inc(w_loaded, 16)

        @block.vector
        def _(dve):
            layer_norm(nc, dve, step, squared, rooted, x1[:, :, :], mean, var, root, square, NB)
            for c in range(NCHUNK):
                b = c % 2
                dve.wait_ge(x_turned, c + 1)
                nc.vector.tensor_copy(x1_t[b][:, :], x1_ps[b][:, :]).then_inc(x_copied, 1)
                if c >= 1:
                    dve.wait_ge(multiplied, c)
                    nc.vector.tensor_copy(g_all[:, (c - 1) * CHUNK:c * CHUNK, :].rearrange("p r f -> p (r f)"), g_ps[1 - b][:, :]
                                          ).then_inc(copied, 1)
            dve.wait_ge(multiplied, NCHUNK)
            nc.vector.tensor_copy(g_all[:, (NCHUNK - 1) * CHUNK:, :].rearrange("p r f -> p (r f)"), g_ps[(NCHUNK - 1) % 2][:, :]
                                  ).then_inc(copied, 1)

        @block.scalar
        def _(act):
            layer_norm_act(nc, act, step, squared, rooted, x1[:, :, :], var, root, square)
            act.wait_ge(w_loaded, 48)
            for c in range(NCHUNK):
                act.wait_ge(projected, c + 1)
                nc.scalar.activation(h2_t[c % 2][:, :], h2_ps[c % 2][:, :], ACT.Tanh, bias=b_proj[:, :]).then_inc(activated, 1)

        @block.tensor
        def _(pe):
            def turn(c):
                if c >= 2:
                    pe.wait_ge(x_copied, c - 1)
                for r in range(CHUNK):
                    mm = nc.tensor.transpose(x1_ps[c % 2][:, r * P:(r + 1) * P], x1[:, c * CHUNK + r, :], ident[:, :])
                mm.then_inc(x_turned, 1)

            def project(c):
                pe.wait_ge(x_copied, c + 1)
                nc.tensor.matmul(h2_ps[c % 2][:, :], w_proj[:, :], x1_t[c % 2][:, :], start=True, stop=True).then_inc(projected, 1)

            pe.wait_ge(w_loaded, 48)
            pe.wait_ge(step, LN_STEPS)
            turn(0)
            project(0)
            for c in range(NCHUNK):
                if c + 1 < NCHUNK:
                    turn(c + 1)
                    project(c + 1)
                pe.wait_ge(activated, c + 1)
                if c >= 2:
                    pe.wait_ge(copied, c - 1)
                for r in range(CHUNK):
                    mm = nc.tensor.matmul(g_ps[c % 2][:, r * P:(r + 1) * P], h2_t[c % 2][:, r * P:(r + 1) * P], w_gcn[:, :],
                                          start=True, stop=True)
                mm.then_inc(multiplied, 1)


def graph_phase(nc, sem, dram, keep, source):
    tag = {"adj_t": "f", "adj_top_t": "t"}[source]
    loaded = [sem(f"{tag}_loaded0"), sem(f"{tag}_loaded1")]
    b_loaded, squared_a, filtered, products = (sem(tag + n) for n in ("_b_loaded", "_squared_a", "_filtered", "_products"))
    relu_done, turned, y_done = (sem(tag + n) for n in ("_relu_done", "_turned", "_y_done"))
    step, squared, rooted, stored = (sem(tag + n) for n in ("_step", "_squared", "_rooted", "_stored"))
    with ExitStack() as ctx:
        m = Mem(nc, ctx)
        a_t = [m.sb(f"{tag}f_t{b}", [P, CHUNK, N]) for b in range(2)]
        b_gcn = m.sb(tag + "b_gcn", [P, 1])
        feat_t = [m.sb(f"{tag}feat_t{b}", [P, CW]) for b in range(2)]
        y2 = m.sb(tag + "y2", [P, NB, H])
        mean, var, root = (m.sb(tag + n, [P, NB]) for n in ("mean", "var", "root"))
        f_ps = [m.ps(f"{tag}f_ps{b}", [P, CW]) for b in range(2)]
        y_ps = [m.ps(f"{tag}yt_ps{b}", [P, CW]) for b in range(2)]
        x1, g_all, ident = keep["y_all"], keep["g_all"], keep["ident"]
        square = a_t[0][:, 0, :].rearrange("p (t f) -> p t f", f=H)
        block = ctx.enter_context(nc.Block())

        @block.sync
        def _(sp):
            def load(b, c):
                for r in range(CHUNK):
                    sp.dma_start(a_t[b][:, r, :], dram[source][bass.ds(c * CHUNK + r, 1), :, :].rearrange("a p n -> p (a n)")
                                 ).then_inc(loaded[b], 16)

            sp.dma_start(b_gcn[:, :], dram["b_gcn"].unsqueeze(1)).then_inc(b_loaded, 16)
            for b in range(2):
                load(b, b)
            with sp.Fori(0, NCHUNK // 2 - 1) as i:
                for b in range(2):
                    sp.wait_ge(products, 2 * i + b + 1)
                    load(b, 2 * i + b + 2)
            sp.wait_ge(step, LN_STEPS)
            sp.dma_start(dram["out"].rearrange("(t p) f -> p t f", p=P), y2[:, :, :]).then_inc(stored, 16)
            sp.wait_ge(stored, 16)

        @block.gpsimd
        def _(pool):
            pool.sem_inc(y_done, 2)

        def group(b, g):
            return a_t[b][:, :, g * GRP * P:(g + 1) * GRP * P]

        @block.vector
        def _(dve):
            def square_a(c, b, i):
                dve.wait_ge(loaded[b], 16 * CHUNK * (i + 1))
                for g in range(NGRP):
                    nc.vector.scalar_tensor_tensor(group(b, g), group(b, g), 0.0, group(b, g), ALU.max, ALU.mult
                                                   ).then_inc(squared_a, 1)

            def add_x1(c, b):
                dve.wait_ge(turned, c + 3)
                rows = bass.ds(c * CHUNK, CHUNK)
                nc.vector.tensor_tensor(y2[:, rows, :], y_ps[b][:, :].rearrange("p (r f) -> p r f", f=H), x1[:, rows, :],
                                        ALU.add).then_inc(y_done, 1)

            square_a(0, 0, 0)
            with dve.Fori(0, NCHUNK // 2 - 1) as i:
                square_a(2 * i + 1, 1, i)
                add_x1(2 * i, 0)
                square_a(2 * i + 2, 0, i + 1)
                add_x1(2 * i + 1, 1)
            square_a(NCHUNK - 1, 1, NCHUNK // 2 - 1)
            add_x1(NCHUNK - 2, 0)
            add_x1(NCHUNK - 1, 1)
            dve.wait_ge(y_done, NCHUNK + 2)
            layer_norm(nc, dve, step, squared, rooted, y2[:, :, :], mean, var, root, square, NB)

        @block.scalar
        def _(act):
            def tanh(c, b):
                for g in range(NGRP):
                    act.wait_ge(squared_a, NGRP * c + g + 1)
                    nc.scalar.activation(group(b, g), group(b, g), ACT.Tanh).then_inc(filtered, 1)

            def relu(c, b):
                act.wait_ge(products, c + 1)
                act.wait_ge(turned, c + 1)
                nc.scalar.activation(feat_t[b][:, :], f_ps[b][:, :], ACT.Relu, bias=b_gcn[:, :]).then_inc(relu_done, 1)

            tanh(0, 0)
            act.wait_ge(b_loaded, 16)
            with act.Fori(0, NCHUNK // 2 - 1) as i:
                for s in range(2):
                    tanh(2 * i + 1 + s, 1 - s)
                    relu(2 * i + s, s)
            tanh(NCHUNK - 1, 1)
            relu(NCHUNK - 2, 0)
            relu(NCHUNK - 1, 1)
            layer_norm_act(nc, act, step, squared, rooted, y2[:, :, :], var, root, square)

        @block.tensor
        def _(pe):
            def turn(c, b):
                pe.wait_ge(relu_done, c + 1)
                pe.wait_ge(y_done, c + 1)
                for r in range(CHUNK):
                    mm = nc.tensor.transpose(y_ps[b][:, r * P:(r + 1) * P], feat_t[b][:, r * P:(r + 1) * P], ident[:, :])
                mm.then_inc(turned, 1)

            def products_of(c, b, turn_before):
                for g in range(NGRP):
                    pe.wait_ge(filtered, NGRP * c + g + 1)
                    for j in range(GRP):
                        k = g * GRP + j
                        mm = nc.tensor.matmul(f_ps[b][:, :].rearrange("p (r n) -> p r n", n=P), g_all[:, k, :],
                                              a_t[b][:, :, k * P:(k + 1) * P], start=k == 0, stop=k == NB - 1)
                    if g == 1 and turn_before:
                        turn(c - 1, 1 - b)
                mm.then_inc(products, 1)

            pe.sem_inc(turned, 2)
            products_of(0, 0, False)
            with pe.Fori(0, NCHUNK // 2 - 1) as i:
                for s in range(2):
                    products_of(2 * i + 1 + s, 1 - s, True)
            products_of(NCHUNK - 1, 1, True)
            turn(NCHUNK - 1, 1)


def top_k_phase(nc, sem, dram, keep):
    PAD = -TOPK % 8
    ROUNDS = (TOPK + PAD) // 8
    W = PAD + N
    loaded, stored = sem("k_loaded"), sem("k_stored")
    padded, filtered, step, found, removed, kept, turned, copied = (
        sem("k_" + n) for n in ("padded", "filtered", "step", "found", "removed", "kept", "turned", "copied"))
    with ExitStack() as ctx:
        m = Mem(nc, ctx)
        row, f, left, out_t = m.sb("k_row", [P, N]), m.sb("k_f", [P, W]), m.sb("k_left", [P, W]), m.sb("k_out_t", [P, N])
        best, pause = m.sb("k_best", [P, 8]), m.sb("k_pause", [P, 1])
        ps = [m.ps(f"k_ps{b}", [P, CW]) for b in range(2)]
        ident = keep["ident"]
        block = ctx.enter_context(nc.Block())

        @block.sync
        def _(sp):
            with sp.Fori(0, NB) as t:
                sp.wait_ge(turned, NCHUNK * (t + 1))
                sp.dma_start(row[:, :], dram["adj"][bass.ds(t * P, P), :]).then_inc(loaded, 16)
                sp.wait_ge(copied, NCHUNK * (t + 1) + 2)
                sp.dma_start(dram["adj_top_t"][bass.ds(t, 1), :, :].rearrange("a p n -> p (a n)"), out_t[:, :]).then_inc(stored, 16)
            sp.wait_ge(stored, 16 * (NB + 1))

        @block.scalar
        def _(act):
            with act.Fori(0, NB) as t:
                act.wait_ge(step, 3 * t + 1)
                nc.scalar.activation(f[:, PAD:W], f[:, PAD:W], ACT.Tanh).then_inc(filtered, 1)

        @block.vector
        def _(dve):
            nc.vector.memset(f[:, 0:PAD], 2.0).then_inc(padded, 1)
            dve.wait_ge(padded, 1)
            dve.sem_inc(stored, 16)
            with dve.Fori(0, NB) as t:
                dve.wait_ge(loaded, 16 * (t + 1))
                nc.vector.scalar_tensor_tensor(f[:, PAD:W], row[:, :], 0.0, row[:, :], ALU.max, ALU.mult).then_inc(step, 1)
                dve.wait_ge(filtered, t + 1)
                nc.vector.tensor_copy(left[:, :], f[:, :]).then_inc(step, 1)
                dve.wait_ge(step, 3 * t + 2)
                nc.vector.memset(pause[:, :], 0.0)
                with dve.Fori(0, ROUNDS) as r:
                    nc.vector.max(best[:, :], left[:, :]).then_inc(found, 1)
                    dve.wait_ge(found, t * ROUNDS + r + 1)
                    nc.vector.memset(pause[:, :], 0.0)
                    nc.vector.match_replace(left[:, :], best[:, :], left[:, :], -1.0).then_inc(removed, 1)
                    dve.wait_ge(removed, t * ROUNDS + r + 1)
                    nc.vector.memset(pause[:, :], 0.0)
                nc.vector.tensor_tensor(left[:, PAD:W], left[:, PAD:W], f[:, PAD:W], ALU.not_equal).then_inc(step, 1)
                dve.wait_ge(step, 3 * t + 3)
                nc.vector.tensor_tensor(row[:, :], row[:, :], left[:, PAD:W], ALU.mult).then_inc(kept, 1)
                dve.wait_ge(stored, 16 * (t + 1))
                for c in range(NCHUNK):
                    dve.wait_ge(turned, NCHUNK * (t + 1) + c + 1)
                    nc.vector.tensor_copy(out_t[:, c * CW:(c + 1) * CW], ps[c % 2][:, :]).then_inc(copied, 1)

        @block.tensor
        def _(pe):
            pe.sem_inc(turned, NCHUNK)
            pe.sem_inc(copied, 2)
            with pe.Fori(0, NB) as t:
                pe.wait_ge(kept, t + 1)
                for c in range(NCHUNK):
                    pe.wait_ge(copied, NCHUNK * t + c + 1)
                    for r in range(CHUNK):
                        k = c * CHUNK + r
                        mm = nc.tensor.transpose(ps[c % 2][:, r * P:(r + 1) * P], row[:, k * P:(k + 1) * P], ident[:, :])
                    mm.then_inc(turned, 1)


def build(nc, dram):
    with ExitStack() as top:
        def sem(name):
            return top.enter_context(nc.semaphore(name))

        m = Mem(nc, top)
        keep = {
            "ident": m.sb("ident", [P, P]),
            "off_diag": m.sb("off_diag", [P, P]),
            "sel": m.sb("sel", [P, 2, NUV]),
            "diag_bias": m.sb("diag_bias", [P, P], BF16),
            "den": m.sb("den", [P, NB, HEADS]),
            "ones": m.sb("ones", [P, 1]),
            "flags": m.sb("flags", [1, 2], I32),
        }
        keep["x_sb"] = keep["y_all"] = m.sb("x_sb", [P, NB, H])
        with ExitStack() as masks:
            mm = Mem(nc, masks)
            keep["uv_parts"] = mm.sb("uv_parts", [P, NB, NST], BF16)
            with ExitStack() as support:
                ms = Mem(nc, support)
                keep["x_hi"], keep["x_lo"] = ms.sb("x_hi", [P, NB, H], F32R), ms.sb("x_lo", [P, NB, H], F32R)
                keep["pieces"] = ms.sb("pieces", [P, RING, CHUNK, PW])
                keep["clear"] = ms.sb("clear", [P, 2 * NPIECE - 1, P])
                keep["loaded"] = [sem(f"a_loaded{g}") for g in range(RING)]
                setup_phase(nc, sem, dram, keep)
                support_phase(nc, sem, dram, keep)
            negative = nc.values_load(keep["flags"][0:1, 0:1], min_val=0, max_val=1)
            with nc.If(negative):
                signed_scores_phase(nc, sem, dram, keep)
                attention_phase(nc, sem, dram, keep, signed=True)
        with nc.Else():
            attention_phase(nc, sem, dram, keep, signed=False)
        gate_phase(nc, sem, dram, keep)
        keep["g_all"] = m.sb("g_all", [P, NB, H])
        norm_phase(nc, sem, dram, keep)
        many = nc.values_load(keep["flags"][0:1, 1:2], min_val=0, max_val=1)
        with nc.If(many):
            top_k_phase(nc, sem, dram, keep)
            graph_phase(nc, sem, dram, keep, "adj_top_t")
        with nc.Else():
            graph_phase(nc, sem, dram, keep, "adj_t")


def host_constants():
    import numpy as np

    ident = np.eye(P, dtype=np.float32)
    sel = np.zeros((P, 2, NUV), np.float32)
    for k in range(NPART):
        for h in range(HEADS):
            u, v = 1 + k * NUV + 2 * h, 1 + k * NUV + 2 * h + 1
            sel[u, 0, h] = sel[v, 1, h] = 1.0
            sel[v, 0, HEADS + h] = sel[u, 1, HEADS + h] = 1.0
    return {"ident": ident, "off_diag": 1.0 - ident, "sel": sel}


def host_layout(inputs):
    import numpy as np

    adj, x = np.asarray(inputs["adj"]), np.asarray(inputs["x"])
    lay = {
        "x": x,
        "x_t": x.T,
        "adj": adj,
        "adj_t": adj.reshape(NB, P, NB, P).transpose(0, 3, 2, 1).reshape(NB, P, N),
        "gat_W": np.asarray(inputs["L0_gnn_gat_W"]).transpose(1, 0, 2),
        "gat_W_t": np.asarray(inputs["L0_gnn_gat_W"]).transpose(0, 2, 1),
        "gat_a": np.asarray(inputs["L0_gnn_gat_a"]).reshape(HEADS, 2, H).transpose(2, 0, 1),
    }
    for k in ("edge", "node"):
        for w in ("Wih", "Whh"):
            lay[f"{k}_{w}_t"] = np.asarray(inputs[f"L0_gnn_{k}_{w}"]).T
        for w in ("bih", "bhh"):
            lay[f"{k}_{w}"] = np.asarray(inputs[f"L0_gnn_{k}_{w}"])
    for k in ("W_proj", "b_proj", "W_gcn", "b_gcn"):
        lay[k] = np.asarray(inputs[f"L1_gnn_{k}"])
    return {k: np.ascontiguousarray(v) for k, v in lay.items()}


def kernel(**inputs):
    import concourse.bacc as bacc
    from concourse.bass_utils import run_bass_kernel_spmd as run

    nc = bacc.Bacc("TRN2", target_bir_lowering=False, num_devices=1)
    arrays, dram = {}, {}
    for name, a in {**host_layout(inputs), **host_constants()}.items():
        arrays["in_" + name] = a
        dram[name] = nc.dram_tensor("in_" + name, a.shape, mybir.dt.from_np(a.dtype), kind="ExternalInput").ap()
    for name, shape in SCRATCH.items():
        dram[name] = nc.dram_tensor("scratch_" + name, shape, F32, kind="Internal").ap()
    dram["out"] = nc.dram_tensor("out", (N, H), F32, kind="ExternalOutput").ap()
    build(nc, dram)
    return run(nc, [arrays], core_ids=[0]).results[0]["out"]
```

```python
from contextlib import ExitStack

import concourse.bass as bass
from concourse import mybir

ALU = mybir.AluOpType
ACT = mybir.ActivationFunctionType
AX_X = mybir.AxisListType.X
F32 = mybir.dt.float32
F32R = mybir.dt.float32r
BF16 = mybir.dt.bfloat16
I32 = mybir.dt.int32

P = 128
N = 4096
H = 128
HEADS = 3
NB = N // P
CHUNK = 4
CW = CHUNK * P
NCHUNK = NB // CHUNK
GRP = 8
NGRP = NB // GRP
QUARTER = N // 4
PIECE = 4
PW = PIECE * P
NPIECE = NB // PIECE
RING = 4
HIS = 4
ALPHA = 0.2
NEG_INF = -9000000000000000.0
TOPK = 350
EPS = 1e-5
NPART = 3
NUV = 2 * HEADS
NST = 1 + NPART * NUV
LOWEST = -3.0e38
KINDS = ("edge", "node")
SCRATCH = {
    "e": (HEADS, N),
    "e_signed": (NUV, N),
    "ns_t": (P, N),
    "r_den": (HEADS, N),
    "y_t": (NB, P, HEADS * P),
    "adj_top_t": (NB, P, N),
}


class Mem:

    def __init__(self, nc, ctx):
        self.nc, self.ctx = nc, ctx

    def sb(self, name, shape, dt=F32):
        return self.ctx.enter_context(self.nc.sbuf_tensor(name, shape, dt))

    def ps(self, name, shape, dt=F32):
        return self.ctx.enter_context(self.nc.psum_tensor(name, shape, dt))


def load_piece(sp, dram, keep, c, g):
    sp.dma_start(keep["pieces"][g % RING],
                 dram["adj_t"][bass.ds(c * CHUNK, CHUNK), :, g * PW:(g + 1) * PW].rearrange("r p n -> p r n")
                 ).then_inc(keep["loaded"][g % RING], 16)


def setup_phase(nc, sem, dram, keep):
    x_ready, x_t_ready, w_ready = sem("s_x"), sem("s_xT"), sem("s_w")
    folded, folded_out = sem("s_folded"), sem("s_folded_out")
    uv_done, uv_out = sem("s_uv_done"), sem("s_uv_out")
    split, x_split = sem("s_split"), sem("s_x_split")
    with ExitStack() as ctx:
        m = Mem(nc, ctx)
        x_t = m.sb("x_t", [P, N])
        w_t = m.sb("w_t", [P, HEADS, H])
        a_sb = m.sb("a_sb", [P, HEADS, 2])
        w6 = m.sb("w6", [P, NUV])
        uv = m.sb("uv", [P, NB, NUV])
        rest = m.sb("rest", [P, NB, NUV])
        w6_ps = m.ps("w6_ps", [P, 512])
        uv_ps = m.ps("uv_ps", [P, 512])
        x_sb, uv_parts, ident, off_diag = keep["x_sb"], keep["uv_parts"], keep["ident"], keep["off_diag"]
        part = [uv_parts[:, :, 1 + k * NUV:1 + (k + 1) * NUV] for k in range(NPART)]
        block = ctx.enter_context(nc.Block())

        @block.sync
        def _(sp):
            sp.dma_start(w_t[:, :, :], dram["gat_W_t"].rearrange("h g f -> g h f")).then_inc(w_ready, 16)
            sp.dma_start(a_sb[:, :, :], dram["gat_a"]).then_inc(w_ready, 16)
            sp.dma_start(x_t[:, :], dram["x_t"]).then_inc(x_t_ready, 16)
            sp.dma_start(x_sb[:, :, :], dram["x"].rearrange("(t p) f -> p t f", p=P)).then_inc(x_ready, 16)
            sp.dma_start(ident[:, :], dram["ident"]).then_inc(x_ready, 16)
            sp.dma_start(off_diag[:, :], dram["off_diag"]).then_inc(x_ready, 16)
            sp.dma_start(keep["sel"][:, :], dram["sel"]).then_inc(x_ready, 16)
            for g in range(RING):
                if g == RING // 2:
                    sp.wait_ge(x_split, 3)
                load_piece(sp, dram, keep, 0, g)
            sp.wait_ge(x_ready, 64)

        @block.tensor
        def _(pe):
            pe.wait_ge(w_ready, 32)
            for h in range(HEADS):
                last = nc.tensor.matmul(w6_ps[:, 2 * h:2 * h + 2], w_t[:, h, :], a_sb[:, h, :], start=True, stop=True)
            last.then_inc(folded, 1)
            pe.wait_ge(folded_out, 1)
            pe.wait_ge(x_t_ready, 16)
            for t in range(NB):
                last = nc.tensor.matmul(uv_ps[:, t * NUV:(t + 1) * NUV], x_t[:, t * P:(t + 1) * P], w6[:, :],
                                        start=True, stop=True)
            last.then_inc(uv_done, 1)

        @block.vector
        def _(dve):
            nc.vector.memset(keep["ones"][:, :], 1.0)
            nc.vector.memset(uv_parts[:, :, 0:1], 1.0)
            nc.vector.memset(keep["clear"][:, :, :], 1.0).then_inc(x_split, 1)
            dve.wait_ge(folded, 1)
            nc.vector.tensor_copy(w6[:, :], w6_ps[:, 0:NUV]).then_inc(folded_out, 1)
            dve.wait_ge(x_ready, 64)
            nc.vector.tensor_scalar(keep["diag_bias"][:, :], ident[:, :], NEG_INF, None, ALU.mult)
            nc.vector.tensor_copy(keep["x_hi"][:, :, :], x_sb[:, :, :]).then_inc(x_split, 1)
            dve.wait_ge(x_split, 2)
            nc.vector.tensor_copy(keep["clear"][:, NPIECE - 1, :], off_diag[:, :])
            nc.vector.tensor_tensor(keep["x_lo"][:, :, :], x_sb[:, :, :], keep["x_hi"][:, :, :].bitcast(F32), ALU.subtract
                                    ).then_inc(x_split, 1)
            dve.wait_ge(uv_done, 1)
            nc.vector.tensor_copy(uv[:, :, :], uv_ps[:, 0:NB * NUV].rearrange("p (t j) -> p t j", j=NUV)).then_inc(uv_out, 1)
            dve.wait_ge(uv_out, 1)
            left = uv
            for k in range(NPART):
                nc.vector.tensor_copy(part[k], left[:, :, :]).then_inc(split, 1)
                dve.wait_ge(split, 2 * k + 1)
                if k < NPART - 1:
                    nc.vector.tensor_tensor(rest[:, :, :], left[:, :, :], part[k], ALU.subtract).then_inc(split, 1)
                    dve.wait_ge(split, 2 * k + 2)
                    left = rest


def support_phase(nc, sem, dram, keep):
    cleared, rounded, made, piece_done = sem("a_cleared"), sem("a_rounded"), sem("a_made"), sem("a_piece_done")
    products_out, e_sum, e_out, counted = sem("a_products_out"), sem("a_e_sum"), sem("a_e_out"), sem("a_counted")
    signed, paused = sem("a_signed"), sem("a_paused")
    e_step, flag_step, signs_added, signs_total = sem("a_e_step"), sem("a_flag_step"), sem("a_signs_added"), sem("a_signs_total")
    e_stored = [sem("a_e_stored0"), sem("a_e_stored1")]
    ns_stored = [sem("a_ns_stored0"), sem("a_ns_stored1")]
    with ExitStack() as ctx:
        m = Mem(nc, ctx)
        a_hi = [m.sb(f"a_hi{b}", [P, CHUNK, PW], F32R) for b in range(HIS)]
        pos = [m.sb(f"pos{b}", [P, CHUNK, PW], BF16) for b in range(2)]
        a_lo = [m.sb(f"a_lo{b}", [P, CHUNK, PW], F32R) for b in range(2)]
        signs = m.sb("signs", [P, CHUNK, PW], BF16)
        prod_sb = [m.sb(f"prod_sb{b}", [P, CW]) for b in range(2)]
        ns_sb = [m.sb(f"ns_sb{b}", [P, CW]) for b in range(2)]
        e_scl = m.sb("e_scl", [HEADS, CW])
        e_sb = [m.sb(f"e_sb{b}", [HEADS, CW]) for b in range(2)]
        pause = m.sb("a_pause", [P, 1])
        sign_sums = m.sb("sign_sums", [P, NCHUNK * NPIECE])
        sign_sum = m.sb("sign_sum", [P, 1])
        counts = m.sb("counts", [NST, NCHUNK])
        max_counts = m.sb("max_counts", [1, NCHUNK])
        max_count, count, negatives = m.sb("max_count", [1, 1]), m.sb("count", [1, 1]), m.sb("negatives", [1, 1])
        pos_ps = [m.ps(f"pos_ps{b}", [P, CW]) for b in range(2)]
        ns_ps = [m.ps(f"ns_ps{b}", [P, CW]) for b in range(2)]
        e_ps = m.ps("e_ps", [P, CW])
        total_ps = m.ps("total_ps", [P, CW])
        pieces, loaded, clear, x_hi, x_lo, uv_parts, sel = (
            keep[k] for k in ("pieces", "loaded", "clear", "x_hi", "x_lo", "uv_parts", "sel"))
        block = ctx.enter_context(nc.Block())

        @block.sync
        def _(sp):
            def spread_e(c, b, i):
                sp.wait_ge(e_stored[b], 16 * (i + 1))
                cols = bass.ds(c * CW, CW)
                sp.dma_start(keep["e_all"][:, :, cols], dram["e"][:, cols].partition_broadcast(P)).then_inc(keep["e_spread"], 16)

            def load(c, g):
                sp.wait_ge(made, 2 * (NPIECE * c + g - RING + 2))
                load_piece(sp, dram, keep, c, g)

            for g in range(RING, NPIECE):
                load(0, g)
            for g in range(NPIECE):
                load(1, g)
            with sp.Fori(1, NCHUNK // 2) as i:
                for b in range(2):
                    for g in range(NPIECE):
                        load(2 * i + b, g)
                        if g == 1:
                            spread_e(2 * i + b - 2, b, i)
            for k in range(2):
                sp.dma_start(keep["row"][k][:, :], dram["adj"][0:P, k * QUARTER:(k + 1) * QUARTER]).then_inc(keep["row_loaded"][k], 16)
            for b in range(2):
                spread_e(NCHUNK - 2 + b, b, NCHUNK // 2)

        @block.gpsimd
        def _(pool):
            pool.sem_inc(paused, 1)
            with pool.Fori(0, NCHUNK) as c:
                for g in range(NPIECE):
                    pool.wait_ge(loaded[g % RING], 16 * (NPIECE // RING * c + g // RING + 1))
                    pool.wait_ge(paused, NPIECE * c + g + 1)
                    nc.gpsimd.tensor_tensor(pause[:, :], keep["ones"][:, :], keep["ones"][:, :], ALU.mult).then_inc(paused, 1)
                    factor = clear[:, bass.ds(NPIECE - 1 + g - c, 1), :].rearrange("p a n -> p (a n)")
                    for r in range(CHUNK):
                        one = pieces[g % RING][:, r, r * P:(r + 1) * P]
                        nc.gpsimd.tensor_tensor(one, one, factor, ALU.mult).then_inc(cleared, 1)

        @block.scalar
        def _(act):
            act.sem_inc(products_out, 4)
            act.sem_inc(signed, 2)
            for b in range(2):
                act.sem_inc(e_stored[b], 16)
                act.sem_inc(ns_stored[b], 16)

            def split(c, b, g):
                n = NPIECE * c + g
                act.wait_ge(cleared, CHUNK * (n + 1))
                act.wait_ge(piece_done, n + 1)
                nc.scalar.copy(a_hi[g % HIS][:, :, :], pieces[g % RING]).then_inc(rounded, 1)
                act.wait_ge(signed, n + 2)
                nc.scalar.activation(signs[:, :, :], pieces[g % RING], ACT.Sign,
                                     accum_out=sign_sums[:, bass.ds(n, 1)]).then_inc(signed, 1)

            def take_out(c, b, i):
                act.wait_ge(piece_done, NPIECE * (c + 1) + HIS)
                act.wait_ge(e_sum, c + 1)
                act.wait_ge(counted, c + 1)
                nc.scalar.activation(prod_sb[b][0:NST, :], pos_ps[b][0:NST, :], ACT.Copy,
                                     accum_out=counts[:, bass.ds(c, 1)]).then_inc(products_out, 1)
                act.wait_ge(ns_stored[b], 16 * (i + 1))
                nc.scalar.copy(ns_sb[b][:, :], ns_ps[b][:, :]).then_inc(products_out, 1)
                act.wait_ge(products_out, 2 * (c + 1) + 4)
                act.dma_start(dram["ns_t"][:, bass.ds(c * CW, CW)], ns_sb[b][:, :]).then_inc(ns_stored[b], 16)

            def store_e(c, b):
                act.wait_ge(e_out, c + 3)
                act.dma_start(dram["e"][:, bass.ds(c * CW, CW)], e_sb[b][:, :]).then_inc(e_stored[b], 16)

            for g in range(NPIECE):
                split(0, 0, g)
            with act.Fori(0, NCHUNK // 2 - 1) as i:
                for s in range(2):
                    c, b = 2 * i + 1 + s, 1 - s
                    split(c, b, 0)
                    take_out(c - 1, s, i)
                    for g in range(1, NPIECE):
                        split(c, b, g)
                        if g == 5:
                            store_e(c - 1, s)
            split(NCHUNK - 1, 1, 0)
            take_out(NCHUNK - 2, 0, NCHUNK // 2 - 1)
            for g in range(1, NPIECE):
                split(NCHUNK - 1, 1, g)
            store_e(NCHUNK - 2, 0)
            take_out(NCHUNK - 1, 1, NCHUNK // 2 - 1)
            store_e(NCHUNK - 1, 1)
            for b in range(2):
                act.wait_ge(ns_stored[b], 16 * (NCHUNK // 2 + 1))
                act.wait_ge(e_stored[b], 16 * (NCHUNK // 2 + 1))

        @block.vector
        def _(dve):
            def make(c, b, g):
                n = NPIECE * c + g
                dve.wait_ge(cleared, CHUNK * (n + 1))
                dve.wait_ge(piece_done, n + 3)
                nc.vector.tensor_scalar(pos[g % 2][:, :, :], pieces[g % RING], 0.0, None, ALU.is_gt).then_inc(made, 1)
                dve.wait_ge(rounded, n + 1)
                dve.wait_ge(signed, n + 2)
                nc.vector.tensor_tensor(a_lo[g % 2][:, :, :], pieces[g % RING], a_hi[g % HIS][:, :, :].bitcast(F32),
                                        ALU.subtract).then_inc(made, 1)

            def count_rows(c, b):
                dve.wait_ge(products_out, 2 * (c + 1) + 3)
                nc.vector.tensor_reduce(max_counts[:, bass.ds(c, 1)], prod_sb[b][0:1, :], AX_X, ALU.max).then_inc(counted, 1)

            def make_e(c, b, i):
                dve.wait_ge(e_sum, c + 3)
                nc.vector.tensor_scalar(e_scl[:, :], e_ps[0:HEADS, :], ALPHA, None, ALU.mult).then_inc(e_step, 1)
                dve.wait_ge(e_step, c + 1)
                dve.wait_ge(e_stored[b], 16 * (i + 1))
                nc.vector.tensor_tensor(e_sb[b][:, :], e_ps[0:HEADS, :], e_scl[:, :], ALU.max).then_inc(e_out, 1)

            dve.sem_inc(e_out, 2)
            for b in range(2):
                nc.vector.memset(prod_sb[b][:, :], 0.0).then_inc(counted, 1)
            for g in range(NPIECE):
                make(0, 0, g)
            with dve.Fori(0, NCHUNK // 2 - 1) as i:
                for s in range(2):
                    c, b = 2 * i + 1 + s, 1 - s
                    for g in range(NPIECE):
                        make(c, b, g)
                        if g == 2:
                            count_rows(c - 1, s)
                        if g == 3:
                            make_e(c - 1, s, i)
            for g in range(NPIECE):
                make(NCHUNK - 1, 1, g)
            count_rows(NCHUNK - 2, 0)
            make_e(NCHUNK - 2, 0, NCHUNK // 2 - 1)
            dve.wait_ge(signed, NCHUNK * NPIECE + 2)
            nc.vector.tensor_reduce(sign_sum[:, :], sign_sums[:, :], AX_X, ALU.add).then_inc(signs_added, 1)
            count_rows(NCHUNK - 1, 1)
            dve.wait_ge(counted, NCHUNK + 2)
            nc.vector.tensor_reduce(max_count[:, :], max_counts[:, :], AX_X, ALU.max).then_inc(flag_step, 1)
            nc.vector.tensor_reduce(count[:, :], counts[0:1, :], AX_X, ALU.add).then_inc(flag_step, 1)
            dve.wait_ge(signs_total, 1)
            dve.wait_ge(flag_step, 2)
            nc.vector.tensor_tensor(negatives[:, :], count[:, :], total_ps[0:1, 0:1], ALU.subtract).then_inc(flag_step, 1)
            dve.wait_ge(flag_step, 3)
            nc.vector.tensor_scalar(keep["flags"][0:1, 0:1], negatives[:, :], 0.0, None, ALU.is_le)
            nc.vector.tensor_scalar(keep["flags"][0:1, 1:2], max_count[:, :], float(TOPK), None, ALU.is_le)
            make_e(NCHUNK - 1, 1, NCHUNK // 2 - 1)

        @block.tensor
        def _(pe):
            def wide(ps, rows=P):
                return ps[0:rows, :].rearrange("p (r n) -> p r n", n=P)

            def products(c, b, g):
                if g == 0:
                    pe.wait_ge(products_out, 2 * (c + 1))
                pe.wait_ge(made, 2 * (NPIECE * c + g + 1))
                for j in range(PIECE):
                    k = g * PIECE + j
                    cols = slice(j * P, (j + 1) * P)
                    first, last = k == 0, k == NB - 1
                    hi, lo = a_hi[g % HIS][:, :, cols], a_lo[g % 2][:, :, cols]
                    nc.tensor.matmul(wide(pos_ps[b], NST), uv_parts[:, k, :], pos[g % 2][:, :, cols], start=first, stop=last)
                    nc.tensor.matmul(wide(ns_ps[b]), x_hi[:, k, :], hi, start=first, stop=False)
                    nc.tensor.matmul(wide(ns_ps[b]), x_hi[:, k, :], lo, start=False, stop=False)
                    mm = nc.tensor.matmul(wide(ns_ps[b]), x_lo[:, k, :], hi, start=False, stop=last)
                mm.then_inc(piece_done, 1)

            def sum_e(c, b):
                pe.wait_ge(products_out, 2 * (c + 1) + 3)
                pe.wait_ge(e_out, c + 2)
                nc.tensor.matmul(e_ps[0:HEADS, :], sel[:, 0, 0:HEADS], prod_sb[b][:, :], start=True, stop=True
                                 ).then_inc(e_sum, 1)

            pe.sem_inc(piece_done, HIS)
            pe.sem_inc(e_sum, 2)
            for g in range(NPIECE):
                products(0, 0, g)
            with pe.Fori(0, NCHUNK // 2 - 1) as i:
                for s in range(2):
                    c, b = 2 * i + 1 + s, 1 - s
                    for g in range(NPIECE):
                        products(c, b, g)
                        if g == 2:
                            sum_e(c - 1, s)
            for g in range(NPIECE):
                products(NCHUNK - 1, 1, g)
                if g == 2:
                    sum_e(NCHUNK - 2, 0)
            pe.wait_ge(signs_added, 1)
            nc.tensor.matmul(total_ps[0:1, 0:1], sign_sum[:, :], keep["ones"][:, :], start=True, stop=True
                             ).then_inc(signs_total, 1)
            sum_e(NCHUNK - 1, 1)


def signed_scores_phase(nc, sem, dram, keep):
    loaded = [sem("m_loaded0"), sem("m_loaded1")]
    cleared, masked, mask_free = sem("m_cleared"), sem("m_masked"), sem("m_mask_free")
    products_out = sem("m_products_out")
    e_sum, e_step, e_out = sem("m_e_sum"), sem("m_e_step"), sem("m_e_out")
    e_stored = [sem("m_e_stored0"), sem("m_e_stored1")]
    with ExitStack() as ctx:
        m = Mem(nc, ctx)
        a_t = [m.sb(f"m_a_t{b}", [P, CHUNK, N]) for b in range(2)]
        pos = [m.sb(f"m_pos{b}", [P, CHUNK, GRP * P], BF16) for b in range(2)]
        neg = [m.sb(f"m_neg{b}", [P, CHUNK, GRP * P], BF16) for b in range(2)]
        prod_sb = [m.sb(f"m_prod_sb{b}", [P, 2, CW]) for b in range(2)]
        e_scl = m.sb("m_e_scl", [NUV, CW])
        e_sb = [m.sb(f"m_e_sb{b}", [NUV, CW]) for b in range(2)]
        pos_ps = [m.ps(f"m_pos_ps{b}", [P, CW]) for b in range(2)]
        neg_ps = [m.ps(f"m_neg_ps{b}", [P, CW]) for b in range(2)]
        e_ps = m.ps("m_e_ps", [P, CW])
        uv_parts, off_diag, sel = (keep[k] for k in ("uv_parts", "off_diag", "sel"))
        block = ctx.enter_context(nc.Block())

        @block.sync
        def _(sp):
            def load(b, c):
                for r in range(CHUNK):
                    sp.dma_start(a_t[b][:, r, :],
                                 dram["adj_t"][bass.ds(c * CHUNK + r, 1), :, :].rearrange("a p n -> p (a n)")
                                 ).then_inc(loaded[b], 16)

            sp.wait_ge(keep["e_spread"], 16 * NCHUNK)
            for k in range(2):
                sp.wait_ge(keep["row_loaded"][k], 16)
            for b in range(2):
                load(b, b)
            with sp.Fori(0, NCHUNK // 2 - 1) as i:
                for b in range(2):
                    sp.wait_ge(mask_free, NGRP * (2 * i + b + 1) + 2)
                    load(b, 2 * i + b + 2)

        @block.gpsimd
        def _(pool):
            with pool.Fori(0, NCHUNK // 2) as i:
                for b in range(2):
                    pool.wait_ge(loaded[b], 16 * CHUNK * (i + 1))
                    for r in range(CHUNK):
                        diag = a_t[b][:, r, bass.ds(((2 * i + b) * CHUNK + r) * P, P)]
                        nc.gpsimd.tensor_tensor(diag, diag, off_diag[:, :], ALU.mult).then_inc(cleared, 1)

        @block.vector
        def _(dve):
            for b in range(2):
                nc.vector.memset(prod_sb[b][:, :, :], 0.0).then_inc(e_out, 1)
            with dve.Fori(0, NCHUNK // 2) as i:
                for b in range(2):
                    c = 2 * i + b
                    dve.wait_ge(cleared, CHUNK * (c + 1))
                    for g in range(NGRP):
                        src = a_t[b][:, :, g * GRP * P:(g + 1) * GRP * P]
                        dve.wait_ge(mask_free, NGRP * c + g + 1)
                        nc.vector.tensor_scalar(pos[g % 2][:, :, :], src, 0.0, None, ALU.is_gt)
                        nc.vector.tensor_scalar(neg[g % 2][:, :, :], src, 0.0, None, ALU.is_lt).then_inc(masked, 1)
                    dve.wait_ge(e_sum, c + 1)
                    nc.vector.tensor_scalar(e_scl[:, :], e_ps[0:NUV, :], ALPHA, None, ALU.mult).then_inc(e_step, 1)
                    dve.wait_ge(e_step, c + 1)
                    dve.wait_ge(e_stored[b], 16 * (i + 1))
                    nc.vector.tensor_tensor(e_sb[b][:, :], e_ps[0:NUV, :], e_scl[:, :], ALU.max).then_inc(e_out, 1)

        @block.tensor
        def _(pe):
            pe.sem_inc(mask_free, 2)
            with pe.Fori(0, NCHUNK // 2) as i:
                for b in range(2):
                    c = 2 * i + b
                    pe.wait_ge(products_out, 2 * (c + 1))
                    for g in range(NGRP):
                        pe.wait_ge(masked, NGRP * c + g + 1)
                        for j in range(GRP):
                            k = g * GRP + j
                            cols = slice(j * P, (j + 1) * P)
                            first, last = k == 0, k == NB - 1
                            nc.tensor.matmul(pos_ps[b][0:NST, :].rearrange("p (r n) -> p r n", n=P), uv_parts[:, k, :],
                                             pos[g % 2][:, :, cols], start=first, stop=last)
                            mm = nc.tensor.matmul(neg_ps[b][0:NST, :].rearrange("p (r n) -> p r n", n=P), uv_parts[:, k, :],
                                                  neg[g % 2][:, :, cols], start=first, stop=last)
                        mm.then_inc(mask_free, 1)
                    pe.wait_ge(products_out, 2 * (c + 1) + 4)
                    pe.wait_ge(e_out, c + 2)
                    nc.tensor.matmul(e_ps[0:NUV, :], sel[:, 0, :], prod_sb[b][:, 0, :], start=True, stop=False)
                    nc.tensor.matmul(e_ps[0:NUV, :], sel[:, 1, :], prod_sb[b][:, 1, :], start=False, stop=True
                                     ).then_inc(e_sum, 1)

        @block.scalar
        def _(act):
            act.sem_inc(products_out, 4)
            for b in range(2):
                act.sem_inc(e_stored[b], 16)
            with act.Fori(0, NCHUNK // 2) as i:
                for b in range(2):
                    c = 2 * i + b
                    act.wait_ge(mask_free, NGRP * (c + 1) + 2)
                    act.wait_ge(e_out, c + 1)
                    nc.scalar.copy(prod_sb[b][0:NST, 0, :], pos_ps[b][0:NST, :]).then_inc(products_out, 1)
                    nc.scalar.copy(prod_sb[b][0:NST, 1, :], neg_ps[b][0:NST, :]).then_inc(products_out, 1)
                    act.wait_ge(e_out, c + 3)
                    act.dma_start(dram["e_signed"][:, bass.ds(c * CW, CW)], e_sb[b][:, :]).then_inc(e_stored[b], 16)
            for b in range(2):
                act.wait_ge(e_stored[b], 16 * (NCHUNK // 2 + 1))


UNIT = 2
NUNIT = NB // UNIT
SLOTS = 3
LEAD = 3
S_SLOTS = LEAD + 1
COLS = 8


def slot_of(u, b):
    return (u + b) % SLOTS


def units_since(u, b, parities):
    if u >= SLOTS:
        return SLOTS
    before = (b - 1) % parities
    return u + NUNIT - max(v for v in range(NUNIT) if slot_of(v, before) == slot_of(u, b))


def attention_phase(nc, sem, dram, keep, signed):
    tag = "s" if signed else "b"
    sets = 1 if signed else 2
    ahead = max(S_SLOTS, *(1 + units_since(u, b, sets) for u in range(SLOTS) for b in range(sets)))
    e_loaded = sem("s_e_loaded") if signed else keep["e_spread"]
    x_loaded = sem("b_x_loaded")
    row_loaded = [sem(f"s_row_loaded{s}") for s in range(2)] if signed else keep["row_loaded"]
    sign_done, bias_made, bias_ready = sem("b_sign_done"), sem("b_bias_made"), sem("b_bias_ready")
    logits_done, max_negated, exps_done = sem("b_logits_done"), sem("b_max_negated"), sem("b_exps_done")
    cols_loaded = [sem(f"b_cols_loaded{s}") for s in range(2)]
    transposed, scaled, multiplied = sem("b_transposed"), sem("b_scaled"), sem("b_multiplied")
    y_out = sem("b_y_out")
    y_stored = [sem(f"b_y_stored{s}") for s in range(2)]
    e_neg_loaded, e_neg_used, neg_step = (sem(f"b_{n}") for n in ("e_neg_loaded", "e_neg_used", "neg_step")) if signed else (None,) * 3
    with ExitStack() as ctx:
        m = Mem(nc, ctx)
        e_pos = m.sb(tag + "e_pos", [P, HEADS, N]) if signed else keep["e_all"]
        q = [m.sb(f"{tag}q{b}", [P, HEADS, N]) for b in range(sets)]
        bias = [m.sb(f"{tag}bias{b}", [P, N], BF16) for b in range(sets)]
        if signed:
            bias_neg = m.sb(tag + "bias_neg", [P, N], BF16)
            e_neg = m.sb(tag + "e_neg", [P, N])
            logits_neg = m.sb(tag + "logits_neg", [P, N])
        row = [m.sb(f"{tag}row{s}", [P, QUARTER]) for s in range(2)] if signed else keep["row"]
        cols = [m.sb(f"{tag}cols{s}", [P, N // COLS]) for s in range(2)]
        s_t = [m.sb(f"{tag}s_t{s}", [P, UNIT, HEADS * P]) for s in range(S_SLOTS)]
        row_max = m.sb(tag + "row_max", [P, 2, HEADS])
        neg_max = m.sb(tag + "neg_max", [P, 2, HEADS])
        y_sb = [m.sb(f"{tag}y_sb{s}", [P, HEADS * P]) for s in range(2)]
        pause = m.sb(tag + "pause", [P, 1])
        q_t = [m.ps(f"{tag}q_t{s}", [P, UNIT, 512]) for s in range(SLOTS)]
        y_ps = [m.ps(f"{tag}y_ps{b}", [P, 512]) for b in range(2)]
        x_sb, ident, diag_bias, den = keep["x_sb"], keep["ident"], keep["diag_bias"], keep["den"]
        block = ctx.enter_context(nc.Block())

        @block.sync
        def _(sp):
            if signed:
                for h in range(HEADS):
                    sp.dma_start(e_pos[:, h, :], dram["e_signed"][h, :].partition_broadcast(P)).then_inc(e_loaded, 16)
            sp.dma_start(x_sb[:, :, :], dram["x"].rearrange("(t p) f -> p t f", p=P)).then_inc(x_loaded, 16)
            with nc.allow_non_contiguous_dma(reason="biases and the diagonal"):
                for j, k in enumerate(KINDS):
                    for s, w in enumerate(("_bih", "_bhh")):
                        sp.dma_start(keep["biases"][:, j, s, :], dram[k + w].rearrange("(g p) -> p g", p=P)
                                     ).then_inc(keep["small_loaded"], 16)
                sp.dma_start(keep["diag"][:, :], dram["adj"].rearrange("a b -> (a b)")[0:N * N:N + 1]
                             .rearrange("(t p) -> p t", p=P)).then_inc(keep["small_loaded"], 16)

            def load_cols(t):
                for k in range(COLS):
                    sp.wait_ge(scaled, NUNIT // COLS * (COLS * t + k - 1) + ahead)
                    sp.dma_start(cols[k % 2][:, :], dram["adj_t"][bass.ds(t, 1), :, k * N // COLS:(k + 1) * N // COLS]
                                 .rearrange("a p n -> p (a n)")).then_inc(cols_loaded[k % 2], 16)

            with sp.Fori(0, NB) as t:
                if signed:
                    for h in range(HEADS):
                        sp.wait_ge(e_neg_used, HEADS * t + h + 1)
                        sp.dma_start(e_neg[:, :], dram["e_signed"][HEADS + h, :].partition_broadcast(P)).then_inc(e_neg_loaded, 16)
                load_cols(t)
            sp.wait_ge(keep["small_loaded"], 16 * 5)

        @block.gpsimd
        def _(pool):
            per_tile = 8 if signed else 4
            with pool.Fori(0, NB // sets) as i:
                for b in range(sets):
                    t = sets * i + b
                    pool.wait_ge(bias_made, per_tile * (t + 1))
                    for buf in [bias[b]] + ([bias_neg] if signed else []):
                        diag = buf[:, bass.ds(t * P, P)]
                        nc.gpsimd.tensor_tensor(diag, diag, diag_bias[:, :], ALU.add).then_inc(bias_ready, 1)

        @block.scalar
        def _(act):
            def load_row(t, k):
                act.dma_start(row[k % 2][:, :], dram["adj"][bass.ds(t * P, P), k * QUARTER:(k + 1) * QUARTER]
                              ).then_inc(row_loaded[k % 2], 16)

            def make_bias(t, b, more=True):
                for k in range(4):
                    piece = slice(k * QUARTER, (k + 1) * QUARTER)
                    act.wait_ge(row_loaded[k % 2], 16 * (2 * t + k // 2 + 1))
                    if k == 0:
                        act.wait_ge(logits_done, HEADS * (t + 1))
                    sign = (bias_neg if signed else bias[b])[:, piece]
                    nc.scalar.activation(sign, row[k % 2][:, :], ACT.Sign).then_inc(sign_done, 1)
                    act.wait_ge(sign_done, 4 * t + k + 1)
                    if k < 2:
                        load_row(t, k + 2)
                    elif more:
                        load_row(t + 1, k - 2)
                    if signed:
                        nc.scalar.activation(bias[b][:, piece], sign, ACT.Copy, bias=NEG_INF, scale=-NEG_INF).then_inc(bias_made, 1)
                        act.wait_ge(bias_made, 8 * t + 2 * k + 1)
                        nc.scalar.activation(sign, sign, ACT.Copy, bias=NEG_INF, scale=NEG_INF).then_inc(bias_made, 1)
                    else:
                        nc.scalar.activation(sign, sign, ACT.Copy, bias=NEG_INF, scale=-NEG_INF).then_inc(bias_made, 1)

            def make_exps(t, b):
                for h in range(HEADS):
                    act.wait_ge(logits_done, HEADS * (t + sets) + h + 1)
                    nc.scalar.mul(neg_max[:, b, h:h + 1], row_max[:, b, h:h + 1], -1.0).then_inc(max_negated, 1)
                    act.wait_ge(max_negated, HEADS * t + h + 1)
                    nc.scalar.activation(q[b][:, h, :], q[b][:, h, :], ACT.Exp, bias=neg_max[:, b, h:h + 1],
                                         accum_out=den[:, bass.ds(t, 1), h]).then_inc(exps_done, 1)

            def store_y(t, s, i):
                act.wait_ge(multiplied, NUNIT * (t + 1) + ahead)
                act.wait_ge(y_stored[s], 16 * (i + 1))
                nc.scalar.copy(y_sb[s][:, :], y_ps[s][:, 0:HEADS * P]).then_inc(y_out, 1)
                act.wait_ge(y_out, t + 3)
                act.dma_start(dram["y_t"][bass.ds(t, 1), :, :].rearrange("a p n -> p (a n)"), y_sb[s][:, :]
                              ).then_inc(y_stored[s], 16)

            act.sem_inc(y_out, 2)
            for s in range(2):
                act.sem_inc(y_stored[s], 16)
                if signed:
                    load_row(0, s)
            if signed:
                make_bias(0, 0)
                make_exps(0, 0)
                with act.Fori(0, NB // 2 - 1) as i:
                    for s in range(2):
                        make_bias(2 * i + s + 1, 0)
                        make_exps(2 * i + s + 1, 0)
                        store_y(2 * i + s, s, i)
                make_bias(NB - 1, 0, more=False)
                make_exps(NB - 1, 0)
                store_y(NB - 2, 0, NB // 2 - 1)
                store_y(NB - 1, 1, NB // 2 - 1)
            else:
                make_bias(0, 0)
                make_exps(0, 0)
                make_bias(1, 1)
                make_bias(2, 0)
                with act.Fori(0, NB // 2 - 2) as i:
                    for s in range(2):
                        make_exps(2 * i + s + 1, 1 - s)
                        store_y(2 * i + s, s, i)
                        make_bias(2 * i + s + 3, 1 - s)
                for t in range(NB - 4, NB):
                    if t + 1 < NB:
                        make_exps(t + 1, 1 - t % 2)
                    store_y(t, t % 2, t // 2)
                    if t + 3 < NB:
                        make_bias(t + 3, 1 - t % 2, more=False)
            for s in range(2):
                act.wait_ge(y_stored[s], 16 * (NB // 2 + 1))

        @block.vector
        def _(dve):
            def logits(t, b, h):
                if h == 0:
                    dve.wait_ge(bias_ready, (2 if signed else 1) * (t + 1))
                    dve.wait_ge(transposed, NUNIT * (t + 1))
                    nc.vector.memset(pause[:, :], 0.0)
                ttr = nc.vector.tensor_tensor_reduce(q[b][:, h, :], bias[b][:, :], e_pos[:, h, :], 1.0, LOWEST,
                                                     ALU.add, ALU.max, row_max[:, b, h:h + 1])
                if not signed:
                    ttr.then_inc(logits_done, 1)
                    return
                ttr.then_inc(neg_step, 1)
                n = 3 * (HEADS * t + h)
                dve.wait_ge(e_neg_loaded, 16 * (HEADS * t + h + 1))
                nc.vector.tensor_tensor(logits_neg[:, :], bias_neg[:, :], e_neg[:, :], ALU.add).then_inc(neg_step, 1)
                dve.wait_ge(neg_step, n + 2)
                dve.sem_inc(e_neg_used, 1)
                nc.vector.tensor_tensor(q[b][:, h, :], q[b][:, h, :], logits_neg[:, :], ALU.max).then_inc(neg_step, 1)
                dve.wait_ge(neg_step, n + 3)
                nc.vector.tensor_reduce(row_max[:, b, h:h + 1], q[b][:, h, :], AX_X, ALU.max).then_inc(logits_done, 1)

            def scale_units(t, b, between):
                for u in range(NUNIT):
                    s, per = slot_of(u, b), NUNIT // COLS
                    n = NUNIT * t + u
                    if u % per == 0:
                        k = u // per
                        dve.wait_ge(cols_loaded[k % 2], 16 * (COLS // 2 * t + k // 2 + 1))
                    dve.wait_ge(transposed, n + 1 + NUNIT * sets)
                    dve.wait_ge(multiplied, n - S_SLOTS + 1 + ahead)
                    a = cols[u // per % 2][:, (u % per) * UNIT * P:(u % per + 1) * UNIT * P]
                    a = a.rearrange("p (k r) -> p k r", r=P).unsqueeze(2).broadcast_to([P, UNIT, HEADS, P])
                    nc.vector.tensor_tensor(s_t[u % S_SLOTS][:, :, :].rearrange("p k (h r) -> p k h r", r=P),
                                            q_t[s][:, :, 0:HEADS * P].rearrange("p k (h r) -> p k h r", r=P),
                                            a, ALU.mult).then_inc(scaled, 1)
                    if u in between:
                        between[u]()

            dve.sem_inc(logits_done, HEADS * sets)
            dve.sem_inc(scaled, ahead)
            if signed:
                dve.sem_inc(e_neg_used, 1)
            dve.wait_ge(e_loaded, 16 * (HEADS if signed else NCHUNK))
            if signed:
                with dve.Fori(0, NB) as t:
                    for h in range(HEADS):
                        logits(t, 0, h)
                    scale_units(t, 0, {})
            else:
                def with_next(t, b):
                    scale_units(t, b, {u: (lambda h=h: logits(t + 1, 1 - b, h)) for h, u in enumerate((1, 5, 9))})

                for h in range(HEADS):
                    logits(0, 0, h)
                with dve.Fori(0, NB // 2 - 1) as i:
                    for b in range(2):
                        with_next(2 * i + b, b)
                with_next(NB - 2, 0)
                scale_units(NB - 1, 1, {})

        @block.tensor
        def _(pe):
            def transposes(t, b, u):
                s = slot_of(u, b)
                if u == 0:
                    pe.wait_ge(exps_done, HEADS * (t + 1))
                pe.wait_ge(scaled, NUNIT * t + u - units_since(u, b, sets) + 1 + ahead)
                for j in range(UNIT):
                    k = UNIT * u + j
                    for h in range(HEADS):
                        mm = nc.tensor.transpose(q_t[s][:, j, h * P:(h + 1) * P], q[b][:, h, k * P:(k + 1) * P], ident[:, :])
                mm.then_inc(transposed, 1)

            def products(t, b, y, u):
                pe.wait_ge(scaled, NUNIT * t + u + 1 + ahead)
                for j in range(UNIT):
                    k = UNIT * u + j
                    mm = nc.tensor.matmul(y_ps[y][:, 0:HEADS * P], x_sb[:, k, :], s_t[u % S_SLOTS][:, j, :],
                                          start=k == 0, stop=k == NB - 1)
                mm.then_inc(multiplied, 1)

            def tile(t, b, y, more=True):
                for u in range(NUNIT):
                    if u < NUNIT - LEAD:
                        transposes(t, b, u + LEAD)
                    elif more:
                        transposes(t + 1, (b + 1) % sets, u + LEAD - NUNIT)
                    if u == 0:
                        pe.wait_ge(y_out, t + 1)
                    products(t, b, y, u)

            pe.sem_inc(transposed, NUNIT * sets)
            pe.sem_inc(multiplied, ahead)
            for u in range(LEAD):
                transposes(0, 0, u)
            pe.wait_ge(x_loaded, 16)
            with pe.Fori(0, NB // 2 - 1) as i:
                for y in range(2):
                    tile(2 * i + y, y % sets, y)
            tile(NB - 2, 0, 0)
            tile(NB - 1, 1 % sets, 1, more=False)


GATES = ("hid_n", "r", "z", "in_n")
ES_STEPS = 2 * HEADS - 1


def gate_phase(nc, sem, dram, keep):
    w_loaded, bias_step, recip, turned_den, den_out, r_stored = (
        sem("g_" + n) for n in ("w_loaded", "bias_step", "recip", "turned_den", "den_out", "r_stored"))
    loaded = [sem("g_loaded0"), sem("g_loaded1")]
    r_loaded = [sem("g_r_loaded0"), sem("g_r_loaded1")]
    supports, es_step, cells, turned, y_done, centered = (
        sem("g_" + n) for n in ("supports", "es_step", "cells", "turned", "y_done", "centered"))
    gates_made, gates_read, pre_step, n_made, cell_step = (
        {k: sem(f"g_{k}_{n}") for k in KINDS} for n in ("gates", "read", "pre", "n", "cell"))
    squared = keep["squared"]
    with ExitStack() as ctx:
        m = Mem(nc, ctx)
        gat_w = m.sb("gat_w", [P, HEADS, H])
        wih = {k: m.sb(k + "_wih", [P, 3 * H]) for k in KINDS}
        whh = {k: m.sb(k + "_whh", [P, 3 * H]) for k in KINDS}
        r_den = m.sb("r_den", [P, HEADS, NB])
        r_den_t = m.sb("r_den_t", [HEADS * NB, P])

        def pair(name, shape):
            return [m.sb(f"g_{name}{b}", shape) for b in range(2)]

        x_t, ns_t, y_t, r_rows = (pair("x_t", [P, CW]), pair("ns_t", [P, CW]), pair("y_t", [P, CHUNK, HEADS * P]),
                                  pair("r_rows", [P, HEADS, CW]))
        scaled = m.sb("g_scaled", [P, HEADS, CW])
        es, both = m.sb("g_es", [P, CW]), m.sb("g_both", [P, CW])
        hid_n, r, z, n, pre, cell = ({k: m.sb(f"g_{k}_{name}", [P, CW]) for k in KINDS}
                                     for name in ("hid_n", "r", "z", "n", "pre", "cell"))
        squares = m.sb("g_squares", [P, CHUNK, H])
        mean = m.sb("g_mean", [P, NB])
        bias_cols = m.sb("g_bias", [P, len(KINDS), 4])
        gate_bias = {k: {"rz": bias_cols[:, j, 0:2], "r": bias_cols[:, j, 0:1], "z": bias_cols[:, j, 1:2],
                         "in_n": bias_cols[:, j, 2:3], "hid_n": bias_cols[:, j, 3:4]} for j, k in enumerate(KINDS)}
        ps = {k: {g: m.ps(f"g_ps_{k}_{g}", [P, CW]) for g in GATES} for k in KINDS}
        head_ps = [ps["edge"][g] for g in ("r", "z", "in_n")]
        turned_ps = ps["node"]["in_n"]
        ident, y_all, diag, square_sums = (keep[k] for k in ("ident", "y_all", "diag", "square_sums"))
        block = ctx.enter_context(nc.Block())

        def weights(k, g):
            at = {"r": 0, "z": H, "in_n": 2 * H, "hid_n": 2 * H}[g]
            return (None if g == "in_n" else whh[k][:, at:at + H]), (None if g == "hid_n" else wih[k][:, at:at + H])

        @block.sync
        def _(sp):
            def load(c, b):
                sp.dma_start(x_t[b][:, :], dram["x_t"][:, bass.ds(c * CW, CW)]).then_inc(loaded[b], 16)
                sp.dma_start(y_t[b][:, :, :], dram["y_t"][bass.ds(c * CHUNK, CHUNK), :, :].rearrange("r p n -> p r n")
                             ).then_inc(loaded[b], 16)
                sp.dma_start(ns_t[b][:, :], dram["ns_t"][:, bass.ds(c * CW, CW)]).then_inc(loaded[b], 16)

            def load_r(c, b):
                sp.dma_start(r_rows[b][:, :, :], dram["r_den"][:, bass.ds(c * CW, CW)].partition_broadcast(P)
                             ).then_inc(r_loaded[b], 16)

            sp.dma_start(gat_w[:, :, :], dram["gat_W"]).then_inc(w_loaded, 16)
            load(0, 0)
            for k in KINDS:
                sp.dma_start(wih[k][:, :], dram[k + "_Wih_t"]).then_inc(w_loaded, 16)
                sp.dma_start(whh[k][:, :], dram[k + "_Whh_t"]).then_inc(w_loaded, 16)
            sp.wait_ge(den_out, 1)
            sp.dma_start(dram["r_den"].rearrange("h (t p) -> (h t) p", p=P), r_den_t[:, :]).then_inc(r_stored, 16)
            load(1, 1)
            sp.wait_ge(r_stored, 16)
            load_r(0, 0)
            load_r(1, 1)
            prefetch_graph(sp, dram, keep)
            with sp.Fori(1, NCHUNK // 2) as i:
                for b in range(2):
                    sp.wait_ge(cells, 2 * i + b - 1)
                    load(2 * i + b, b)
                    load_r(2 * i + b, b)

        @block.tensor
        def _(pe):
            def gate(k, g, b):
                w_hid, w_in = weights(k, g)
                if w_hid is not None:
                    mm = nc.tensor.matmul(ps[k][g][:, :], w_hid, x_t[b][:, :], start=True, stop=w_in is None)
                if w_in is not None:
                    mm = nc.tensor.matmul(ps[k][g][:, :], w_in, (ns_t[b] if k == "edge" else es)[:, :],
                                          start=w_hid is None, stop=True)
                mm.then_inc(gates_made[k], 1)

            def stage(c, b, i, before, after, long_before):
                if after:
                    pe.wait_ge(loaded[b], 3 * 16 * (i + 1))
                    if before:
                        pe.wait_ge(pre_step["edge"], 2 * c)
                    for h in range(HEADS):
                        nc.tensor.matmul(head_ps[h][:, :].rearrange("p (r n) -> p r n", n=P), gat_w[:, h, :],
                                         y_t[b][:, :, h * P:(h + 1) * P], start=True, stop=True).then_inc(supports, 1)
                    gate("edge", "hid_n", b)
                    for h, g in enumerate(("r", "z", "in_n")):
                        pe.wait_ge(es_step, ES_STEPS * c + h + 1)
                        gate("edge", g, b)
                if before:
                    pe.wait_ge(cells, c)
                    for q in range(CHUNK):
                        mm = nc.tensor.transpose(turned_ps[:, q * P:(q + 1) * P], both[:, q * P:(q + 1) * P], ident[:, :])
                    mm.then_inc(turned, 1)
                if after:
                    gate("node", "hid_n", b)
                    pe.wait_ge(es_step, ES_STEPS * (c + 1))
                    gate("node", "r", b)
                    gate("node", "z", b)
                    if before:
                        pe.wait_ge(y_done, CHUNK * c)
                    gate("node", "in_n", b)

            pe.wait_ge(recip, 2)
            nc.tensor.transpose(ps["node"]["r"][0:HEADS * NB, 0:P], r_den[:, :, :].rearrange("p h t -> p (h t)"), ident[:, :]
                                ).then_inc(turned_den, 1)
            pe.wait_ge(w_loaded, 16 * 5)
            stages(pe, stage)

        @block.scalar
        def _(act):
            def read_gates(k, c):
                made = gates_made[k]
                act.wait_ge(made, 4 * c + 1)
                nc.scalar.activation(hid_n[k][:, :], ps[k]["hid_n"][:, :], ACT.Identity, bias=gate_bias[k]["hid_n"]).then_inc(gates_read[k], 1)
                for j, (g, out) in enumerate((("r", r), ("z", z))):
                    act.wait_ge(made, 4 * c + 2 + j)
                    nc.scalar.activation(out[k][:, :], ps[k][g][:, :], ACT.Tanh, bias=gate_bias[k][g], scale=0.5).then_inc(gates_read[k], 1)

            def make_n(k, c):
                act.wait_ge(pre_step[k], 2 * (c + 1))
                nc.scalar.activation(n[k][:, :], pre[k][:, :], ACT.Tanh, bias=gate_bias[k]["in_n"]).then_inc(n_made[k], 1)

            def square_y(c):
                act.wait_ge(centered, 3 * (c + 1))
                for q in range(CHUNK):
                    t = CHUNK * c + q
                    act.wait_ge(squared, t + 1)
                    nc.scalar.activation(squares[:, q, :], y_all[:, bass.ds(t, 1), :].rearrange("p a f -> p (a f)"), ACT.Square,
                                         accum_out=square_sums[:, bass.ds(t, 1)]).then_inc(squared, 1)

            def stage(c, b, i, before, after, long_before):
                if before:
                    read_gates("node", c - 1)
                    make_n("node", c - 1)
                if long_before:
                    square_y(c - 2)
                if after:
                    read_gates("edge", c)
                    make_n("edge", c)

            act.sem_inc(squared, 1)
            act.wait_ge(bias_step, 8)
            stages(act, stage)
            square_y(NCHUNK - 1)

        @block.vector
        def _(dve):
            def pre_n(k, c):
                dve.wait_ge(gates_read[k], 3 * (c + 1))
                nc.vector.scalar_tensor_tensor(pre[k][:, :], r[k][:, :], 1.0, hid_n[k][:, :], ALU.add, ALU.mult).then_inc(pre_step[k], 1)
                dve.wait_ge(pre_step[k], 2 * c + 1)
                dve.wait_ge(gates_made[k], 4 * (c + 1))
                nc.vector.scalar_tensor_tensor(pre[k][:, :], pre[k][:, :], 0.5, ps[k]["in_n"][:, :], ALU.mult, ALU.add
                                               ).then_inc(pre_step[k], 1)

            def make_cell(k, c, b):
                out, step = cell[k][:, :], cell_step[k]
                dve.wait_ge(n_made[k], c + 1)
                nc.vector.tensor_tensor(out, x_t[b][:, :], n[k][:, :], ALU.subtract).then_inc(step, 1)
                dve.wait_ge(step, 3 * c + 1)
                nc.vector.scalar_tensor_tensor(out, z[k][:, :], 1.0, out, ALU.add, ALU.mult).then_inc(step, 1)
                dve.wait_ge(step, 3 * c + 2)
                nc.vector.scalar_tensor_tensor(out, out, 0.5, n[k][:, :], ALU.mult, ALU.add).then_inc(step, 1)

            def support(c, b, i):
                dve.wait_ge(r_loaded[b], 16 * (i + 1))
                for h in range(HEADS):
                    dve.wait_ge(supports, HEADS * c + h + 1)
                    nc.vector.tensor_tensor(scaled[:, h, :], head_ps[h][:, :], r_rows[b][:, h, :], ALU.mult).then_inc(es_step, 1)
                dve.wait_ge(es_step, ES_STEPS * c + 2)
                nc.vector.tensor_tensor(es[:, :], scaled[:, 0, :], scaled[:, 1, :], ALU.add).then_inc(es_step, 1)
                dve.wait_ge(es_step, ES_STEPS * c + 4)
                nc.vector.tensor_tensor(es[:, :], es[:, :], scaled[:, 2, :], ALU.add).then_inc(es_step, 1)

            def make_y(c):
                dve.wait_ge(turned, c + 1)
                for q in range(CHUNK):
                    one = bass.ds(CHUNK * c + q, 1)
                    y = y_all[:, one, :].rearrange("p a f -> p (a f)")
                    nc.vector.scalar_tensor_tensor(y, turned_ps[:, q * P:(q + 1) * P], diag[:, one], y, ALU.mult, ALU.add
                                                   ).then_inc(y_done, 1)

            def center(c):
                rows = bass.ds(CHUNK * c, CHUNK)
                y, mu = y_all[:, rows, :], mean[:, rows]
                dve.wait_ge(y_done, CHUNK * (c + 1))
                nc.vector.tensor_reduce(mu, y, AX_X, ALU.add).then_inc(centered, 1)
                dve.wait_ge(centered, 3 * c + 1)
                nc.vector.tensor_scalar(mu, mu, 1.0 / H, None, ALU.mult).then_inc(centered, 1)
                dve.wait_ge(centered, 3 * c + 2)
                nc.vector.tensor_tensor(y, y, mu.unsqueeze(2).broadcast_to([P, CHUNK, H]), ALU.subtract).then_inc(centered, 1)

            def stage(c, b, i, before, after, long_before):
                if before:
                    pre_n("node", c - 1)
                if after:
                    support(c, b, i)
                if before:
                    make_cell("node", c - 1, 1 - b)
                    dve.wait_ge(cell_step["node"], 3 * c)
                    dve.wait_ge(cell_step["edge"], 3 * c)
                    nc.vector.tensor_tensor(both[:, :], cell["edge"][:, :], cell["node"][:, :], ALU.add).then_inc(cells, 1)
                if after:
                    pre_n("edge", c)
                if before:
                    make_y(c - 1)
                if after:
                    make_cell("edge", c, b)
                if before:
                    center(c - 1)

            for j, k in enumerate(KINDS):
                rz, b_in, b_hid = gate_bias[k]["rz"], keep["biases"][:, j, 0, :], keep["biases"][:, j, 1, :]
                nc.vector.tensor_tensor(rz, b_in[:, 0:2], b_hid[:, 0:2], ALU.add).then_inc(bias_step, 1)
                dve.wait_ge(bias_step, 4 * j + 1)
                nc.vector.tensor_scalar(rz, rz, 0.5, None, ALU.mult).then_inc(bias_step, 1)
                nc.vector.tensor_copy(gate_bias[k]["in_n"], b_in[:, 2:3]).then_inc(bias_step, 1)
                nc.vector.tensor_copy(gate_bias[k]["hid_n"], b_hid[:, 2:3]).then_inc(bias_step, 1)
            nc.vector.reciprocal(r_den[:, :, :].rearrange("p h t -> p t h"), keep["den"][:, :, :]).then_inc(recip, 1)
            dve.wait_ge(recip, 1)
            nc.vector.tensor_scalar(r_den[:, :, :], r_den[:, :, :], 1.0 / HEADS, None, ALU.mult).then_inc(recip, 1)
            dve.wait_ge(turned_den, 1)
            nc.vector.tensor_copy(r_den_t[:, :], ps["node"]["r"][0:HEADS * NB, 0:P]).then_inc(den_out, 1)
            stages(dve, stage)


def stages(engine, stage):
    stage(0, 0, 0, before=False, after=True, long_before=False)
    stage(1, 1, 0, before=True, after=True, long_before=False)
    with engine.Fori(1, NCHUNK // 2) as i:
        for b in range(2):
            stage(2 * i + b, b, i, before=True, after=True, long_before=True)
    stage(NCHUNK, 0, NCHUNK // 2, before=True, after=False, long_before=True)


def norm_phase(nc, sem, dram, keep):
    w_loaded, var_made, rooted, x_done = sem("u_w_loaded"), sem("u_var_made"), sem("u_rooted"), sem("u_x_done")
    x_turned, x_copied, projected, activated, multiplied, copied = (
        sem("u_" + n) for n in ("x_turned", "x_copied", "projected", "activated", "multiplied", "copied"))
    with ExitStack() as ctx:
        m = Mem(nc, ctx)
        w_proj, w_gcn, b_proj = m.sb("w_proj", [P, H]), m.sb("w_gcn", [P, H]), m.sb("b_proj", [P, 1])
        var, root = m.sb("u_var", [P, NB]), m.sb("u_root", [P, NB])
        x1_t = [m.sb(f"x1_t{b}", [P, CW]) for b in range(2)]
        h2_t = [m.sb(f"h2_t{b}", [P, CW]) for b in range(2)]
        x1_ps = [m.ps(f"x1_ps{b}", [P, CW]) for b in range(2)]
        h2_ps = [m.ps(f"h2_ps{b}", [P, CW]) for b in range(2)]
        g_ps = [m.ps(f"g_ps{b}", [P, CW]) for b in range(2)]
        x1, g_all, ident = keep["y_all"], keep["g_all"], keep["ident"]
        block = ctx.enter_context(nc.Block())

        @block.sync
        def _(sp):
            sp.dma_start(w_proj[:, :], dram["W_proj"]).then_inc(w_loaded, 16)
            sp.dma_start(w_gcn[:, :], dram["W_gcn"]).then_inc(w_loaded, 16)
            sp.dma_start(b_proj[:, :], dram["b_proj"].unsqueeze(1)).then_inc(w_loaded, 16)
            for g in range(NGRP):
                sp.wait_ge(keep["first_loaded"][g], 16)

        @block.vector
        def _(dve):
            dve.wait_ge(keep["squared"], NB + 1)
            inverse_roots(nc, dve, var[:, :], root[:, :], keep["square_sums"][:, :], var_made, rooted)

            def finish_x(c):
                rows = slice(c * CHUNK, (c + 1) * CHUNK)
                nc.vector.tensor_tensor(x1[:, rows, :], x1[:, rows, :], root[:, rows].unsqueeze(2).broadcast_to([P, CHUNK, H]),
                                        ALU.mult).then_inc(x_done, 1)

            finish_x(0)
            finish_x(1)
            for c in range(NCHUNK):
                if c + 2 < NCHUNK:
                    finish_x(c + 2)
                dve.wait_ge(x_turned, c + 1)
                if c >= 2:
                    dve.wait_ge(projected, c - 1)
                nc.vector.tensor_copy(x1_t[c % 2][:, :], x1_ps[c % 2][:, :]).then_inc(x_copied, 1)

        @block.scalar
        def _(act):
            act.wait_ge(var_made, 1)
            nc.scalar.activation(root[:, :], var[:, :], ACT.Sqrt).then_inc(rooted, 1)
            act.wait_ge(w_loaded, 48)
            for c in range(NCHUNK + 1):
                if c < NCHUNK:
                    act.wait_ge(projected, c + 1)
                    nc.scalar.activation(h2_t[c % 2][:, :], h2_ps[c % 2][:, :], ACT.Tanh, bias=b_proj[:, :]).then_inc(activated, 1)
                if c >= 1:
                    act.wait_ge(multiplied, c)
                    nc.scalar.copy(g_all[:, (c - 1) * CHUNK:c * CHUNK, :].rearrange("p r f -> p (r f)"), g_ps[(c - 1) % 2][:, :]
                                   ).then_inc(copied, 1)

        @block.tensor
        def _(pe):
            def turn(c):
                pe.wait_ge(x_done, c + 1)
                if c >= 2:
                    pe.wait_ge(x_copied, c - 1)
                for r in range(CHUNK):
                    mm = nc.tensor.transpose(x1_ps[c % 2][:, r * P:(r + 1) * P], x1[:, c * CHUNK + r, :], ident[:, :])
                mm.then_inc(x_turned, 1)

            def project(c):
                pe.wait_ge(x_copied, c + 1)
                if c >= 2:
                    pe.wait_ge(activated, c - 1)
                nc.tensor.matmul(h2_ps[c % 2][:, :], w_proj[:, :], x1_t[c % 2][:, :], start=True, stop=True).then_inc(projected, 1)

            pe.wait_ge(w_loaded, 48)
            turn(0)
            turn(1)
            project(0)
            for c in range(NCHUNK):
                if c + 2 < NCHUNK:
                    turn(c + 2)
                if c + 1 < NCHUNK:
                    project(c + 1)
                pe.wait_ge(activated, c + 1)
                if c >= 2:
                    pe.wait_ge(copied, c - 1)
                for r in range(CHUNK):
                    mm = nc.tensor.matmul(g_ps[c % 2][:, r * P:(r + 1) * P], h2_t[c % 2][:, r * P:(r + 1) * P], w_gcn[:, :],
                                          start=True, stop=True)
                mm.then_inc(multiplied, 1)


def inverse_roots(nc, dve, var, root, square_sums, var_made, rooted, part=0):
    nc.vector.tensor_scalar(var, square_sums, 1.0 / H, EPS, ALU.mult, ALU.add).then_inc(var_made, 1)
    dve.wait_ge(rooted, 2 * part + 1)
    nc.vector.reciprocal(root, root).then_inc(rooted, 1)
    dve.wait_ge(rooted, 2 * part + 2)


def load_graph_group(engine, dram, a_t, loaded, source, c, g):
    engine.dma_start(a_t[:, :, g * GRP * P:(g + 1) * GRP * P],
                     dram[source][bass.ds(c * CHUNK, CHUNK), :, g * GRP * P:(g + 1) * GRP * P].rearrange("r p n -> p r n")
                     ).then_inc(loaded[g], 16)


def prefetch_graph(engine, dram, keep):
    for g in range(NGRP):
        load_graph_group(engine, dram, keep["first_a_t"], keep["first_loaded"], "adj_t", 0, g)


def graph_phase(nc, sem, dram, keep, source):
    tag = {"adj_t": "f", "adj_top_t": "t"}[source]
    prefetched = source == "adj_t"
    loaded = [keep["first_loaded"] if prefetched else [sem(f"t_loaded0{g}") for g in range(NGRP)],
              [sem(f"f_loaded1{g}") for g in range(NGRP)]]
    b_loaded, squared_a, filtered, products = (sem("f" + n) for n in ("_b_loaded", "_squared_a", "_filtered", "_products"))
    relu_done, turned, y_done, centered = (sem("f" + n) for n in ("_relu_done", "_turned", "_y_done", "_centered"))
    squared, var_made, rooted, finished, stored = (
        sem("f" + n) for n in ("_squared", "_var_made", "_rooted", "_finished", "_stored"))
    with ExitStack() as ctx:
        m = Mem(nc, ctx)
        a_t = [keep["first_a_t"] if prefetched else m.sb(tag + "f_t0", [P, CHUNK, N]), m.sb(tag + "f_t1", [P, CHUNK, N])]
        b_gcn = m.sb(tag + "b_gcn", [P, 1])
        feat_t = [m.sb(f"{tag}feat_t{b}", [P, CW]) for b in range(2)]
        y2 = m.sb(tag + "y2", [P, NB, H])
        squares = m.sb(tag + "squares", [P, CHUNK, H])
        mean, var, root, square_sums = (m.sb(tag + n, [P, NB]) for n in ("mean", "var", "root", "square_sums"))
        f_ps = [m.ps(f"{tag}f_ps{b}", [P, CW]) for b in range(2)]
        y_ps = [m.ps(f"{tag}yt_ps{b}", [P, CW]) for b in range(2)]
        x1, g_all, ident = keep["y_all"], keep["g_all"], keep["ident"]
        block = ctx.enter_context(nc.Block())

        @block.sync
        def _(sp):
            sp.dma_start(b_gcn[:, :], dram["b_gcn"].unsqueeze(1)).then_inc(b_loaded, 16)
            for b in range(prefetched, 2):
                for g in range(NGRP):
                    load_graph_group(sp, dram, a_t[b], loaded[b], source, b, g)
            with sp.Fori(0, NCHUNK // 2 - 1) as i:
                for b in range(2):
                    for g in range(NGRP):
                        sp.wait_ge(products, NGRP * (2 * i + b) + g + 1)
                        load_graph_group(sp, dram, a_t[b], loaded[b], source, 2 * i + b + 2, g)
            for c in range(NCHUNK):
                rows = slice(c * CHUNK, (c + 1) * CHUNK)
                sp.wait_ge(finished, c + 1)
                sp.dma_start(dram["out"].rearrange("(t p) f -> p t f", p=P)[:, rows, :], y2[:, rows, :]).then_inc(stored, 16)
            sp.wait_ge(stored, 16 * NCHUNK)

        @block.gpsimd
        def _(pool):
            pool.sem_inc(y_done, 2)

        def group(b, g):
            return a_t[b][:, :, g * GRP * P:(g + 1) * GRP * P]

        @block.vector
        def _(dve):
            def square_a(c, b, i):
                for g in range(NGRP):
                    dve.wait_ge(loaded[b][g], 16 * (i + 1))
                    nc.vector.scalar_tensor_tensor(group(b, g), group(b, g), 0.0, group(b, g), ALU.max, ALU.mult
                                                   ).then_inc(squared_a, 1)

            def add_x1(c, b):
                dve.wait_ge(turned, c + 3)
                rows = bass.ds(c * CHUNK, CHUNK)
                y, mu = y2[:, rows, :], mean[:, rows]
                nc.vector.tensor_tensor(y, y_ps[b][:, :].rearrange("p (r f) -> p r f", f=H), x1[:, rows, :], ALU.add
                                        ).then_inc(y_done, 1)
                dve.wait_ge(y_done, c + 3)
                nc.vector.tensor_reduce(mu, y, AX_X, ALU.add).then_inc(centered, 1)
                dve.wait_ge(centered, 3 * c + 1)
                nc.vector.tensor_scalar(mu, mu, 1.0 / H, None, ALU.mult).then_inc(centered, 1)
                dve.wait_ge(centered, 3 * c + 2)
                nc.vector.tensor_tensor(y, y, mu.unsqueeze(2).broadcast_to([P, CHUNK, H]), ALU.subtract).then_inc(centered, 1)

            def finish(part, first, end):
                tiles = slice(first * CHUNK, end * CHUNK)
                dve.wait_ge(squared, end * CHUNK + 1)
                inverse_roots(nc, dve, var[:, tiles], root[:, tiles], square_sums[:, tiles], var_made, rooted, part)
                for c in range(first, end):
                    rows = slice(c * CHUNK, (c + 1) * CHUNK)
                    nc.vector.tensor_tensor(y2[:, rows, :], y2[:, rows, :], root[:, rows].unsqueeze(2).broadcast_to([P, CHUNK, H]),
                                            ALU.mult).then_inc(finished, 1)

            square_a(0, 0, 0)
            with dve.Fori(0, NCHUNK // 2 - 1) as i:
                square_a(2 * i + 1, 1, i)
                add_x1(2 * i, 0)
                square_a(2 * i + 2, 0, i + 1)
                add_x1(2 * i + 1, 1)
            square_a(NCHUNK - 1, 1, NCHUNK // 2 - 1)
            add_x1(NCHUNK - 2, 0)
            finish(0, 0, NCHUNK - 1)
            add_x1(NCHUNK - 1, 1)
            finish(1, NCHUNK - 1, NCHUNK)

        @block.scalar
        def _(act):
            def tanh(c, b, g):
                act.wait_ge(squared_a, NGRP * c + g + 1)
                nc.scalar.activation(group(b, g), group(b, g), ACT.Tanh).then_inc(filtered, 1)

            def relu(c, b):
                act.wait_ge(products, NGRP * (c + 1))
                act.wait_ge(turned, c + 1)
                nc.scalar.activation(feat_t[b][:, :], f_ps[b][:, :], ACT.Relu, bias=b_gcn[:, :]).then_inc(relu_done, 1)

            def square_y(c):
                act.wait_ge(centered, 3 * (c + 1))
                for q in range(CHUNK):
                    t = CHUNK * c + q
                    act.wait_ge(squared, t + 1)
                    nc.scalar.activation(squares[:, q, :], y2[:, bass.ds(t, 1), :].rearrange("p a f -> p (a f)"), ACT.Square,
                                         accum_out=square_sums[:, bass.ds(t, 1)]).then_inc(squared, 1)

            def take_root(part, first, end):
                tiles = slice(first * CHUNK, end * CHUNK)
                act.wait_ge(var_made, part + 1)
                nc.scalar.activation(root[:, tiles], var[:, tiles], ACT.Sqrt).then_inc(rooted, 1)

            def stage(c, b, before_last):
                tanh(c, b, 0)
                relu(c - 1, 1 - b)
                tanh(c, b, 1)
                tanh(c, b, 2)
                if before_last:
                    square_y(c - 2)
                tanh(c, b, 3)

            act.sem_inc(squared, 1)
            for g in range(NGRP):
                tanh(0, 0, g)
            act.wait_ge(b_loaded, 16)
            stage(1, 1, False)
            with act.Fori(1, NCHUNK // 2) as i:
                for b in range(2):
                    stage(2 * i + b, b, True)
            square_y(NCHUNK - 2)
            take_root(0, 0, NCHUNK - 1)
            relu(NCHUNK - 1, 1)
            square_y(NCHUNK - 1)
            take_root(1, NCHUNK - 1, NCHUNK)

        @block.tensor
        def _(pe):
            def turn(c, b):
                pe.wait_ge(relu_done, c + 1)
                pe.wait_ge(y_done, c + 1)
                for r in range(CHUNK):
                    mm = nc.tensor.transpose(y_ps[b][:, r * P:(r + 1) * P], feat_t[b][:, r * P:(r + 1) * P], ident[:, :])
                mm.then_inc(turned, 1)

            def products_of(c, b, turn_before):
                for g in range(NGRP):
                    pe.wait_ge(filtered, NGRP * c + g + 1)
                    for j in range(GRP):
                        k = g * GRP + j
                        mm = nc.tensor.matmul(f_ps[b][:, :].rearrange("p (r n) -> p r n", n=P), g_all[:, k, :],
                                              a_t[b][:, :, k * P:(k + 1) * P], start=k == 0, stop=k == NB - 1)
                    mm.then_inc(products, 1)
                    if g == 1 and turn_before:
                        turn(c - 1, 1 - b)

            pe.sem_inc(turned, 2)
            products_of(0, 0, False)
            with pe.Fori(0, NCHUNK // 2 - 1) as i:
                for s in range(2):
                    products_of(2 * i + 1 + s, 1 - s, True)
            products_of(NCHUNK - 1, 1, True)
            turn(NCHUNK - 1, 1)


def top_k_phase(nc, sem, dram, keep):
    PAD = -TOPK % 8
    ROUNDS = (TOPK + PAD) // 8
    W = PAD + N
    loaded, stored = sem("k_loaded"), sem("k_stored")
    padded, filtered, step, found, removed, kept, turned, copied = (
        sem("k_" + n) for n in ("padded", "filtered", "step", "found", "removed", "kept", "turned", "copied"))
    with ExitStack() as ctx:
        m = Mem(nc, ctx)
        row, f, left, out_t = m.sb("k_row", [P, N]), m.sb("k_f", [P, W]), m.sb("k_left", [P, W]), m.sb("k_out_t", [P, N])
        best, pause = m.sb("k_best", [P, 8]), m.sb("k_pause", [P, 1])
        ps = [m.ps(f"k_ps{b}", [P, CW]) for b in range(2)]
        ident = keep["ident"]
        block = ctx.enter_context(nc.Block())

        @block.sync
        def _(sp):
            with sp.Fori(0, NB) as t:
                sp.wait_ge(turned, NCHUNK * (t + 1))
                sp.dma_start(row[:, :], dram["adj"][bass.ds(t * P, P), :]).then_inc(loaded, 16)
                sp.wait_ge(copied, NCHUNK * (t + 1) + 2)
                sp.dma_start(dram["adj_top_t"][bass.ds(t, 1), :, :].rearrange("a p n -> p (a n)"), out_t[:, :]).then_inc(stored, 16)
            sp.wait_ge(stored, 16 * (NB + 1))

        @block.scalar
        def _(act):
            with act.Fori(0, NB) as t:
                act.wait_ge(step, 3 * t + 1)
                nc.scalar.activation(f[:, PAD:W], f[:, PAD:W], ACT.Tanh).then_inc(filtered, 1)

        @block.vector
        def _(dve):
            nc.vector.memset(f[:, 0:PAD], 2.0).then_inc(padded, 1)
            dve.wait_ge(padded, 1)
            dve.sem_inc(stored, 16)
            with dve.Fori(0, NB) as t:
                dve.wait_ge(loaded, 16 * (t + 1))
                nc.vector.scalar_tensor_tensor(f[:, PAD:W], row[:, :], 0.0, row[:, :], ALU.max, ALU.mult).then_inc(step, 1)
                dve.wait_ge(filtered, t + 1)
                nc.vector.tensor_copy(left[:, :], f[:, :]).then_inc(step, 1)
                dve.wait_ge(step, 3 * t + 2)
                nc.vector.memset(pause[:, :], 0.0)
                with dve.Fori(0, ROUNDS) as r:
                    nc.vector.max(best[:, :], left[:, :]).then_inc(found, 1)
                    dve.wait_ge(found, t * ROUNDS + r + 1)
                    nc.vector.memset(pause[:, :], 0.0)
                    nc.vector.match_replace(left[:, :], best[:, :], left[:, :], -1.0).then_inc(removed, 1)
                    dve.wait_ge(removed, t * ROUNDS + r + 1)
                    nc.vector.memset(pause[:, :], 0.0)
                nc.vector.tensor_tensor(left[:, PAD:W], left[:, PAD:W], f[:, PAD:W], ALU.not_equal).then_inc(step, 1)
                dve.wait_ge(step, 3 * t + 3)
                nc.vector.tensor_tensor(row[:, :], row[:, :], left[:, PAD:W], ALU.mult).then_inc(kept, 1)
                dve.wait_ge(stored, 16 * (t + 1))
                for c in range(NCHUNK):
                    dve.wait_ge(turned, NCHUNK * (t + 1) + c + 1)
                    nc.vector.tensor_copy(out_t[:, c * CW:(c + 1) * CW], ps[c % 2][:, :]).then_inc(copied, 1)

        @block.tensor
        def _(pe):
            pe.sem_inc(turned, NCHUNK)
            pe.sem_inc(copied, 2)
            with pe.Fori(0, NB) as t:
                pe.wait_ge(kept, t + 1)
                for c in range(NCHUNK):
                    pe.wait_ge(copied, NCHUNK * t + c + 1)
                    for r in range(CHUNK):
                        k = c * CHUNK + r
                        mm = nc.tensor.transpose(ps[c % 2][:, r * P:(r + 1) * P], row[:, k * P:(k + 1) * P], ident[:, :])
                    mm.then_inc(turned, 1)


def build(nc, dram):
    with ExitStack() as top:
        sems = {}

        def sem(name):
            if name not in sems:
                sems[name] = top.enter_context(nc.semaphore(name))
            return sems[name]

        m = Mem(nc, top)
        keep = {
            "ident": m.sb("ident", [P, P]),
            "off_diag": m.sb("off_diag", [P, P]),
            "sel": m.sb("sel", [P, 2, NUV]),
            "diag_bias": m.sb("diag_bias", [P, P], BF16),
            "den": m.sb("den", [P, NB, HEADS]),
            "ones": m.sb("ones", [P, 1]),
            "flags": m.sb("flags", [1, 2], I32),
            "diag": m.sb("diag", [P, NB]),
            "biases": m.sb("biases", [P, len(KINDS), 2, 3]),
            "small_loaded": sem("b_small_loaded"),
            "square_sums": m.sb("square_sums", [P, NB]),
            "squared": sem("g_squared"),
            "first_loaded": [sem(f"f_loaded0{g}") for g in range(NGRP)],
        }
        keep["x_sb"] = keep["y_all"] = m.sb("x_sb", [P, NB, H])
        keep["uv_parts"] = m.sb("uv_parts", [P, NB, NST], BF16)
        with ExitStack() as ahead:
            ma = Mem(nc, ahead)
            keep["e_all"] = ma.sb("e_all", [P, HEADS, N])
            keep["row"] = [ma.sb(f"row{s}", [P, QUARTER]) for s in range(2)]
            keep["row_loaded"], keep["e_spread"] = [sem(f"b_row_loaded{s}") for s in range(2)], sem("b_e_spread")
            with ExitStack() as support:
                ms = Mem(nc, support)
                keep["x_hi"], keep["x_lo"] = ms.sb("x_hi", [P, NB, H], F32R), ms.sb("x_lo", [P, NB, H], F32R)
                half = RING // 2
                own = ms.sb("pieces", [P, half, CHUNK, PW])
                shared = keep["x_sb"][:, :, :].rearrange("p t f -> p (t f)").rearrange("p (g r n) -> p g r n", g=half, r=CHUNK)
                keep["pieces"] = [own[:, g, :, :] for g in range(half)] + [shared[:, g, :, :] for g in range(half)]
                keep["clear"] = ms.sb("clear", [P, 2 * NPIECE - 1, P])
                keep["loaded"] = [sem(f"a_loaded{g}") for g in range(RING)]
                setup_phase(nc, sem, dram, keep)
                support_phase(nc, sem, dram, keep)
            without_negatives = nc.values_load(keep["flags"][0:1, 0:1], min_val=0, max_val=1)
            with nc.If(without_negatives):
                attention_phase(nc, sem, dram, keep, signed=False)
        with nc.Else():
            signed_scores_phase(nc, sem, dram, keep)
            attention_phase(nc, sem, dram, keep, signed=True)
        keep["g_all"] = m.sb("g_all", [P, NB, H])
        with ExitStack() as ahead:
            keep["first_a_t"] = Mem(nc, ahead).sb("first_a_t", [P, CHUNK, N])
            gate_phase(nc, sem, dram, keep)
            norm_phase(nc, sem, dram, keep)
            few = nc.values_load(keep["flags"][0:1, 1:2], min_val=0, max_val=1)
            with nc.If(few):
                graph_phase(nc, sem, dram, keep, "adj_t")
        with nc.Else():
            top_k_phase(nc, sem, dram, keep)
            graph_phase(nc, sem, dram, keep, "adj_top_t")


def host_constants():
    import numpy as np

    ident = np.eye(P, dtype=np.float32)
    sel = np.zeros((P, 2, NUV), np.float32)
    for k in range(NPART):
        for h in range(HEADS):
            u, v = 1 + k * NUV + 2 * h, 1 + k * NUV + 2 * h + 1
            sel[u, 0, h] = sel[v, 1, h] = 1.0
            sel[v, 0, HEADS + h] = sel[u, 1, HEADS + h] = 1.0
    return {"ident": ident, "off_diag": 1.0 - ident, "sel": sel}


def host_layout(inputs):
    import numpy as np

    adj, x = np.asarray(inputs["adj"]), np.asarray(inputs["x"])
    lay = {
        "x": x,
        "x_t": x.T,
        "adj": adj,
        "adj_t": adj.reshape(NB, P, NB, P).transpose(0, 3, 2, 1).reshape(NB, P, N),
        "gat_W": np.asarray(inputs["L0_gnn_gat_W"]).transpose(1, 0, 2),
        "gat_W_t": np.asarray(inputs["L0_gnn_gat_W"]).transpose(0, 2, 1),
        "gat_a": np.asarray(inputs["L0_gnn_gat_a"]).reshape(HEADS, 2, H).transpose(2, 0, 1),
    }
    for k in ("edge", "node"):
        for w in ("Wih", "Whh"):
            lay[f"{k}_{w}_t"] = np.asarray(inputs[f"L0_gnn_{k}_{w}"]).T
        for w in ("bih", "bhh"):
            lay[f"{k}_{w}"] = np.asarray(inputs[f"L0_gnn_{k}_{w}"])
    for k in ("W_proj", "b_proj", "W_gcn", "b_gcn"):
        lay[k] = np.asarray(inputs[f"L1_gnn_{k}"])
    return {k: np.ascontiguousarray(v) for k, v in lay.items()}


def kernel(**inputs):
    import concourse.bacc as bacc
    from concourse.bass_utils import run_bass_kernel_spmd as run

    nc = bacc.Bacc("TRN2", target_bir_lowering=False, num_devices=1)
    arrays, dram = {}, {}
    for name, a in {**host_layout(inputs), **host_constants()}.items():
        arrays["in_" + name] = a
        dram[name] = nc.dram_tensor("in_" + name, a.shape, mybir.dt.from_np(a.dtype), kind="ExternalInput").ap()
    for name, shape in SCRATCH.items():
        dram[name] = nc.dram_tensor("scratch_" + name, shape, F32, kind="Internal").ap()
    dram["out"] = nc.dram_tensor("out", (N, H), F32, kind="ExternalOutput").ap()
    build(nc, dram)
    return run(nc, [arrays], core_ids=[0]).results[0]["out"]
```
